# Optimizing a Trainium2 kernel written in Bass

```python
import numpy as np
import jax
import jax.numpy as jnp

def _softmax(x, axis=-1):
    return jax.nn.softmax(x, axis=axis)

def _gelu(x):
    return jax.nn.gelu(x, approximate=True)

def _silu(x):
    return jax.nn.silu(x)

def _sigmoid(x):
    return jax.nn.sigmoid(x)

def _layernorm(x, axis=-1, eps=1e-05):
    m = jnp.mean(x, axis=axis, keepdims=True)
    v = jnp.var(x, axis=axis, keepdims=True)
    return (x - m) / jnp.sqrt(v + eps)

def _scatter_add(tgt, idx, src, axis=0):
    return tgt.at[idx].add(src)

def _segment_sum(src, seg, n):
    return jax.ops.segment_sum(src, seg, n)
kernel_name = 'mk_seq_preln_d1_jaxref_r8_23dd58'

def setup_inputs(seed: int=0):
    np.random.seed(seed)
    _w = jnp.asarray

    def _L0_attn_setup():
        import jax, jax.numpy as jnp
        import numpy as np
        D_MODEL = 128
        D_INNER = 256
        N_HEADS = 8
        HEAD_DIM = D_INNER // N_HEADS
        D_STATE = 64
        CHUNK = 64
        D_CONV = 4
        EPS = float(np.finfo(np.float32).eps)
        PROJ_OUT = 2 * D_INNER + 2 * N_HEADS * D_STATE + N_HEADS

        def rmsnorm(x, w):
            return x * jax.lax.rsqrt(jnp.mean(x * x, axis=-1, keepdims=True) + EPS) * w

        def ssd_scan(x, dt, B_in, C_in, A_log):
            Bz, S, H, P = x.shape
            N = B_in.shape[-1]
            nc = S // CHUNK
            A = -jnp.exp(A_log)
            resh = lambda t: jnp.moveaxis(t.reshape((Bz, nc, CHUNK) + t.shape[2:]), 1, 0)
            xs = (resh(x), resh(dt), resh(B_in), resh(C_in))
            mask = jnp.tril(jnp.ones((CHUNK, CHUNK), bool))
            h0 = jnp.zeros((Bz, H, P, N), jnp.float32)

            def step(h, inp):
                x_c, dt_c, B_c, C_c = inp
                lcs = jnp.cumsum(dt_c * A, axis=1)
                lcsT = jnp.transpose(lcs, (0, 2, 1))
                diff = lcsT[:, :, :, None] - lcsT[:, :, None, :]
                M = jnp.exp(jnp.where(mask, diff, -jnp.inf))
                G = jnp.einsum('blhn,bihn->bhli', C_c, B_c)
                intra = jnp.einsum('bhli,bihp->blhp', M * G, x_c)
                inter = jnp.einsum('blh,blhn,bhpn->blhp', jnp.exp(lcs), C_c, h)
                total_decay = jnp.exp(lcsT[:, :, -1])
                h_new = total_decay[:, :, None, None] * h + jnp.einsum('bhl,blhp,blhn->bhpn', M[:, :, -1, :], x_c, B_c)
                return (h_new, intra + inter)
            _, ys = jax.lax.scan(step, h0, xs)
            return jnp.moveaxis(ys, 0, 1).reshape(Bz, S, H, P)
        key = jax.random.key(seed)
        ks = jax.random.split(key, 8)
        hidden = jax.random.normal(ks[0], (2, 512, D_MODEL), jnp.float32)
        w_in_proj = 0.02 * jax.random.normal(ks[1], (D_MODEL, PROJ_OUT), jnp.float32)
        conv_w = 0.2 * jax.random.normal(ks[2], (D_INNER, 1, D_CONV), jnp.float32)
        conv_b = jnp.zeros((D_INNER,), jnp.float32)
        w_dt = 0.02 * jax.random.normal(ks[3], (N_HEADS, D_INNER), jnp.float32)
        b_dt = 0.02 * jax.random.normal(ks[4], (D_INNER,), jnp.float32)
        A_log = jax.random.uniform(ks[5], (N_HEADS,), jnp.float32, np.log(0.001), np.log(0.1))
        D = jnp.ones((N_HEADS,), jnp.float32)
        w_out_proj = 0.02 * jax.random.normal(ks[6], (D_INNER, D_MODEL), jnp.float32)
        return {'hidden': hidden, 'w_norm_in': jnp.ones((D_MODEL,), jnp.float32), 'w_in_proj': w_in_proj, 'conv_w': conv_w, 'conv_b': conv_b, 'w_dt': w_dt, 'b_dt': b_dt, 'A_log': A_log, 'D': D, 'w_norm_out': jnp.ones((D_INNER,), jnp.float32), 'w_out_proj': w_out_proj}
    _L0_attn_in = _L0_attn_setup()

    def _L0_ffn_setup():
        import jax, jax.numpy as jnp
        import numpy as np
        B, S, D, F, O = (4, 256, 128, 512, 128)
        E, NS, K = (4, 2, 2)
        key = jax.random.key(seed)
        ks = jax.random.split(key, 6)

        def w(k, shape, fan_in):
            return jax.random.normal(k, shape, jnp.float32) * fan_in ** (-0.5)
        return {'x': jax.random.normal(ks[0], (B, S, D), jnp.float32), 'gate_w': w(ks[1], (D, E), D), 'gate_b': jnp.zeros((E,), jnp.float32), 'sw1': w(ks[2], (NS, D, F), D), 'sb1': jnp.zeros((NS, F), jnp.float32), 'sw2': w(ks[3], (NS, F, O), F), 'sb2': jnp.zeros((NS, O), jnp.float32), 'rw1': w(ks[4], (E, D, F), D), 'rb1': jnp.zeros((E, F), jnp.float32), 'rw2': w(ks[5], (E, F, O), F), 'rb2': jnp.zeros((E, O), jnp.float32)}
    _L0_ffn_in = _L0_ffn_setup()
    _d = {'L0_attn_hidden': _L0_attn_in['hidden'], 'L0_attn_w_norm_in': _L0_attn_in['w_norm_in'], 'L0_attn_w_in_proj': _L0_attn_in['w_in_proj'], 'L0_attn_conv_w': _L0_attn_in['conv_w'], 'L0_attn_conv_b': _L0_attn_in['conv_b'], 'L0_attn_w_dt': _L0_attn_in['w_dt'], 'L0_attn_b_dt': _L0_attn_in['b_dt'], 'L0_attn_A_log': _L0_attn_in['A_log'], 'L0_attn_D': _L0_attn_in['D'], 'L0_attn_w_norm_out': _L0_attn_in['w_norm_out'], 'L0_attn_w_out_proj': _L0_attn_in['w_out_proj'], 'L0_ffn_gate_w': _L0_ffn_in['gate_w'], 'L0_ffn_gate_b': _L0_ffn_in['gate_b'], 'L0_ffn_sw1': _L0_ffn_in['sw1'], 'L0_ffn_sb1': _L0_ffn_in['sb1'], 'L0_ffn_sw2': _L0_ffn_in['sw2'], 'L0_ffn_sb2': _L0_ffn_in['sb2'], 'L0_ffn_rw1': _L0_ffn_in['rw1'], 'L0_ffn_rb1': _L0_ffn_in['rb1'], 'L0_ffn_rw2': _L0_ffn_in['rw2'], 'L0_ffn_rb2': _L0_ffn_in['rb2']}
    _x0 = _d['L0_attn_hidden']
    _d['L0_attn_hidden'] = jax.random.normal(jax.random.fold_in(jax.random.key(seed), 1), (8, 512, 128), dtype=_x0.dtype)
    del _x0
    return _d

def reference(L0_attn_hidden, L0_attn_w_norm_in, L0_attn_w_in_proj, L0_attn_conv_w, L0_attn_conv_b, L0_attn_w_dt, L0_attn_b_dt, L0_attn_A_log, L0_attn_D, L0_attn_w_norm_out, L0_attn_w_out_proj, L0_ffn_gate_w, L0_ffn_gate_b, L0_ffn_sw1, L0_ffn_sb1, L0_ffn_sw2, L0_ffn_sb2, L0_ffn_rw1, L0_ffn_rb1, L0_ffn_rw2, L0_ffn_rb2):

    def _L0_attn_ref(hidden, w_norm_in, w_in_proj, conv_w, conv_b, w_dt, b_dt, A_log, D, w_norm_out, w_out_proj):
        import jax, jax.numpy as jnp
        import numpy as np
        D_MODEL = 128
        D_INNER = 256
        N_HEADS = 8
        HEAD_DIM = D_INNER // N_HEADS
        D_STATE = 64
        CHUNK = 64
        D_CONV = 4
        EPS = float(np.finfo(np.float32).eps)
        PROJ_OUT = 2 * D_INNER + 2 * N_HEADS * D_STATE + N_HEADS

        def rmsnorm(x, w):
            return x * jax.lax.rsqrt(jnp.mean(x * x, axis=-1, keepdims=True) + EPS) * w

        def ssd_scan(x, dt, B_in, C_in, A_log):
            Bz, S, H, P = x.shape
            N = B_in.shape[-1]
            nc = S // CHUNK
            A = -jnp.exp(A_log)
            resh = lambda t: jnp.moveaxis(t.reshape((Bz, nc, CHUNK) + t.shape[2:]), 1, 0)
            xs = (resh(x), resh(dt), resh(B_in), resh(C_in))
            mask = jnp.tril(jnp.ones((CHUNK, CHUNK), bool))
            h0 = jnp.zeros((Bz, H, P, N), jnp.float32)

            def step(h, inp):
                x_c, dt_c, B_c, C_c = inp
                lcs = jnp.cumsum(dt_c * A, axis=1)
                lcsT = jnp.transpose(lcs, (0, 2, 1))
                diff = lcsT[:, :, :, None] - lcsT[:, :, None, :]
                M = jnp.exp(jnp.where(mask, diff, -jnp.inf))
                G = jnp.einsum('blhn,bihn->bhli', C_c, B_c)
                intra = jnp.einsum('bhli,bihp->blhp', M * G, x_c)
                inter = jnp.einsum('blh,blhn,bhpn->blhp', jnp.exp(lcs), C_c, h)
                total_decay = jnp.exp(lcsT[:, :, -1])
                h_new = total_decay[:, :, None, None] * h + jnp.einsum('bhl,blhp,blhn->bhpn', M[:, :, -1, :], x_c, B_c)
                return (h_new, intra + inter)
            _, ys = jax.lax.scan(step, h0, xs)
            return jnp.moveaxis(ys, 0, 1).reshape(Bz, S, H, P)
        Bz, S, _ = hidden.shape
        residual = hidden
        h = rmsnorm(hidden, w_norm_in)
        proj = h @ w_in_proj
        o1, o2 = (D_INNER, 2 * D_INNER)
        o3 = o2 + N_HEADS * D_STATE
        o4 = o3 + N_HEADS * D_STATE
        z = proj[..., :o1]
        x = proj[..., o1:o2]
        B_flat = proj[..., o2:o3]
        C_flat = proj[..., o3:o4]
        dt_raw = proj[..., o4:]
        xt = jnp.transpose(x, (0, 2, 1))
        xc = jax.lax.conv_general_dilated(xt, conv_w, (1,), [(D_CONV - 1, 0)], dimension_numbers=('NCH', 'OIH', 'NCH'), feature_group_count=D_INNER) + conv_b[None, :, None]
        x = jax.nn.silu(jnp.transpose(xc, (0, 2, 1)))
        dt = jax.nn.softplus(dt_raw @ w_dt + b_dt)
        dt_h = dt.reshape(Bz, S, N_HEADS, HEAD_DIM).mean(-1)
        B_ssm = B_flat.reshape(Bz, S, N_HEADS, D_STATE)
        C_ssm = C_flat.reshape(Bz, S, N_HEADS, D_STATE)
        x_h = x.reshape(Bz, S, N_HEADS, HEAD_DIM)
        y = ssd_scan(x_h, dt_h, B_ssm, C_ssm, A_log)
        y = y + x_h * D[None, None, :, None]
        y = y.reshape(Bz, S, D_INNER)
        y = y * jax.nn.silu(z)
        y = rmsnorm(y, w_norm_out)
        return residual + y @ w_out_proj

    def _L0_ffn_ref(x, gate_w, gate_b, sw1, sb1, sw2, sb2, rw1, rb1, rw2, rb2):
        import jax, jax.numpy as jnp
        import numpy as np
        B, S, D, F, O = (4, 256, 128, 512, 128)
        E, NS, K = (4, 2, 2)
        weights = jax.nn.softmax(x @ gate_w + gate_b, axis=-1)
        topk_w, topk_i = jax.lax.top_k(weights, K)
        sh = jax.nn.relu(jnp.einsum('bsd,ndf->bsnf', x, sw1) + sb1)
        shared = (jnp.einsum('bsnf,nfo->bsno', sh, sw2) + sb2).sum(axis=2) / NS
        rh = jax.nn.relu(jnp.einsum('bsd,edf->bsef', x, rw1) + rb1)
        eo = jnp.einsum('bsef,efo->bseo', rh, rw2) + rb2
        gathered = jnp.take_along_axis(eo, topk_i[..., None], axis=2)
        routed = (gathered * topk_w[..., None]).sum(axis=2)
        return shared + routed
    x = L0_attn_hidden
    x = x + _L0_attn_ref(_layernorm(x, axis=-1), L0_attn_w_norm_in, L0_attn_w_in_proj, L0_attn_conv_w, L0_attn_conv_b, L0_attn_w_dt, L0_attn_b_dt, L0_attn_A_log, L0_attn_D, L0_attn_w_norm_out, L0_attn_w_out_proj)
    x = x + _L0_ffn_ref(_layernorm(x, axis=-1), L0_ffn_gate_w, L0_ffn_gate_b, L0_ffn_sw1, L0_ffn_sb1, L0_ffn_sw2, L0_ffn_sb2, L0_ffn_rw1, L0_ffn_rb1, L0_ffn_rw2, L0_ffn_rb2)
    return x

_drawn_inputs = setup_inputs


def setup_inputs(seed=0):
    import zlib

    import numpy as np

    out = dict(_drawn_inputs(seed))
    spreads = {'L0_attn_w_norm_in': (1.0, 0.2),
     'L0_attn_conv_b': (0.0, 0.1),
     'L0_attn_D': (1.0, 0.6),
     'L0_attn_w_norm_out': (1.0, 0.2),
     'L0_ffn_gate_b': (0.0, 0.1),
     'L0_ffn_sb1': (0.0, 0.332),
     'L0_ffn_sb2': (0.0, 0.1),
     'L0_ffn_rb1': (0.0, 0.4),
     'L0_ffn_rb2': (0.0, 0.271)}
    factors = {'L0_attn_w_dt': 200.0, 'L0_attn_b_dt': 200.0}
    for name, (base, spread) in spreads.items():
        noise = np.random.default_rng([zlib.crc32(name.encode()), seed]).standard_normal(out[name].shape)
        drawn = base * np.exp(spread * noise) if base else spread * noise
        out[name] = jnp.asarray(drawn.astype(out[name].dtype))
    for name, factor in factors.items():
        out[name] = (out[name] * factor).astype(out[name].dtype)
    return out
```

```python
from contextlib import ExitStack

import numpy as np

import concourse.bass as bass
from concourse import mybir

ALU = mybir.AluOpType
ACT = mybir.ActivationFunctionType
AX_X = mybir.AxisListType.X
F32 = mybir.dt.float32
F32R = mybir.dt.float32r
BF16 = mybir.dt.bfloat16

P = 128
NCH = 4
SEQ = NCH * P
DI = 256
NB = DI // P
NH = 8
NP = NH // 2
HD = DI // NH
NS = 64
NG = 6
NE = 4
NF = 4
NBLK = NG * NF
TAPS = 4
RING = 3
LAG = 2
LN_EPS = 1e-5
RMS_EPS = float(np.finfo(np.float32).eps)
CLAMP = 30.0
MASKED = -1e30

Z0, DT0, X0, B0, C0, WCOLS = 0, 256, 512, 768, 1280, 1792


def nth(s, per, k):
    if isinstance(s, int) and s * per + k <= 0:
        return None
    return s * per + k


def is_seq(s, n):
    return isinstance(s, int) and s == n


def build(nc, a, out):
    n_seq = a["hidden"].shape[0]
    x_dram = a["hidden"].rearrange("s (c p) d -> s p c d", p=P)
    out_dram = out.rearrange("s (c p) d -> s p c d", p=P)

    with ExitStack() as ctx:
        def sb(name, shape, dt=F32):
            return ctx.enter_context(nc.sbuf_tensor(name, shape, dt))

        def sem(name):
            return ctx.enter_context(nc.semaphore(name))

        bank = [ctx.enter_context(nc.psum_tensor(f"bank{i}", [P, 512], F32)) for i in range(8)]
        HID = bank[0:2]
        FOUT = bank[2]
        TR = bank[3]
        MAIN = bank[4:8]
        TR_BF = TR[:, 0:256].bitcast(BF16)

        ident = sb("ident", [P, P])
        ident_bf = sb("ident_bf", [P, P], BF16)
        ones = sb("ones", [P, P])
        upto = sb("upto", [P, P])
        mask = sb("mask", [P, NP, P], BF16)
        pick_head = sb("pick_head", [3 * NH, NH, P], BF16)
        minus_head = sb("minus_head", [3 * NH, NH, P], BF16)
        pick_expert = sb("pick_expert", [3 * NE, NE, P], BF16)
        lower = sb("lower", [P, NE, NE])
        carrier = sb("carrier", [P, RING + 1])
        half = sb("half", [P, 8])

        BT = sb("BT", [P, NP, SEQ])
        CT = sb("CT", [P, NP, SEQ])
        w_all = BT[:].rearrange("p n t -> p (n t)")[:, 0:WCOLS]
        w_raw = CT[:].rearrange("p n t -> p (n t)")[:, 0:1544]
        wh = sb("wh", [P, WCOLS], F32R)
        wl = sb("wl", [P, WCOLS], F32R)
        rows = sb("rows", [35, P])
        cols = sb("cols", [P, 35])
        b1 = cols[:, 0:24]
        b2s = cols[:, 24:26]
        b2r = cols[:, 26:30]
        conv_b = cols[:, 30:32]
        wn_in = cols[:, 32:33]
        wn_out = cols[:, 33:35]
        b2sh = sb("b2sh", [P, 1])
        b2sum = sb("b2sum", [P, 1])
        conv_w = sb("conv_w", [P, NB, TAPS])
        w_dt = sb("w_dt", [NH, DI])
        wdtT = sb("wdtT", [NH, P])
        b_dt = sb("b_dt", [P, DI])
        a_log = sb("a_log", [P, NH])
        a_exp = sb("a_exp", [P, NH])
        a_neg = sb("a_neg", [P, NH])
        d_bc = sb("d_bc", [P, NH])
        w_out_raw = sb("w_out_raw", [P, NB, P])
        w_out = sb("w_out", [P, NB, P])
        gw = sb("gw", [P, NE])
        gwh = sb("gwh", [P, NE], F32R)
        gwl = sb("gwl", [P, NE], F32R)
        gb = sb("gb", [P, NE])
        late = sb("late", [P, 2 * NG * 512])
        wf_raw = late[:].rearrange("p (a n f) -> p a n f", a=2, n=NG)
        used = [0]

        def late_part(n):
            used[0] += n
            return late[:, used[0] - n:used[0]]

        w1h = sb("w1h", [P, NG, 512], F32R)
        w1l = sb("w1l", [P, NG, 512], F32R)
        w2h = sb("w2h", [P, NG, NF, P], F32R)
        w2l = sb("w2l", [P, NG, NF, P], F32R)

        x_in = sb("x_in", [P, NCH, P])
        st1 = sb("st1", [P, NCH, 6])
        mv1 = sb("mv1", [P, NCH, 2])
        v1 = sb("v1", [P, 2, NCH])
        rs1 = sb("rs1", [P, 2, NCH])
        one_rs = sb("one_rs", [P, NCH])
        mean_rs = sb("mean_rs", [P, NCH])
        hn = sb("hn", [P, NCH, P])
        xr = sb("xr", [P, NCH, P])
        hTh = sb("hTh", [P, SEQ], F32R)
        hTl = sb("hTl", [P, SEQ], F32R)
        xpad = sb("xpad", [P, NB, TAPS - 1 + SEQ])
        cv = sb("cv", [P, NB, SEQ])
        xs = sb("xs", [P, NCH, DI])
        sz = sb("sz", [P, NCH, DI])
        dtv = sb("dtv", [P, NCH, DI])
        sp = sb("sp", [P, NCH, DI])
        dsum = sb("dsum", [P, NCH * NH])
        dta = sb("dta", [P, NCH * NH])
        ecs = sb("ecs", [P, NCH, NH])
        tdx = sb("tdx", [P, NCH, NP])
        rem1 = sb("rem1", [P, NCH, NH])
        rem2 = sb("rem2", [P, NCH, NH])
        lparts = sb("lparts", [P, NCH, 3, NH], BF16)
        lT = sb("lT", [3 * NH, SEQ], BF16)
        btok = sb("btok", [P, NP * P])
        decay = sb("decay", [P, 2, NP, P])
        mg = sb("mg", [P, 2, NP, P])
        xw = sb("xw", [P, NP, 2, HD])
        xd = sb("xd", [P, DI])
        state = sb("state", [P, NP, 2 * HD])
        state_m = sb("state_m", [P, NP, 2 * HD])
        yt = sb("yt", [P, DI])
        yz = sb("yz", [P, DI])
        junk = sb("junk", [P, DI])
        ssq = sb("ssq", [P, NCH])
        msq = sb("msq", [P, NCH])
        rstd = sb("rstd", [P, NCH])
        yT = sb("yT", [P, NB, SEQ])
        x1 = late_part(NCH * P).rearrange("p (c d) -> p c d", c=NCH)
        st2 = sb("st2", [P, NCH, 6])
        mv2 = sb("mv2", [P, NCH, 2])
        v2 = sb("v2", [P, NCH])
        rs2 = sb("rs2", [P, NCH])
        fn = late_part(NCH * P).rearrange("p (c d) -> p c d", c=NCH)
        fTh = sb("fTh", [P, SEQ], F32R)
        fTl = sb("fTl", [P, SEQ], F32R)
        lg = sb("lg", [P, NCH, NE])
        gmax = sb("gmax", [P, NCH])
        gexp = sb("gexp", [P, NCH, NE])
        gsum = sb("gsum", [P, NCH])
        gw_n = sb("gw_n", [P, NCH, NE])
        above = sb("above", [P, NCH, NE, NE])
        level = sb("level", [P, NCH, NE, NE])
        rank = sb("rank", [P, NCH * NE])
        kept = sb("kept", [P, NCH, NE])
        grem1 = sb("grem1", [P, NCH, NE])
        grem2 = sb("grem2", [P, NCH, NE])
        gparts = sb("gparts", [P, NCH, 3, NE], BF16)
        gT = sb("gT", [3 * NE, SEQ], BF16)
        wbc = late_part(NE * SEQ).rearrange("p (e t) -> p e t", e=NE)
        act_f = late_part(RING * SEQ).rearrange("p (r t) -> p r t", r=RING)
        act_h = sb("act_h", [P, RING, SEQ], F32R)
        act_l = sb("act_l", [P, RING, SEQ], F32R)
        acc = late_part(SEQ)
        term = late_part(SEQ)
        out_t = late_part(NCH * P).rearrange("p (c d) -> p c d", c=NCH)

        def f(ap):
            return ap.bitcast(F32)

        rows_in, win_in, wdt_in, wf_in, small_in = (sem(n) for n in ("rows_in", "win_in", "wdt_in", "wf_in", "small_in"))
        zeros_set, consts_set, tables_set = sem("zeros_set"), sem("consts_set"), sem("tables_set")
        cols_psum, cols_set, w_scaled, wdtT_psum, wdtT_set = (sem(n) for n in ("cols_psum", "cols_set", "w_scaled", "wdtT_psum", "wdtT_set"))
        wdt_psum, wdt_set, wh_set, weights_set, a_set, b2_set = (sem(n) for n in ("wdt_psum", "wdt_set", "wh_set", "weights_set", "a_set", "b2_set"))
        fh_set = sem("fh_set")
        x_loaded = sem("x_loaded")
        ln1_stats = sem("ln1_stats")
        ln1_mv = sem("ln1_mv")
        ln1_v = sem("ln1_v")
        ln1_rs = sem("ln1_rs")
        hn_ready = sem("hn_ready")
        hnT_psum = sem("hnT_psum")
        hTh_ready = sem("hTh_ready")
        hTl_ready = sem("hTl_ready")
        xr_scales = sem("xr_scales")
        xr_ready = sem("xr_ready")
        proj_psum = sem("proj_psum")
        xpad_ready = sem("xpad_ready")
        sz_ready = sem("sz_ready")
        dtv_ready = sem("dtv_ready")
        b_ready = sem("b_ready")
        c_ready = sem("c_ready")
        conv_step = sem("conv_step")
        xtok_psum = sem("xtok_psum")
        xs_ready = sem("xs_ready")
        dt_clamped = sem("dt_clamped")
        dt_exp = sem("dt_exp")
        dt_log = sem("dt_log")
        dt_steps = sem("dt_steps")
        lcs_psum = sem("lcs_psum")
        ecs_ready = sem("ecs_ready")
        lpart_steps = sem("lpart_steps")
        lT_psum = sem("lT_psum")
        lT_ready = sem("lT_ready")
        seg_psum = sem("seg_psum")
        decay_ready = sem("decay_ready")
        btok_psum = sem("btok_psum")
        btok_ready = sem("btok_ready")
        g_psum = sem("g_psum")
        mg_ready = sem("mg_ready")
        xw_ready = sem("xw_ready")
        xd_ready = sem("xd_ready")
        y_psum = sem("y_psum")
        s_psum = sem("s_psum")
        state_step = sem("state_step")
        y_steps = sem("y_steps")
        yz_ready = sem("yz_ready")
        ssq_ready = sem("ssq_ready")
        yT_psum = sem("yT_psum")
        yT_ready = sem("yT_ready")
        o_psum = sem("o_psum")
        msq_ready = sem("msq_ready")
        rstd_ready = sem("rstd_ready")
        x1_ready = sem("x1_ready")
        ln2_stats = sem("ln2_stats")
        ln2_mv = sem("ln2_mv")
        ln2_v = sem("ln2_v")
        ln2_rs = sem("ln2_rs")
        fn_ready = sem("fn_ready")
        fT_psum = sem("fT_psum")
        fTh_ready = sem("fTh_ready")
        fTl_ready = sem("fTl_ready")
        gate_psum = sem("gate_psum")
        gate_logits = sem("gate_logits")
        gate_exp = sem("gate_exp")
        gate_steps = sem("gate_steps")
        gate_kept = sem("gate_kept")
        gT_psum = sem("gT_psum")
        gT_ready = sem("gT_ready")
        wbc_psum = sem("wbc_psum")
        wbc_ready = sem("wbc_ready")
        hid_psum = sem("hid_psum")
        act_ready = sem("act_ready")
        act_h_ready = sem("act_h_ready")
        act_l_ready = sem("act_l_ready")
        second_done = sem("second_done")
        shared_ready = sem("shared_ready")
        term_ready = sem("term_ready")
        acc_ready = sem("acc_ready")
        outT_psum = sem("outT_psum")
        out_ready = sem("out_ready")
        out_stored = sem("out_stored")

        block = ctx.enter_context(nc.Block())

        def bodies(eng, body):
            body(0, None)
            body(1, 0)
            with eng.Fori(2, n_seq - 1) as s:
                body(s, s - 1)
            body(n_seq - 1, n_seq - 2)
            body(None, n_seq - 1)

        def at(k):
            return slice(k * P, (k + 1) * P)

        @block.sync
        def _(sp_eng):
            src = [a["sb1"].rearrange("n (b p) -> (n b) p", p=P), a["rb1"].rearrange("n (b p) -> (n b) p", p=P),
                   a["sb2"], a["rb2"], a["conv_b"].rearrange("(b p) -> b p", p=P),
                   a["w_norm_in"].rearrange("(b p) -> b p", p=P), a["w_norm_out"].rearrange("(b p) -> b p", p=P)]
            r = 0
            for v in src:
                sp_eng.dma_start(rows[r:r + v.shape[0], :], v).then_inc(rows_in, 16)
                r += v.shape[0]
            sp_eng.dma_start(w_raw, a["w_in_proj"]).then_inc(win_in, 16)
            sp_eng.dma_start(x_in[:], x_dram[0]).then_inc(x_loaded, 16)
            sp_eng.dma_start(w_dt[:], a["w_dt"]).then_inc(wdt_in, 16)
            sp_eng.dma_start(b_dt[:], a["b_dt"].partition_broadcast(P)).then_inc(small_in, 16)
            sp_eng.dma_start(a_log[:], a["A_log"].partition_broadcast(P)).then_inc(small_in, 16)
            sp_eng.dma_start(d_bc[:], a["D"].partition_broadcast(P)).then_inc(small_in, 16)
            sp_eng.dma_start(gb[:], a["gate_b"].partition_broadcast(P)).then_inc(small_in, 16)
            sp_eng.dma_start(gw[:], a["gate_w"]).then_inc(small_in, 16)
            sp_eng.dma_start(conv_w[:], a["conv_w"].rearrange("(b p) one k -> p b (one k)", p=P)).then_inc(small_in, 16)
            sp_eng.dma_start(w_out_raw[:], a["w_out_proj"].rearrange("(b p) o -> p b o", p=P)).then_inc(small_in, 16)
            sp_eng.dma_start(wf_raw[:, 0, 0:2, :], a["sw1"].rearrange("n d f -> d n f")).then_inc(wf_in, 16)
            sp_eng.dma_start(wf_raw[:, 0, 2:6, :], a["rw1"].rearrange("n d f -> d n f")).then_inc(wf_in, 16)
            sp_eng.dma_start(wf_raw[:, 1, 0:2, :].rearrange("p n (b o) -> p n b o", o=P),
                             a["sw2"].rearrange("n (b p) o -> p n b o", p=P)).then_inc(wf_in, 16)
            sp_eng.dma_start(wf_raw[:, 1, 2:6, :].rearrange("p n (b o) -> p n b o", o=P),
                             a["rw2"].rearrange("n (b p) o -> p n b o", p=P)).then_inc(wf_in, 16)

            def body(s, prev):
                if s is not None and not (is_seq(s, n_seq - 1)):
                    sp_eng.wait_ge(xr_ready, nth(s, 4, 4))
                    sp_eng.dma_start(x_in[:], x_dram[s + 1]).then_inc(x_loaded, 16)
                if prev is not None:
                    sp_eng.wait_ge(out_ready, nth(prev, 1, 1))
                    sp_eng.dma_start(out_dram[prev], out_t).then_inc(out_stored, 16)

            bodies(sp_eng, body)
            sp_eng.wait_ge(out_stored, 16 * n_seq)

        @block.tensor
        def _(pe):
            mm = nc.tensor.matmul

            pe.wait_ge(tables_set, 1)
            pe.wait_ge(rows_in, 7 * 16)
            nc.tensor.transpose(MAIN[0][:, 0:35], rows[:], ident[0:35, 0:35]).then_inc(cols_psum, 1)
            pe.wait_ge(w_scaled, 1)
            nc.tensor.transpose(MAIN[1][0:NH, 0:P], w_raw[:, 1536:1544], ident[:]).then_inc(wdtT_psum, 1)
            pe.wait_ge(wdtT_set, 1)
            pe.wait_ge(wdt_in, 16)
            mm(MAIN[2][:, 0:DI], wdtT[:], w_dt[:], start=True, stop=True).then_inc(wdt_psum, 1)

            def split(dst, stat_h, stat_l, mov_h, mov_l):
                mm(dst, stat_h, mov_l, start=True, stop=False)
                mm(dst, stat_l, mov_h, start=False, stop=False)
                return mm(dst, stat_h, mov_h, start=False, stop=True)

            def hn_transposes(s):
                if (v := nth(s, 1, -1)) is not None:
                    pe.wait_ge(out_ready, v)
                if is_seq(s, 0):
                    pe.wait_ge(tables_set, 4)
                for c in range(NCH):
                    pe.wait_ge(hn_ready, nth(s, 4, c + 1))
                    ins = nc.tensor.transpose(TR[:, at(c)], hn[:, c, :], ident[:])
                ins.then_inc(hnT_psum, 1)

            def proj(s, j):
                dst = MAIN[j % 4]
                pe.wait_ge(hTl_ready, nth(s, 1, 1))
                if is_seq(s, 0) and j == 0:
                    pe.wait_ge(weights_set, 1)
                if j in (0, 1) and (v := nth(s, 4, 0)) is not None:
                    pe.wait_ge(yz_ready if j == 0 else x1_ready, v)
                if j == 2 and (v := nth(s, 4, 0)) is not None:
                    pe.wait_ge(x1_ready, v)
                if j in (4, 5):
                    pe.wait_ge(xpad_ready, nth(s, 2, j - 3))
                if j in (6, 7, 8, 9):
                    pe.wait_ge(dtv_ready, nth(s, 4, j - 5))
                if j < 2:
                    ins = split(dst[:], wh[:, X0 + j * P:X0 + (j + 1) * P], wl[:, X0 + j * P:X0 + (j + 1) * P], hTh[:], hTl[:])
                elif j < 6:
                    c = j - 2
                    ins = split(dst[:], hTh[:, at(c)], hTl[:, at(c)], wh[:, 0:512], wl[:, 0:512])
                else:
                    k = B0 + (j - 6) * P
                    ins = split(dst[:], wh[:, k:k + P], wl[:, k:k + P], hTh[:], hTl[:])
                ins.then_inc(proj_psum, 1)

            def proj_c(s, b):
                dst = MAIN[(3, 1, 2, 3)[b]]
                if b == 0:
                    pe.wait_ge(b_ready, nth(s, 4, 2))
                if b == 1:
                    pe.wait_ge(b_ready, nth(s, 4, 4))
                if b == 2:
                    pe.wait_ge(xs_ready, nth(s, 2, 1))
                if b == 3:
                    pe.wait_ge(c_ready, nth(s, 4, 1))
                k = C0 + b * P
                split(dst[:], wh[:, k:k + P], wl[:, k:k + P], hTh[:], hTl[:]).then_inc(proj_psum, 1)

            def x_tokens(s, i):
                if i == 0:
                    pe.wait_ge(b_ready, nth(s, 4, 1))
                    pe.wait_ge(conv_step, nth(s, 8, 8))
                else:
                    pe.wait_ge(b_ready, nth(s, 4, 3))
                for j in range(2):
                    for b in range(NB):
                        ins = nc.tensor.transpose(MAIN[2 * (1 - i)][:, at(2 * j + b)], cv[:, b, at(2 * i + j)], ident[:])
                ins.then_inc(xtok_psum, 1)

            def lcs(s, prev):
                if prev is not None:
                    pe.wait_ge(wbc_ready, nth(prev, 4, 4))
                pe.wait_ge(dt_steps, nth(s, 3, 3))
                mm(TR[:, 0:32], upto[:], dta[:], start=True, stop=True)
                mm(TR[:, 32:64], ones[:], dta[:], start=True, stop=True).then_inc(lcs_psum, 1)

            def l_transposes(s):
                pe.wait_ge(ecs_ready, nth(s, 3, 3))
                pe.wait_ge(lpart_steps, nth(s, 5, 5))
                for c in range(NCH):
                    ins = nc.tensor.transpose(TR_BF[0:3 * NH, at(c)], lparts[:, c, :, :].rearrange("p a h -> p (a h)"), ident_bf[:])
                ins.then_inc(lT_psum, 1)

            def segments(s, c):
                for hf in range(2):
                    dst = MAIN[hf]
                    if c == 0 and hf == 0:
                        pe.wait_ge(lT_ready, nth(s, 1, 1))
                        pe.wait_ge(xs_ready, nth(s, 2, 2))
                        pe.wait_ge(c_ready, nth(s, 4, 2))
                    if c > 0 and hf == 0:
                        pe.wait_ge(yz_ready, nth(s, 4, c))
                    if c > 0 and hf == 1:
                        pe.wait_ge(state_step, nth(s, 8, (2, 5, 8)[c - 1]))
                    mm(dst[:], ident_bf[:], mask[:].rearrange("p n l -> p (n l)"), start=True, stop=False)
                    for n in range(NP):
                        mm(dst[:, at(n)], pick_head[:, 2 * n + hf, :], lT[:, at(c)], start=False, stop=False)
                    mm(dst[:], lT[:, at(c)], minus_head[:].rearrange("r (n t) l -> r t n l", t=2)[:, hf, :, :],
                       start=False, stop=True).then_inc(seg_psum, 1)

            def b_tokens(s, c):
                if c == 0:
                    pe.wait_ge(lT_ready, nth(s, 1, 1))
                    pe.wait_ge(b_ready, nth(s, 4, 4))
                else:
                    pe.wait_ge(yT_ready, nth(s, 4, c))
                for n in range(NP):
                    ins = nc.tensor.transpose(TR[:, at(n)], BT[:, n, at(c)], ident[:])
                ins.then_inc(btok_psum, 1)

            def gram(s, c):
                if c == 0:
                    pe.wait_ge(c_ready, nth(s, 4, 4))
                else:
                    pe.wait_ge(mg_ready, nth(s, 8, 2 * c))
                for n in range(NP):
                    for hf in range(2):
                        q = slice(NS * hf, NS * hf + NS)
                        ins = mm(MAIN[2 + hf][:, at(n)], BT[q, n, at(c)], CT[q, n, at(c)], start=True, stop=True)
                        if n == NP - 1:
                            ins.then_inc(g_psum, 1)

            def y_product(s, c):
                pe.wait_ge(decay_ready, nth(s, 8, 2 * c + 2))
                if c > 0:
                    pe.wait_ge(state_step, nth(s, 8, (2, 5, 8)[c - 1]))
                    for n in range(NP):
                        mm(MAIN[0][:, 256 + n * 64:320 + n * 64], CT[:, n, at(c)], state[:, n, :], start=True, stop=True)
                if c < NCH - 1:
                    pe.wait_ge(btok_ready, nth(s, 3, c + 1))
                    pe.wait_ge(xw_ready, nth(s, 6, 2 * c + 2))
                    for n in range(NP):
                        ins = mm(MAIN[1][:, n * 64:(n + 1) * 64], btok[:, at(n)], xw[:, n, :, :].rearrange("p t d -> p (t d)"),
                                 start=True, stop=True)
                    ins.then_inc(s_psum, 1)
                pe.wait_ge(mg_ready, nth(s, 8, 2 * c + 2))
                for hf in range(2):
                    for n in range(NP):
                        h = 2 * n + hf
                        ins = mm(MAIN[0][:, h * HD:(h + 1) * HD], mg[:, hf, n, :], xs[:, c, h * HD:(h + 1) * HD],
                                 start=True, stop=True)
                ins.then_inc(y_psum, 1)

            def y_transposes(s, c, prev):
                if c < NCH - 1:
                    pe.wait_ge(btok_ready, nth(s, 3, c + 1))
                else:
                    pe.wait_ge(yT_ready, nth(s, 4, c))
                pe.wait_ge(yz_ready, nth(s, 4, c + 1))
                for b in range(NB):
                    ins = nc.tensor.transpose(TR[:, at(b)], yz[:, at(b)], ident[:])
                ins.then_inc(yT_psum, 1)

            def out_projection(s):
                pe.wait_ge(mg_ready, nth(s, 8, 8))
                pe.wait_ge(yT_ready, nth(s, 4, 4))
                for c in range(NCH):
                    for b in range(NB):
                        ins = mm(MAIN[2][:, at(c)], yT[:, b, at(c)], w_out[:, b, :], start=(b == 0), stop=(b == NB - 1))
                ins.then_inc(o_psum, 1)

            def f_transposes(s, prev):
                if s is not None:
                    pe.wait_ge(hTl_ready, nth(s, 1, 1))
                elif (v := nth(prev, 1, 0)) is not None:
                    pe.wait_ge(out_ready, v)
                    pe.wait_ge(yT_ready, nth(prev, 4, 4))
                for c in range(NCH):
                    pe.wait_ge(fn_ready, nth(prev, 4, c + 1))
                    ins = nc.tensor.transpose(TR[:, at(c)], fn[:, c, :], ident[:])
                ins.then_inc(fT_psum, 1)

            def gate(prev):
                pe.wait_ge(fTl_ready, nth(prev, 1, 1))
                for c in range(NCH):
                    ins = split(TR[:, c * NE:(c + 1) * NE], fTh[:, at(c)], fTl[:, at(c)], gwh[:], gwl[:])
                ins.then_inc(gate_psum, 1)

            def g_transposes(prev):
                pe.wait_ge(gate_steps, nth(prev, 13, 13))
                for c in range(NCH):
                    ins = nc.tensor.transpose(TR_BF[0:3 * NE, at(c)], gparts[:, c, :, :].rearrange("p a h -> p (a h)"), ident_bf[:])
                ins.then_inc(gT_psum, 1)

            def weight_rows(prev, e):
                if e == 0:
                    pe.wait_ge(gT_ready, nth(prev, 1, 1))
                else:
                    pe.wait_ge(wbc_ready, nth(prev, 4, e))
                mm(TR[:], pick_expert[:, e, :], gT[:], start=True, stop=True).then_inc(wbc_psum, 1)

            def first(prev, b):
                if is_seq(prev, 0) and b == 0:
                    pe.wait_ge(fh_set, 4)
                g, k = divmod(b, NF)
                if (v := nth(prev, NBLK, b - 1)) is not None:
                    pe.wait_ge(act_ready, v)
                if b == 0:
                    pe.wait_ge(fTl_ready, nth(prev, 1, 1))
                split(HID[b % 2][:], w1h[:, g, at(k)], w1l[:, g, at(k)], fTh[:], fTl[:]).then_inc(hid_psum, 1)

            def second(prev, b):
                g, k = divmod(b, NF)
                begins = b in (0, 8, 12, 16, 20)
                ends = b in (7, 11, 15, 19, 23)
                if b == 0:
                    if (v := nth(prev, 4, 0)) is not None:
                        pe.wait_ge(term_ready, v)
                if b == 8:
                    pe.wait_ge(shared_ready, nth(prev, 1, 1))
                if b in (12, 16, 20):
                    pe.wait_ge(term_ready, nth(prev, 4, b // 4 - 2))
                r = b % RING
                pe.wait_ge(act_l_ready, nth(prev, NBLK, b + 1))
                mm(FOUT[:], w2h[:, g, k, :], act_l[:, r, :], start=begins, stop=False)
                mm(FOUT[:], w2l[:, g, k, :], act_h[:, r, :], start=False, stop=False)
                mm(FOUT[:], w2h[:, g, k, :], act_h[:, r, :], start=False, stop=ends).then_inc(second_done, 1)

            def out_transposes(s, prev):
                if s is not None:
                    pe.wait_ge(yT_ready, nth(s, 4, 4))
                else:
                    pe.wait_ge(wbc_ready, nth(prev, 4, 4))
                pe.wait_ge(acc_ready, nth(prev, 4, 4))
                for c in range(NCH):
                    ins = nc.tensor.transpose(TR[:, at(c)], acc[:, at(c)], ident[:])
                ins.then_inc(outT_psum, 1)

            def body(s, prev):
                if s is not None:
                    hn_transposes(s)
                    proj(s, 0)
                    proj(s, 1)
                if prev is not None:
                    f_transposes(s, prev)
                if s is not None:
                    proj(s, 2)
                    proj(s, 3)
                if prev is not None:
                    gate(prev)
                if s is not None:
                    proj(s, 4)
                    proj(s, 5)
                for b in range(NBLK):
                    if s is not None:
                        if b in (0, 1):
                            proj(s, 6 + 2 * b)
                            proj(s, 7 + 2 * b)
                        if b in (2, 3):
                            x_tokens(s, b - 2)
                            proj_c(s, b - 2)
                        if b in (4, 5):
                            proj_c(s, b - 2)
                    if prev is not None:
                        if b == 5:
                            g_transposes(prev)
                        if b in (6, 7):
                            weight_rows(prev, 2 * b - 12)
                            weight_rows(prev, 2 * b - 11)
                    if s is not None:
                        if b == 8:
                            lcs(s, prev)
                        if b == 9:
                            l_transposes(s)
                        if b >= 10:
                            attend(s, b - 10, prev)
                    if prev is not None:
                        first(prev, b)
                        if b >= LAG:
                            second(prev, b - LAG)
                if s is not None:
                    for k in range(14, 16):
                        attend(s, k, prev)
                if prev is not None:
                    second(prev, NBLK - 2)
                    second(prev, NBLK - 1)
                if s is not None:
                    out_projection(s)
                if prev is not None:
                    out_transposes(s, prev)

            def attend(s, k, prev):
                c, step = divmod(k, 4)
                if step == 0:
                    segments(s, c)
                if step == 0 and c < NCH - 1:
                    b_tokens(s, c)
                if step == 1:
                    gram(s, c)
                if step == 2:
                    y_product(s, c)
                if step == 3:
                    y_transposes(s, c, prev)

            bodies(pe, body)

        @block.scalar
        def _(act):
            nc.scalar.preload_act_table_set("natural_log_exp_and_others")
            act.wait_ge(small_in, 7 * 16)
            nc.scalar.activation(a_exp[:], a_log[:], ACT.Exp).then_inc(a_set, 1)
            act.wait_ge(cols_psum, 1)
            nc.scalar.copy(cols[:], MAIN[0][:, 0:35]).then_inc(cols_set, 1)
            act.wait_ge(wdtT_psum, 1)
            nc.scalar.copy(wdtT[:], MAIN[1][0:NH, 0:P]).then_inc(wdtT_set, 1)
            act.wait_ge(cols_set, 1)
            nc.scalar.activation(b2sh[:], b2s[:, 0:1], ACT.Identity, bias=b2s[:, 1:2]).then_inc(b2_set, 1)
            act.wait_ge(b2_set, 1)
            nc.scalar.mul(b2sum[:], b2sh[:], 0.5).then_inc(b2_set, 1)
            act.wait_ge(b2_set, 2)

            def hT(s):
                act.wait_ge(hnT_psum, nth(s, 1, 1))
                nc.scalar.copy(hTh[:], TR[:]).then_inc(hTh_ready, 1)

            def x_copy(s, b):
                act.wait_ge(proj_psum, nth(s, 14, b + 1))
                nc.scalar.copy(xpad[:, b, TAPS - 1:], MAIN[b][:]).then_inc(xpad_ready, 1)

            def fT(prev):
                act.wait_ge(fT_psum, nth(prev, 1, 1))
                nc.scalar.copy(fTh[:], TR[:]).then_inc(fTh_ready, 1)

            def silu_z(s, c):
                act.wait_ge(proj_psum, nth(s, 14, c + 3))
                nc.scalar.activation(sz[:, c, :], MAIN[(c + 2) % 4][:, 0:DI], ACT.Silu).then_inc(sz_ready, 1)

            def b_copy(s, b):
                act.wait_ge(proj_psum, nth(s, 14, b + 7))
                nc.scalar.copy(BT[:, b, :], MAIN[(b + 2) % 4][:]).then_inc(b_ready, 1)

            def silu_x(s, i):
                act.wait_ge(xtok_psum, nth(s, 2, i + 1))
                nc.scalar.activation(xs[:, 2 * i:2 * i + 2, :].rearrange("p c d -> p (c d)"), MAIN[2 * (1 - i)][:], ACT.Silu)\
                    .then_inc(xs_ready, 1)

            def softplus(s):
                act.wait_ge(dt_clamped, nth(s, 1, 1))
                nc.scalar.activation(sp[:], sp[:], ACT.Exp).then_inc(dt_exp, 1)
                act.wait_ge(dt_exp, nth(s, 1, 1))
                nc.scalar.activation(sp[:], sp[:], ACT.Ln, bias=1.0).then_inc(dt_log, 1)

            def gate_exps(prev):
                act.wait_ge(gate_logits, nth(prev, 3, 3))
                nc.scalar.activation(gexp[:], lg[:], ACT.Exp).then_inc(gate_exp, 1)

            def chunk_decays(s):
                act.wait_ge(lcs_psum, nth(s, 1, 1))
                nc.scalar.activation(ecs[:].rearrange("p c h -> p (c h)"), TR[:, 0:32], ACT.Exp).then_inc(ecs_ready, 1)
                tot = TR[:, 32:64].rearrange("p (c n t) -> p c n t", n=NP, t=2)
                for t in range(2):
                    q = slice(64 * t, 64 * t + 64)
                    nc.scalar.activation(tdx[q, :, :], tot[q, :, :, t], ACT.Exp).then_inc(ecs_ready, 1)

            def weight_copy(prev, e):
                act.wait_ge(wbc_psum, nth(prev, 4, e + 1))
                nc.scalar.copy(wbc[:, e, :], TR[:]).then_inc(wbc_ready, 1)

            def relu(prev, b):
                act.wait_ge(hid_psum, nth(prev, NBLK, b + 1))
                if (v := nth(prev, NBLK, b + 1 - RING)) is not None:
                    act.wait_ge(act_l_ready, v)
                nc.scalar.activation(act_f[:, b % RING, :], HID[b % 2][:], ACT.Relu, bias=b1[:, b:b + 1])\
                    .then_inc(act_ready, 1)

            def shared_out(prev):
                act.wait_ge(second_done, nth(prev, NBLK, 8))
                if (v := nth(prev, 1, 0)) is not None:
                    act.wait_ge(outT_psum, v)
                nc.scalar.activation(acc, FOUT[:], ACT.Identity, bias=b2sum[:], scale=0.5).then_inc(shared_ready, 1)

            def attend(s, k):
                c, step = divmod(k, 4)
                if step == 0:
                    for hf in range(2):
                        act.wait_ge(seg_psum, nth(s, 8, 2 * c + hf + 1))
                        if hf == 0 and (v := nth(s, 8, 2 * c)) is not None:
                            act.wait_ge(mg_ready, v)
                        if c > 0 and hf == 0:
                            act.wait_ge(xw_ready, nth(s, 6, 2 * c))
                        nc.scalar.activation(decay[:, hf, :, :].rearrange("p n l -> p (n l)"), MAIN[hf][:], ACT.Exp)\
                            .then_inc(decay_ready, 1)
                if step == 0 and c < NCH - 1:
                    act.wait_ge(btok_psum, nth(s, 3, c + 1))
                    nc.scalar.copy(btok[:], TR[:]).then_inc(btok_ready, 1)
                if step == 3:
                    act.wait_ge(yz_ready, nth(s, 4, c + 1))
                    nc.scalar.activation(junk[:], yz[:], ACT.Square, accum_out=ssq[:, c:c + 1]).then_inc(ssq_ready, 1)
                    act.wait_ge(yT_psum, nth(s, 4, c + 1))
                    nc.scalar.copy(yT[:, :, at(c)], TR[:, 0:DI].rearrange("p (b t) -> p b t", t=P)).then_inc(yT_ready, 1)

            def body(s, prev):
                if s is not None:
                    hT(s)
                    x_copy(s, 0)
                    x_copy(s, 1)
                if prev is not None:
                    fT(prev)
                if s is not None:
                    nc.scalar.preload_act_table_set("silu_and_others")
                    for c in range(NCH):
                        silu_z(s, c)
                for b in range(NBLK):
                    if s is not None:
                        if b in (0, 1):
                            b_copy(s, 2 * b)
                            b_copy(s, 2 * b + 1)
                        if b in (2, 3):
                            silu_x(s, b - 2)
                        if b == 3:
                            nc.scalar.preload_act_table_set("natural_log_exp_and_others")
                            softplus(s)
                    if prev is not None:
                        if b == 3:
                            gate_exps(prev)
                        if b in (6, 7):
                            weight_copy(prev, 2 * b - 12)
                            weight_copy(prev, 2 * b - 11)
                    if s is not None:
                        if b == 8:
                            chunk_decays(s)
                        if b >= 10:
                            attend(s, b - 10)
                    if prev is not None:
                        relu(prev, b)
                        if b == 7 + LAG:
                            shared_out(prev)
                if s is not None:
                    attend(s, 14)
                    attend(s, 15)

            bodies(act, body)

        @block.vector
        def _(dve):
            v_ = nc.vector

            dve.wait_ge(cols_set, 1)
            dve.wait_ge(win_in, 16)
            v_.tensor_scalar(w_raw, w_raw, wn_in, None, ALU.mult).then_inc(w_scaled, 1)
            dve.wait_ge(w_scaled, 1)
            v_.tensor_copy(w_all[:, 0:256], w_raw[:, 0:256]).then_inc(wdt_set, 1)
            v_.tensor_copy(w_all[:, X0:], w_raw[:, 256:1536]).then_inc(wdt_set, 1)
            dve.wait_ge(wdt_psum, 1)
            v_.tensor_copy(w_all[:, DT0:DT0 + DI], MAIN[2][:, 0:DI]).then_inc(wdt_set, 1)
            dve.wait_ge(wdt_set, 3)
            v_.tensor_copy(wh[:], w_all).then_inc(wh_set, 1)
            dve.wait_ge(wh_set, 1)
            v_.tensor_tensor(wl[:], w_all, f(wh[:]), ALU.subtract).then_inc(weights_set, 1)
            dve.wait_ge(a_set, 1)
            v_.tensor_scalar(a_neg[:], a_exp[:], -1.0 / HD, None, ALU.mult).then_inc(a_set, 1)
            v_.tensor_copy(gwh[:], gw[:]).then_inc(a_set, 1)
            dve.wait_ge(a_set, 3)
            v_.tensor_tensor(gwl[:], gw[:], f(gwh[:]), ALU.subtract).then_inc(a_set, 1)
            for b in range(NB):
                v_.tensor_scalar(w_out[:, b, :], w_out_raw[:, b, :], wn_out[:, b:b + 1], None, ALU.mult).then_inc(a_set, 1)
            dve.wait_ge(a_set, 6)

            def split_ffn():
                dve.wait_ge(wf_in, 4 * 16)
                v_.tensor_copy(w1h[:], wf_raw[:, 0]).then_inc(fh_set, 1)
                v_.tensor_copy(w2h[:].rearrange("p n b o -> p (n b o)"), wf_raw[:, 1].rearrange("p n f -> p (n f)")).then_inc(fh_set, 1)
                dve.wait_ge(fh_set, 2)
                v_.tensor_tensor(w1l[:], wf_raw[:, 0], f(w1h[:]), ALU.subtract).then_inc(fh_set, 1)
                v_.tensor_tensor(w2l[:].rearrange("p n b o -> p (n b o)"), wf_raw[:, 1].rearrange("p n f -> p (n f)"),
                                 f(w2h[:].rearrange("p n b o -> p (n b o)")), ALU.subtract).then_inc(fh_set, 1)

            def norm1(s):
                dve.wait_ge(x_loaded, nth(s, 16, 16))
                for c in range(NCH):
                    v_.bn_stats(st1[:, c, :], x_in[:, c, :]).then_inc(ln1_stats, 1)
                dve.wait_ge(ln1_stats, nth(s, 4, 4))
                v_.memset(carrier[:, RING:RING + 1], 0.0)
                for c in range(NCH):
                    v_.bn_aggr(mv1[:, c, :], st1[:, c, :]).then_inc(ln1_mv, 1)
                dve.wait_ge(ln1_mv, nth(s, 4, 4))
                v_.tensor_scalar(v1[:, 0, :], mv1[:, :, 1], LN_EPS, None, ALU.add).then_inc(ln1_v, 1)
                v_.tensor_scalar(v1[:, 1, :], mv1[:, :, 1], 1.0 + RMS_EPS, LN_EPS * RMS_EPS, ALU.mult, ALU.add).then_inc(ln1_v, 1)

            def norm1_apply(s):
                dve.wait_ge(ln1_rs, nth(s, 1, 1))
                if (v := nth(s, 1, 0)) is not None:
                    dve.wait_ge(hnT_psum, v)
                for c in range(NCH):
                    v_.tensor_scalar(hn[:, c, :], x_in[:, c, :], mv1[:, c, 0:1], rs1[:, 1, c:c + 1], ALU.subtract, ALU.mult)\
                        .then_inc(hn_ready, 1)

            def residual(s):
                v_.tensor_scalar(one_rs[:], rs1[:, 0, :], 1.0, None, ALU.add).then_inc(xr_scales, 1)
                v_.tensor_tensor(mean_rs[:], mv1[:, :, 0], rs1[:, 0, :], ALU.mult).then_inc(xr_scales, 1)
                dve.wait_ge(xr_scales, nth(s, 2, 2))
                for c in range(NCH):
                    v_.tensor_scalar(xr[:, c, :], x_in[:, c, :], one_rs[:, c:c + 1], mean_rs[:, c:c + 1], ALU.mult, ALU.subtract)\
                        .then_inc(xr_ready, 1)

            def hT_low(s):
                dve.wait_ge(hTh_ready, nth(s, 1, 1))
                v_.tensor_tensor(hTl[:], TR[:], f(hTh[:]), ALU.subtract).then_inc(hTl_ready, 1)

            def conv(s, b):
                dve.wait_ge(xpad_ready, nth(s, 2, b + 1))
                v_.tensor_scalar(cv[:, b, :], xpad[:, b, 0:SEQ], conv_w[:, b, 0:1], conv_b[:, b:b + 1], ALU.mult, ALU.add)\
                    .then_inc(conv_step, 1)
                for k in range(1, TAPS):
                    dve.wait_ge(conv_step, nth(s, 8, 4 * b + k))
                    v_.scalar_tensor_tensor(cv[:, b, :], xpad[:, b, k:k + SEQ], conv_w[:, b, k:k + 1], cv[:, b, :],
                                            ALU.mult, ALU.add).then_inc(conv_step, 1)

            def dt_add(s, c):
                dve.wait_ge(sz_ready, nth(s, 4, c + 1))
                v_.tensor_tensor(dtv[:, c, :], MAIN[(c + 2) % 4][:, DI:2 * DI], b_dt[:], ALU.add).then_inc(dtv_ready, 1)

            def dt_clamp(s):
                dve.wait_ge(dtv_ready, nth(s, 4, 4))
                v_.tensor_scalar(sp[:], dtv[:], CLAMP, None, ALU.min).then_inc(dt_clamped, 1)

            def dt_decay(s):
                dve.wait_ge(dt_log, nth(s, 1, 1))
                v_.tensor_tensor(dtv[:], dtv[:], sp[:], ALU.max).then_inc(dt_steps, 1)
                dve.wait_ge(dt_steps, nth(s, 3, 1))
                v_.tensor_reduce(dsum[:], dtv[:].rearrange("p c (h d) -> p (c h) d", d=HD), AX_X, ALU.add).then_inc(dt_steps, 1)
                dve.wait_ge(dt_steps, nth(s, 3, 2))
                v_.tensor_tensor(dta[:].rearrange("p (c h) -> p c h", h=NH), dsum[:].rearrange("p (c h) -> p c h", h=NH),
                                 a_neg[:].unsqueeze(1).to_broadcast([P, NCH, NH]), ALU.mult).then_inc(dt_steps, 1)

            def three_parts(src, parts, r1, r2, steps, s, per, first):
                v_.tensor_copy(parts[:, :, 0, :], src).then_inc(steps, 1)
                dve.wait_ge(steps, nth(s, per, first + 1))
                v_.tensor_tensor(r1[:], src, parts[:, :, 0, :], ALU.subtract).then_inc(steps, 1)
                dve.wait_ge(steps, nth(s, per, first + 2))
                v_.tensor_copy(parts[:, :, 1, :], r1[:]).then_inc(steps, 1)
                dve.wait_ge(steps, nth(s, per, first + 3))
                v_.tensor_tensor(r2[:], r1[:], parts[:, :, 1, :], ALU.subtract).then_inc(steps, 1)
                dve.wait_ge(steps, nth(s, per, first + 4))
                v_.tensor_copy(parts[:, :, 2, :], r2[:]).then_inc(steps, 1)

            def l_parts(s):
                dve.wait_ge(ecs_ready, nth(s, 3, 3))
                three_parts(TR[:, 0:32].rearrange("p (c h) -> p c h", h=NH), lparts, rem1, rem2, lpart_steps, s, 5, 0)

            def lT_copy(s):
                dve.wait_ge(lT_psum, nth(s, 1, 1))
                v_.tensor_copy(lT[:], TR_BF[0:3 * NH, :]).then_inc(lT_ready, 1)

            def c_copy(s, b):
                dve.wait_ge(proj_psum, nth(s, 14, b + 11))
                v_.tensor_copy(CT[:, b, :], MAIN[(3, 1, 2, 3)[b]][:]).then_inc(c_ready, 1)

            def attend(s, k):
                c, step = divmod(k, 4)
                if step == 1:
                    for hf in range(2):
                        dve.wait_ge(g_psum, nth(s, 8, 2 * c + hf + 1))
                        dve.wait_ge(decay_ready, nth(s, 8, 2 * c + hf + 1))
                        if hf == 0 and (v := nth(s, 4, c)) is not None:
                            dve.wait_ge(y_psum, v)
                        v_.tensor_tensor(mg[:, hf, :, :].rearrange("p n l -> p (n l)"), MAIN[2 + hf][:],
                                         decay[:, hf, :, :].rearrange("p n l -> p (n l)"), ALU.mult).then_inc(mg_ready, 1)
                if step == 2:
                    if c < NCH - 1:
                        first = (0, 2, 5)[c]
                        if c > 0:
                            v_.tensor_tensor(state_m[:], state[:], tdx[:, c, :].unsqueeze(2).to_broadcast([P, NP, 2 * HD]),
                                             ALU.mult).then_inc(state_step, 1)
                            dve.wait_ge(state_step, nth(s, 8, first + 1))
                            first += 1
                        dve.wait_ge(s_psum, nth(s, 3, c + 1))
                        if (v := nth(s, 4, c + 1 if c > 0 else 0)) is not None:
                            dve.wait_ge(y_psum, v)
                        own = MAIN[1][:, 0:256].rearrange("p (n d) -> p n d", n=NP)
                        for t in range(2):
                            q, d = slice(64 * t, 64 * t + 64), slice(HD * t, HD * t + HD)
                            if c == 0:
                                v_.tensor_copy(state[q, :, d], own[q, :, d]).then_inc(state_step, 1)
                            else:
                                v_.tensor_tensor(state[q, :, d], own[q, :, d], state_m[q, :, d], ALU.add).then_inc(state_step, 1)
                        dve.wait_ge(state_step, nth(s, 8, first + 2))
                    dve.wait_ge(y_psum, nth(s, 4, c + 1))
                    dve.wait_ge(xd_ready, nth(s, 4, c + 1))
                    if c == 0:
                        v_.tensor_tensor(yt[:], MAIN[0][:, 0:DI], xd[:], ALU.add).then_inc(y_steps, 1)
                        dve.wait_ge(y_steps, nth(s, 10, 1))
                    else:
                        first = 3 * c - 2
                        v_.tensor_tensor(yt[:].rearrange("p (h d) -> p h d", h=NH),
                                         MAIN[0][:, DI:2 * DI].rearrange("p (h d) -> p h d", h=NH),
                                         ecs[:, c, :].unsqueeze(2).to_broadcast([P, NH, HD]), ALU.mult).then_inc(y_steps, 1)
                        dve.wait_ge(y_steps, nth(s, 10, first + 1))
                        v_.tensor_tensor(yt[:], MAIN[0][:, 0:DI], yt[:], ALU.add).then_inc(y_steps, 1)
                        dve.wait_ge(y_steps, nth(s, 10, first + 2))
                        v_.tensor_tensor(yt[:], yt[:], xd[:], ALU.add).then_inc(y_steps, 1)
                        dve.wait_ge(y_steps, nth(s, 10, first + 3))
                    if (v := nth(s, 4, c)) is not None:
                        dve.wait_ge(ssq_ready, v)
                        dve.wait_ge(yT_psum, v)
                    v_.tensor_tensor(yz[:], yt[:], sz[:, c, :], ALU.mult).then_inc(yz_ready, 1)

            def mean_square(s):
                dve.wait_ge(ssq_ready, nth(s, 4, 4))
                v_.tensor_scalar(msq[:], ssq[:], 1.0 / DI, RMS_EPS, ALU.mult, ALU.add).then_inc(msq_ready, 1)

            def add_residual(prev):
                dve.wait_ge(o_psum, nth(prev, 1, 1))
                dve.wait_ge(rstd_ready, nth(prev, 1, 1))
                if (v := nth(prev, 1, 0)) is not None:
                    dve.wait_ge(out_ready, v)
                for c in range(NCH):
                    v_.scalar_tensor_tensor(x1[:, c, :], MAIN[2][:, at(c)], rstd[:, c:c + 1], xr[:, c, :], ALU.mult, ALU.add)\
                        .then_inc(x1_ready, 1)

            def norm2(prev):
                dve.wait_ge(x1_ready, nth(prev, 4, 4))
                for c in range(NCH):
                    v_.bn_stats(st2[:, c, :], x1[:, c, :]).then_inc(ln2_stats, 1)
                dve.wait_ge(ln2_stats, nth(prev, 4, 4))
                v_.memset(carrier[:, RING:RING + 1], 0.0)
                for c in range(NCH):
                    v_.bn_aggr(mv2[:, c, :], st2[:, c, :]).then_inc(ln2_mv, 1)
                dve.wait_ge(ln2_mv, nth(prev, 4, 4))
                v_.tensor_scalar(v2[:], mv2[:, :, 1], LN_EPS, None, ALU.add).then_inc(ln2_v, 1)

            def norm2_apply(prev):
                dve.wait_ge(ln2_rs, nth(prev, 1, 1))
                for c in range(NCH):
                    v_.tensor_scalar(fn[:, c, :], x1[:, c, :], mv2[:, c, 0:1], rs2[:, c:c + 1], ALU.subtract, ALU.mult)\
                        .then_inc(fn_ready, 1)

            def fT_low(prev):
                dve.wait_ge(fTh_ready, nth(prev, 1, 1))
                v_.tensor_tensor(fTl[:], TR[:], f(fTh[:]), ALU.subtract).then_inc(fTl_ready, 1)

            def logits(prev):
                dve.wait_ge(gate_psum, nth(prev, 1, 1))
                v_.tensor_tensor(lg[:], TR[:, 0:NCH * NE].rearrange("p (c e) -> p c e", e=NE),
                                 gb[:].unsqueeze(1).to_broadcast([P, NCH, NE]), ALU.add).then_inc(gate_logits, 1)
                dve.wait_ge(gate_logits, nth(prev, 3, 1))
                v_.tensor_reduce(gmax[:], lg[:], AX_X, ALU.max).then_inc(gate_logits, 1)
                dve.wait_ge(gate_logits, nth(prev, 3, 2))
                v_.tensor_tensor(lg[:], lg[:], gmax[:].unsqueeze(2).to_broadcast([P, NCH, NE]), ALU.subtract).then_inc(gate_logits, 1)

            def top_two(prev):
                def step(k):
                    dve.wait_ge(gate_steps, nth(prev, 13, k))
                dve.wait_ge(gate_exp, nth(prev, 1, 1))
                v_.tensor_reduce(gsum[:], gexp[:], AX_X, ALU.add).then_inc(gate_steps, 1)
                step(1)
                v_.reciprocal(gsum[:], gsum[:]).then_inc(gate_steps, 1)
                step(2)
                v_.tensor_tensor(gw_n[:], gexp[:], gsum[:].unsqueeze(2).to_broadcast([P, NCH, NE]), ALU.mult).then_inc(gate_steps, 1)
                step(3)
                mine = gw_n[:].unsqueeze(3).to_broadcast([P, NCH, NE, NE])
                other = gw_n[:].unsqueeze(2).to_broadcast([P, NCH, NE, NE])
                v_.tensor_tensor(above[:], mine, other, ALU.is_lt).then_inc(gate_steps, 1)
                v_.tensor_tensor(level[:], mine, other, ALU.is_le).then_inc(gate_steps, 1)
                step(5)
                v_.tensor_tensor(level[:].rearrange("p c e j -> p c (e j)"), level[:].rearrange("p c e j -> p c (e j)"),
                                 lower[:].rearrange("p e j -> p (e j)").unsqueeze(1).to_broadcast([P, NCH, NE * NE]),
                                 ALU.mult).then_inc(gate_steps, 1)
                step(6)
                v_.tensor_tensor(above[:], above[:], level[:], ALU.max).then_inc(gate_steps, 1)
                step(7)
                v_.tensor_reduce(rank[:], above[:].rearrange("p c e j -> p (c e) j"), AX_X, ALU.add).then_inc(gate_steps, 1)
                step(8)
                v_.scalar_tensor_tensor(kept[:].rearrange("p c e -> p (c e)"), rank[:], 1.5, gw_n[:].rearrange("p c e -> p (c e)"),
                                        ALU.is_lt, ALU.mult).then_inc(gate_kept, 1)
                dve.wait_ge(gate_kept, nth(prev, 1, 1))
                three_parts(kept[:], gparts, grem1, grem2, gate_steps, prev, 13, 8)

            def gT_copy(prev):
                dve.wait_ge(gT_psum, nth(prev, 1, 1))
                v_.tensor_copy(gT[:], TR_BF[0:3 * NE, :]).then_inc(gT_ready, 1)

            def act_low(prev, b):
                r = b % RING
                dve.wait_ge(act_h_ready, nth(prev, NBLK, b + 1))
                v_.tensor_tensor(act_l[:, r, :], act_f[:, r, :], f(act_h[:, r, :]), ALU.subtract).then_inc(act_l_ready, 1)

            def routed_out(prev, e):
                dve.wait_ge(second_done, nth(prev, NBLK, 12 + 4 * e))
                dve.wait_ge(wbc_ready, nth(prev, 4, 4))
                if (v := nth(prev, 4, e)) is not None:
                    dve.wait_ge(acc_ready, v)
                v_.scalar_tensor_tensor(term, FOUT[:], b2r[:, e:e + 1], wbc[:, e, :], ALU.add, ALU.mult).then_inc(term_ready, 1)

            def store(prev):
                dve.wait_ge(outT_psum, nth(prev, 1, 1))
                if (v := nth(prev, 16, 0)) is not None:
                    dve.wait_ge(out_stored, v)
                v_.tensor_tensor(out_t.rearrange("p c d -> p (c d)"), TR[:], x1.rearrange("p c d -> p (c d)"), ALU.add)\
                    .then_inc(out_ready, 1)



            def body(s, prev):
                last = is_seq(s, n_seq - 1)
                if is_seq(s, 0):
                    norm1(s)
                    norm1_apply(s)
                if s is not None:
                    hT_low(s)
                if prev is not None:
                    add_residual(prev)
                    norm2(prev)
                if s is not None:
                    residual(s)
                if prev is not None:
                    norm2_apply(prev)
                if s is not None:
                    conv(s, 0)
                if prev is not None:
                    fT_low(prev)
                if s is not None:
                    dt_add(s, 0)
                    dt_add(s, 1)
                    conv(s, 1)
                if prev is not None:
                    logits(prev)
                if s is not None:
                    dt_add(s, 2)
                    dt_add(s, 3)
                    dt_clamp(s)
                if is_seq(s, 0):
                    split_ffn()
                for b in range(NBLK):
                    if s is not None:
                        if 2 <= b < 6:
                            c_copy(s, b - 2)
                        if b == 4:
                            dt_decay(s)
                        if b == 8:
                            l_parts(s)
                        if b == 9:
                            lT_copy(s)
                        if b >= 10:
                            attend(s, b - 10)
                        if b == 12 and not last:
                            norm1(s + 1)
                        if b == 14 and not last:
                            norm1_apply(s + 1)
                    if prev is not None:
                        act_low(prev, b)
                        if b == 4:
                            top_two(prev)
                        if b == 5:
                            gT_copy(prev)
                        if b in (11 + LAG, 15 + LAG, 19 + LAG):
                            routed_out(prev, (b - 11 - LAG) // 4)
                if s is not None:
                    attend(s, 14)
                    attend(s, 15)
                    mean_square(s)
                if prev is not None:
                    routed_out(prev, 3)
                    store(prev)

            bodies(dve, body)

        @block.gpsimd
        def _(pool):
            g = nc.gpsimd
            for t, v in ((ident, 0.0), (ident_bf, 0.0), (ones, 1.0), (upto, 1.0), (mask, 0.0), (pick_head, 0.0),
                         (minus_head, 0.0), (pick_expert, 0.0), (lower, 1.0), (half, -0.5), (state, 0.0)):
                g.memset(t[:], v).then_inc(zeros_set, 1)
            g.memset(xpad[:, :, 0:TAPS - 1], 0.0).then_inc(zeros_set, 1)
            pool.wait_ge(zeros_set, 12)
            g.affine_select(out=ident[:], in_=ident[:], pattern=[[-1, P]], compare_op=ALU.not_equal, fill=1.0, base=0,
                            channel_multiplier=1).then_inc(tables_set, 1)
            g.affine_select(out=ident_bf[:], in_=ident_bf[:], pattern=[[-1, P]], compare_op=ALU.not_equal, fill=1.0, base=0,
                            channel_multiplier=1).then_inc(tables_set, 1)
            g.affine_select(out=upto[:], in_=upto[:], pattern=[[1, P]], compare_op=ALU.is_ge, fill=0.0, base=0,
                            channel_multiplier=-1).then_inc(tables_set, 1)
            g.affine_select(out=mask[:], in_=mask[:], pattern=[[0, NP], [1, P]], compare_op=ALU.is_ge, fill=MASKED, base=0,
                            channel_multiplier=-1).then_inc(tables_set, 1)
            g.affine_select(out=lower[:], in_=lower[:], pattern=[[1, NE], [-1, NE]], compare_op=ALU.is_gt, fill=0.0, base=0,
                            channel_multiplier=0).then_inc(tables_set, 1)
            k = 5
            for t, n, v in ((pick_head, NH, 1.0), (minus_head, NH, -1.0), (pick_expert, NE, 1.0)):
                for part in range(3):
                    g.affine_select(out=t[:], in_=t[:], pattern=[[-1, n], [0, P]], compare_op=ALU.not_equal, fill=v,
                                    base=-part * n, channel_multiplier=1).then_inc(tables_set, 1)
                    k += 1
                    pool.wait_ge(tables_set, k)

            def rsqrt1(s):
                pool.wait_ge(ln1_v, nth(s, 2, 2))
                g.tensor_tensor(rs1[:].rearrange("p a c -> p (a c)"), v1[:].rearrange("p a c -> p (a c)"), half[:], ALU.pow)\
                    .then_inc(ln1_rs, 1)

            def rsqrt2(prev):
                pool.wait_ge(ln2_v, nth(prev, 1, 1))
                g.tensor_tensor(rs2[:], v2[:], half[:, 0:NCH], ALU.pow).then_inc(ln2_rs, 1)

            def rsqrt_y(s):
                pool.wait_ge(msq_ready, nth(s, 1, 1))
                g.tensor_tensor(rstd[:], msq[:], half[:, 0:NCH], ALU.pow).then_inc(rstd_ready, 1)

            def act_high(prev, b):
                r = b % RING
                pool.wait_ge(act_ready, nth(prev, NBLK, b + 1))
                if (v := nth(prev, NBLK, b + 1 - RING)) is not None:
                    pool.wait_ge(second_done, v)
                g.tensor_tensor(carrier[:, r:r + 1], half[:, 0:1], half[:, 1:2], ALU.add)
                g.tensor_copy(act_h[:, r, :], act_f[:, r, :]).then_inc(act_h_ready, 1)

            def skip(s, c):
                if c == 0:
                    pool.wait_ge(xs_ready, nth(s, 2, 2))
                if (v := nth(s, 4, c)) is not None:
                    pool.wait_ge(yz_ready, v)
                g.tensor_tensor(xd[:].rearrange("p (h d) -> p h d", h=NH), xs[:, c, :].rearrange("p (h d) -> p h d", h=NH),
                                d_bc[:].unsqueeze(2).to_broadcast([P, NH, HD]), ALU.mult).then_inc(xd_ready, 1)

            def weigh(s, c):
                for hf in range(2):
                    pool.wait_ge(decay_ready, nth(s, 8, 2 * c + hf + 1))
                    if hf == 0 and (v := nth(s, 3, c)) is not None:
                        pool.wait_ge(s_psum, v)
                    g.tensor_tensor(xw[:, :, hf, :], xs[:, c, :].rearrange("p (n t d) -> p n t d", n=NP, t=2)[:, :, hf, :],
                                    decay[:, hf, :, P - 1:P].to_broadcast([P, NP, HD]), ALU.mult).then_inc(xw_ready, 1)

            def add_term(prev, e):
                pool.wait_ge(term_ready, nth(prev, 4, e + 1))
                if e == 0:
                    pool.wait_ge(shared_ready, nth(prev, 1, 1))
                else:
                    pool.wait_ge(acc_ready, nth(prev, 4, e))
                g.tensor_tensor(acc, acc, term, ALU.add).then_inc(acc_ready, 1)

            def attend(s, k):
                c, step = divmod(k, 4)
                if step == 0:
                    skip(s, c)
                if step == 0 and c < NCH - 1:
                    weigh(s, c)

            def body(s, prev):
                last = is_seq(s, n_seq - 1)
                if is_seq(s, 0):
                    rsqrt1(0)
                if prev is not None:
                    rsqrt2(prev)
                for b in range(NBLK):
                    if s is not None:
                        if b >= 10:
                            attend(s, b - 10)
                        if b == 13 and not last:
                            rsqrt1(s + 1)
                    if prev is not None:
                        act_high(prev, b)
                        if b in (11 + LAG, 15 + LAG, 19 + LAG):
                            add_term(prev, (b - 11 - LAG) // 4)
                if s is not None:
                    rsqrt_y(s)
                if prev is not None:
                    add_term(prev, 3)

            bodies(pool, body)


_INS = ["hidden", "w_norm_in", "w_in_proj", "conv_w", "conv_b", "w_dt", "b_dt", "A_log", "D", "w_norm_out", "w_out_proj"]
_FFN = ["gate_w", "gate_b", "sw1", "sb1", "sw2", "sb2", "rw1", "rb1", "rw2", "rb2"]


def kernel(**inputs):
    import concourse.bacc as _bacc
    from concourse import mybir as _mybir
    from concourse.bass_utils import run_bass_kernel_spmd as _run

    nc = _bacc.Bacc("TRN2", target_bir_lowering=False, num_devices=1)
    arrays, args = {}, {}
    for name in ["L0_attn_" + n for n in _INS] + ["L0_ffn_" + n for n in _FFN]:
        v = np.ascontiguousarray(inputs[name])
        arrays[name + "_dram"] = v
        args[name.split("_", 2)[2]] = nc.dram_tensor(name + "_dram", v.shape, _mybir.dt.from_np(v.dtype), kind="ExternalInput").ap()
    out = nc.dram_tensor("out_dram", inputs["L0_attn_hidden"].shape, _mybir.dt.float32, kind="ExternalOutput").ap()
    build(nc, args, out)
    r = _run(nc, [arrays], core_ids=[0])
    return r.results[0]["out_dram"]
```

```python
from contextlib import ExitStack

import numpy as np

import concourse.bass as bass
from concourse import mybir

ALU = mybir.AluOpType
ACT = mybir.ActivationFunctionType
AX_X = mybir.AxisListType.X
F32 = mybir.dt.float32
F32R = mybir.dt.float32r
BF16 = mybir.dt.bfloat16

P = 128
NCH = 4
SEQ = NCH * P
DI = 256
NB = DI // P
NH = 8
NP = NH // 2
HD = DI // NH
NS = 64
NG = 6
NE = 4
NF = 4
NBLK = NG * NF
TAPS = 4
RING = 3
LAG = 2
CHUNKS_FROM = 12
LATE = 4
LN_EPS = 1e-5
RMS_EPS = float(np.finfo(np.float32).eps)
CLAMP = 30.0
MASKED = -1e30

Z0, DT0, X0, B0, C0, WCOLS = 0, 256, 512, 768, 1280, 1792


def nth(s, per, k):
    if isinstance(s, int) and s * per + k <= 0:
        return None
    return s * per + k


def is_seq(s, n):
    return isinstance(s, int) and s == n


def build(nc, a, out):
    n_seq = a["hidden"].shape[0]
    x_dram = a["hidden"].rearrange("s (c p) d -> s p c d", p=P)
    out_dram = out.rearrange("s (c p) d -> s p c d", p=P)

    with ExitStack() as ctx:
        def sb(name, shape, dt=F32):
            return ctx.enter_context(nc.sbuf_tensor(name, shape, dt))

        def sem(name):
            return ctx.enter_context(nc.semaphore(name))

        bank = [ctx.enter_context(nc.psum_tensor(f"bank{i}", [P, 512], F32)) for i in range(8)]
        HID = bank[0:2]
        FOUT = bank[2]
        TR = bank[3]
        MAIN = bank[4:8]
        TR_BF = TR[:, 0:256].bitcast(BF16)

        ident = sb("ident", [P, P])
        ident_bf = sb("ident_bf", [P, P], BF16)
        ones = sb("ones", [P, P])
        upto = sb("upto", [P, P])
        mask = sb("mask", [P, NP, P], BF16)
        pick_head = sb("pick_head", [3 * NH, NH, P], BF16)
        minus_head = sb("minus_head", [3 * NH, NH, P], BF16)
        pick_expert = sb("pick_expert", [3 * NE, NE, P], BF16)
        lower = sb("lower", [P, NE, NE])
        carrier = sb("carrier", [P, RING + 1])
        half = sb("half", [P, 8])

        BT = sb("BT", [P, NP, SEQ])
        CT = sb("CT", [P, NP, SEQ])
        w_all = BT[:].rearrange("p n t -> p (n t)")[:, 0:WCOLS]
        w_raw = CT[:].rearrange("p n t -> p (n t)")[:, 0:1544]
        wh = sb("wh", [P, WCOLS], F32R)
        wl = sb("wl", [P, WCOLS], F32R)
        rows = sb("rows", [35, P])
        cols = sb("cols", [P, 35])
        b1 = cols[:, 0:24]
        b2s = cols[:, 24:26]
        b2r = cols[:, 26:30]
        conv_b = cols[:, 30:32]
        wn_in = cols[:, 32:33]
        wn_out = cols[:, 33:35]
        b2sh = sb("b2sh", [P, 1])
        b2sum = sb("b2sum", [P, 1])
        conv_w = sb("conv_w", [P, NB, TAPS])
        w_dt = sb("w_dt", [NH, DI])
        wdtT = sb("wdtT", [NH, P])
        b_dt = sb("b_dt", [P, DI])
        a_log = sb("a_log", [P, NH])
        a_exp = sb("a_exp", [P, NH])
        a_neg = sb("a_neg", [P, NH])
        d_bc = sb("d_bc", [P, NH])
        w_out_raw = sb("w_out_raw", [P, NB, P])
        w_out = sb("w_out", [P, NB, P])
        gw = sb("gw", [P, NE])
        gwh = sb("gwh", [P, NE], F32R)
        gwl = sb("gwl", [P, NE], F32R)
        gb = sb("gb", [P, NE])
        late = sb("late", [P, 2 * NG * 512])
        wf_raw = late[:].rearrange("p (a n f) -> p a n f", a=2, n=NG)
        used = [0]

        def late_part(n):
            used[0] += n
            return late[:, used[0] - n:used[0]]

        w1h = sb("w1h", [P, NG, 512], F32R)
        w1l = sb("w1l", [P, NG, 512], F32R)
        w2h = sb("w2h", [P, NG, NF, P], F32R)
        w2l = sb("w2l", [P, NG, NF, P], F32R)

        x_in = sb("x_in", [P, NCH, P])
        st1 = sb("st1", [P, NCH, 6])
        mv1 = sb("mv1", [P, NCH, 2])
        v1 = sb("v1", [P, 2, NCH])
        rs1 = sb("rs1", [P, 2, NCH])
        one_rs = sb("one_rs", [P, NCH])
        mean_rs = sb("mean_rs", [P, NCH])
        hn = sb("hn", [P, NCH, P])
        xr = sb("xr", [P, NCH, P])
        hTh = sb("hTh", [P, SEQ], F32R)
        hTl = sb("hTl", [P, SEQ], F32R)
        xpad = sb("xpad", [P, NB, TAPS - 1 + SEQ])
        cv = sb("cv", [P, NB, SEQ])
        xs = sb("xs", [P, NCH, DI])
        sz = sb("sz", [P, NCH, DI])
        dtv = sb("dtv", [P, NCH, DI])
        sp = sb("sp", [P, NCH, DI])
        dsum = sb("dsum", [P, NCH * NH])
        dta = sb("dta", [P, NCH * NH])
        ecs = sb("ecs", [P, NCH, NH])
        tdx = sb("tdx", [P, NCH, NP])
        rem1 = sb("rem1", [P, NCH, NH])
        rem2 = sb("rem2", [P, NCH, NH])
        lparts = sb("lparts", [P, NCH, 3, NH], BF16)
        lT = sb("lT", [3 * NH, SEQ], BF16)
        btok = sb("btok", [P, NP * P])
        decay = sb("decay", [P, 2, NP, P])
        mg = sb("mg", [P, 2, NP, P])
        xw = sb("xw", [P, NP, 2, HD])
        xd = sb("xd", [P, DI])
        state = sb("state", [P, NP, 2 * HD])
        state_m = sb("state_m", [P, NP, 2 * HD])
        yt = sb("yt", [P, DI])
        yz = sb("yz", [P, DI])
        junk = sb("junk", [P, DI])
        ssq = sb("ssq", [P, NCH])
        msq = sb("msq", [P, NCH])
        rstd = sb("rstd", [P, NCH])
        yT = sb("yT", [P, NB, SEQ])
        x1 = late_part(NCH * P).rearrange("p (c d) -> p c d", c=NCH)
        st2 = sb("st2", [P, NCH, 6])
        mv2 = sb("mv2", [P, NCH, 2])
        v2 = sb("v2", [P, NCH])
        rs2 = sb("rs2", [P, NCH])
        x1_kept = sb("x1_kept", [P, NCH, P])
        fn = late_part(NCH * P).rearrange("p (c d) -> p c d", c=NCH)
        fTh = sb("fTh", [P, SEQ], F32R)
        fTl = sb("fTl", [P, SEQ], F32R)
        lg = sb("lg", [P, NCH, NE])
        gmax = sb("gmax", [P, NCH])
        gexp = sb("gexp", [P, NCH, NE])
        gsum = sb("gsum", [P, NCH])
        gw_n = sb("gw_n", [P, NCH, NE])
        above = sb("above", [P, NCH, NE, NE])
        level = sb("level", [P, NCH, NE, NE])
        rank = sb("rank", [P, NCH * NE])
        kept = sb("kept", [P, NCH, NE])
        grem1 = sb("grem1", [P, NCH, NE])
        grem2 = sb("grem2", [P, NCH, NE])
        gparts = sb("gparts", [P, NCH, 3, NE], BF16)
        gT = sb("gT", [3 * NE, SEQ], BF16)
        wbc = late_part(NE * SEQ).rearrange("p (e t) -> p e t", e=NE)
        act_f = late_part(RING * SEQ).rearrange("p (r t) -> p r t", r=RING)
        act_h = sb("act_h", [P, RING, SEQ], F32R)
        act_l = sb("act_l", [P, RING, SEQ], F32R)
        acc = late_part(SEQ)
        term = late_part(SEQ)
        out_t = late_part(NCH * P).rearrange("p (c d) -> p c d", c=NCH)

        def f(ap):
            return ap.bitcast(F32)

        rows_in, win_in, wdt_in, wf_in, small_in = (sem(n) for n in ("rows_in", "win_in", "wdt_in", "wf_in", "small_in"))
        zeros_set, consts_set, tables_set = sem("zeros_set"), sem("consts_set"), sem("tables_set")
        cols_psum, cols_set, w_scaled, wdtT_psum, wdtT_set = (sem(n) for n in ("cols_psum", "cols_set", "w_scaled", "wdtT_psum", "wdtT_set"))
        wdt_psum, wdt_set, wh_set, weights_set, a_set, b2_set = (sem(n) for n in ("wdt_psum", "wdt_set", "wh_set", "weights_set", "a_set", "b2_set"))
        fh_set = sem("fh_set")
        x_loaded = sem("x_loaded")
        ln1_stats = sem("ln1_stats")
        ln1_mv = sem("ln1_mv")
        ln1_v = sem("ln1_v")
        ln1_rs = sem("ln1_rs")
        hn_ready = sem("hn_ready")
        hnT_psum = sem("hnT_psum")
        hTh_ready = sem("hTh_ready")
        hTl_ready = sem("hTl_ready")
        xr_scales = sem("xr_scales")
        xr_ready = sem("xr_ready")
        proj_psum = sem("proj_psum")
        xpad_ready = sem("xpad_ready")
        sz_ready = sem("sz_ready")
        dtv_ready = sem("dtv_ready")
        b_ready = sem("b_ready")
        c_ready = sem("c_ready")
        conv_step = sem("conv_step")
        xtok_psum = sem("xtok_psum")
        xs_ready = sem("xs_ready")
        dt_clamped = sem("dt_clamped")
        dt_exp = sem("dt_exp")
        dt_log = sem("dt_log")
        dt_steps = sem("dt_steps")
        lcs_psum = sem("lcs_psum")
        ecs_ready = sem("ecs_ready")
        lpart_steps = sem("lpart_steps")
        lT_psum = sem("lT_psum")
        lT_ready = sem("lT_ready")
        seg_psum = sem("seg_psum")
        decay_ready = sem("decay_ready")
        btok_psum = sem("btok_psum")
        btok_ready = sem("btok_ready")
        g_psum = sem("g_psum")
        mg_ready = sem("mg_ready")
        xw_ready = sem("xw_ready")
        xd_ready = sem("xd_ready")
        y_psum = sem("y_psum")
        s_psum = sem("s_psum")
        state_step = sem("state_step")
        y_steps = sem("y_steps")
        yz_ready = sem("yz_ready")
        ssq_ready = sem("ssq_ready")
        yT_psum = sem("yT_psum")
        yT_ready = sem("yT_ready")
        o_psum = sem("o_psum")
        msq_ready = sem("msq_ready")
        rstd_ready = sem("rstd_ready")
        x1_ready = sem("x1_ready")
        x1_kept_ready = sem("x1_kept_ready")
        ln2_stats = sem("ln2_stats")
        ln2_mv = sem("ln2_mv")
        ln2_v = sem("ln2_v")
        ln2_rs = sem("ln2_rs")
        fn_ready = sem("fn_ready")
        fT_psum = sem("fT_psum")
        fTh_ready = sem("fTh_ready")
        fTl_ready = sem("fTl_ready")
        gate_psum = sem("gate_psum")
        gate_logits = sem("gate_logits")
        gate_exp = sem("gate_exp")
        gate_steps = sem("gate_steps")
        gate_kept = sem("gate_kept")
        gT_psum = sem("gT_psum")
        gT_ready = sem("gT_ready")
        wbc_psum = sem("wbc_psum")
        wbc_ready = sem("wbc_ready")
        hid_psum = sem("hid_psum")
        act_ready = sem("act_ready")
        act_h_ready = sem("act_h_ready")
        act_l_ready = sem("act_l_ready")
        second_done = sem("second_done")
        shared_ready = sem("shared_ready")
        term_ready = sem("term_ready")
        acc_ready = sem("acc_ready")
        outT_psum = sem("outT_psum")
        out_ready = sem("out_ready")
        out_stored = sem("out_stored")

        block = ctx.enter_context(nc.Block())

        def bodies(eng, body):
            body(0, None, None)
            body(1, 0, None)
            body(2, 1, 0)
            with eng.Fori(3, n_seq - 1) as s:
                body(s, s - 1, s - 2)
            body(n_seq - 1, n_seq - 2, n_seq - 3)
            body(None, n_seq - 1, n_seq - 2)
            body(None, None, n_seq - 1)

        def block_at(i, prev, older):
            q, b = (older, NBLK - LATE + i) if i < LATE else (prev, i - LATE)
            return None if q is None or i < 0 else (q, b)

        def at(k):
            return slice(k * P, (k + 1) * P)

        @block.sync
        def _(sp_eng):
            src = [a["sb1"].rearrange("n (b p) -> (n b) p", p=P), a["rb1"].rearrange("n (b p) -> (n b) p", p=P),
                   a["sb2"], a["rb2"], a["conv_b"].rearrange("(b p) -> b p", p=P),
                   a["w_norm_in"].rearrange("(b p) -> b p", p=P), a["w_norm_out"].rearrange("(b p) -> b p", p=P)]
            r = 0
            for v in src:
                sp_eng.dma_start(rows[r:r + v.shape[0], :], v).then_inc(rows_in, 16)
                r += v.shape[0]
            sp_eng.dma_start(w_raw, a["w_in_proj"]).then_inc(win_in, 16)
            sp_eng.dma_start(x_in[:], x_dram[0]).then_inc(x_loaded, 16)
            sp_eng.dma_start(w_dt[:], a["w_dt"]).then_inc(wdt_in, 16)
            sp_eng.dma_start(b_dt[:], a["b_dt"].partition_broadcast(P)).then_inc(small_in, 16)
            sp_eng.dma_start(a_log[:], a["A_log"].partition_broadcast(P)).then_inc(small_in, 16)
            sp_eng.dma_start(d_bc[:], a["D"].partition_broadcast(P)).then_inc(small_in, 16)
            sp_eng.dma_start(gb[:], a["gate_b"].partition_broadcast(P)).then_inc(small_in, 16)
            sp_eng.dma_start(gw[:], a["gate_w"]).then_inc(small_in, 16)
            sp_eng.dma_start(conv_w[:], a["conv_w"].rearrange("(b p) one k -> p b (one k)", p=P)).then_inc(small_in, 16)
            sp_eng.dma_start(w_out_raw[:], a["w_out_proj"].rearrange("(b p) o -> p b o", p=P)).then_inc(small_in, 16)
            sp_eng.dma_start(wf_raw[:, 0, 0:2, :], a["sw1"].rearrange("n d f -> d n f")).then_inc(wf_in, 16)
            sp_eng.dma_start(wf_raw[:, 0, 2:6, :], a["rw1"].rearrange("n d f -> d n f")).then_inc(wf_in, 16)
            sp_eng.dma_start(wf_raw[:, 1, 0:2, :].rearrange("p n (b o) -> p n b o", o=P),
                             a["sw2"].rearrange("n (b p) o -> p n b o", p=P)).then_inc(wf_in, 16)
            sp_eng.dma_start(wf_raw[:, 1, 2:6, :].rearrange("p n (b o) -> p n b o", o=P),
                             a["rw2"].rearrange("n (b p) o -> p n b o", p=P)).then_inc(wf_in, 16)

            def body(s, prev, older):
                if s is not None and not is_seq(s, n_seq - 1):
                    sp_eng.wait_ge(xr_ready, nth(s, 4, 4))
                    sp_eng.dma_start(x_in[:], x_dram[s + 1]).then_inc(x_loaded, 16)
                if older is not None:
                    sp_eng.wait_ge(out_ready, nth(older, 1, 1))
                    sp_eng.dma_start(out_dram[older], out_t).then_inc(out_stored, 16)

            bodies(sp_eng, body)
            sp_eng.wait_ge(out_stored, 16 * n_seq)

        @block.tensor
        def _(pe):
            mm = nc.tensor.matmul

            pe.wait_ge(tables_set, 1)
            pe.wait_ge(rows_in, 7 * 16)
            nc.tensor.transpose(MAIN[0][:, 0:35], rows[:], ident[0:35, 0:35]).then_inc(cols_psum, 1)
            pe.wait_ge(w_scaled, 1)
            nc.tensor.transpose(MAIN[1][0:NH, 0:P], w_raw[:, 1536:1544], ident[:]).then_inc(wdtT_psum, 1)
            pe.wait_ge(wdtT_set, 1)
            pe.wait_ge(wdt_in, 16)
            mm(MAIN[2][:, 0:DI], wdtT[:], w_dt[:], start=True, stop=True).then_inc(wdt_psum, 1)

            def split(dst, stat_h, stat_l, mov_h, mov_l):
                mm(dst, stat_h, mov_l, start=True, stop=False)
                mm(dst, stat_l, mov_h, start=False, stop=False)
                return mm(dst, stat_h, mov_h, start=False, stop=True)

            def hn_transposes(s):
                if (v := nth(s, 4, 0)) is not None:
                    pe.wait_ge(yT_ready, v)
                if is_seq(s, 0):
                    pe.wait_ge(tables_set, 4)
                for c in range(NCH):
                    pe.wait_ge(hn_ready, nth(s, 4, c + 1))
                    ins = nc.tensor.transpose(TR[:, at(c)], hn[:, c, :], ident[:])
                ins.then_inc(hnT_psum, 1)

            def proj(s, j):
                dst = MAIN[j % 4]
                pe.wait_ge(hTl_ready, nth(s, 1, 1))
                if is_seq(s, 0) and j == 0:
                    pe.wait_ge(weights_set, 1)
                if j == 0 and (v := nth(s, 4, 0)) is not None:
                    pe.wait_ge(yz_ready, v)
                if j == 1 and (v := nth(s, 8, 0)) is not None:
                    pe.wait_ge(decay_ready, v)
                if j == 2 and (v := nth(s, 4, 0)) is not None:
                    pe.wait_ge(x1_ready, v)
                if j in (4, 5):
                    pe.wait_ge(xpad_ready, nth(s, 2, j - 3))
                if j in (6, 7, 8, 9):
                    pe.wait_ge(dtv_ready, nth(s, 4, j - 5))
                if j < 2:
                    ins = split(dst[:], wh[:, X0 + j * P:X0 + (j + 1) * P], wl[:, X0 + j * P:X0 + (j + 1) * P], hTh[:], hTl[:])
                elif j < 6:
                    c = j - 2
                    ins = split(dst[:], hTh[:, at(c)], hTl[:, at(c)], wh[:, 0:512], wl[:, 0:512])
                else:
                    k = B0 + (j - 6) * P
                    ins = split(dst[:], wh[:, k:k + P], wl[:, k:k + P], hTh[:], hTl[:])
                ins.then_inc(proj_psum, 1)

            def proj_c(s, b):
                dst = MAIN[(3, 1, 2, 3)[b]]
                if b == 0:
                    pe.wait_ge(b_ready, nth(s, 4, 2))
                if b == 1:
                    pe.wait_ge(b_ready, nth(s, 4, 4))
                if b == 2:
                    pe.wait_ge(xs_ready, nth(s, 2, 1))
                if b == 3:
                    pe.wait_ge(c_ready, nth(s, 4, 1))
                k = C0 + b * P
                split(dst[:], wh[:, k:k + P], wl[:, k:k + P], hTh[:], hTl[:]).then_inc(proj_psum, 1)

            def x_tokens(s, i):
                if i == 0:
                    pe.wait_ge(b_ready, nth(s, 4, 1))
                    pe.wait_ge(conv_step, nth(s, 8, 8))
                else:
                    pe.wait_ge(b_ready, nth(s, 4, 3))
                for j in range(2):
                    for b in range(NB):
                        ins = nc.tensor.transpose(MAIN[2 * (1 - i)][:, at(2 * j + b)], cv[:, b, at(2 * i + j)], ident[:])
                ins.then_inc(xtok_psum, 1)

            def lcs(s, prev, older):
                if prev is not None:
                    pe.wait_ge(gT_ready, nth(prev, 1, 1))
                pe.wait_ge(dt_steps, nth(s, 3, 3))
                mm(TR[:, 0:32], upto[:], dta[:], start=True, stop=True)
                mm(TR[:, 32:64], ones[:], dta[:], start=True, stop=True).then_inc(lcs_psum, 1)

            def l_transposes(s):
                pe.wait_ge(ecs_ready, nth(s, 3, 3))
                pe.wait_ge(lpart_steps, nth(s, 5, 5))
                for c in range(NCH):
                    ins = nc.tensor.transpose(TR_BF[0:3 * NH, at(c)], lparts[:, c, :, :].rearrange("p a h -> p (a h)"), ident_bf[:])
                ins.then_inc(lT_psum, 1)

            def segments(s, c):
                for hf in range(2):
                    dst = MAIN[hf]
                    if c == 0 and hf == 0:
                        pe.wait_ge(lT_ready, nth(s, 1, 1))
                        pe.wait_ge(xs_ready, nth(s, 2, 2))
                        pe.wait_ge(c_ready, nth(s, 4, 2))
                    if c > 0 and hf == 0:
                        pe.wait_ge(yz_ready, nth(s, 4, c))
                    if c > 0 and hf == 1:
                        pe.wait_ge(state_step, nth(s, 8, (2, 5, 8)[c - 1]))
                    mm(dst[:], ident_bf[:], mask[:].rearrange("p n l -> p (n l)"), start=True, stop=False)
                    for n in range(NP):
                        mm(dst[:, at(n)], pick_head[:, 2 * n + hf, :], lT[:, at(c)], start=False, stop=False)
                    mm(dst[:], lT[:, at(c)], minus_head[:].rearrange("r (n t) l -> r t n l", t=2)[:, hf, :, :],
                       start=False, stop=True).then_inc(seg_psum, 1)

            def b_tokens(s, c):
                if c == 0:
                    pe.wait_ge(lT_ready, nth(s, 1, 1))
                    pe.wait_ge(b_ready, nth(s, 4, 4))
                else:
                    pe.wait_ge(yT_ready, nth(s, 4, c))
                for n in range(NP):
                    ins = nc.tensor.transpose(TR[:, at(n)], BT[:, n, at(c)], ident[:])
                ins.then_inc(btok_psum, 1)

            def gram(s, c, prev):
                if c == 0:
                    pe.wait_ge(c_ready, nth(s, 4, 4))
                    if prev is not None:
                        pe.wait_ge(wbc_ready, nth(prev, 4, 4))
                else:
                    pe.wait_ge(mg_ready, nth(s, 8, 2 * c))
                for n in range(NP):
                    for hf in range(2):
                        q = slice(NS * hf, NS * hf + NS)
                        ins = mm(MAIN[2 + hf][:, at(n)], BT[q, n, at(c)], CT[q, n, at(c)], start=True, stop=True)
                        if n == NP - 1:
                            ins.then_inc(g_psum, 1)

            def y_product(s, c):
                pe.wait_ge(decay_ready, nth(s, 8, 2 * c + 2))
                if c > 0:
                    pe.wait_ge(state_step, nth(s, 8, (2, 5, 8)[c - 1]))
                    for n in range(NP):
                        mm(MAIN[0][:, 256 + n * 64:320 + n * 64], CT[:, n, at(c)], state[:, n, :], start=True, stop=True)
                if c < NCH - 1:
                    pe.wait_ge(btok_ready, nth(s, 3, c + 1))
                    pe.wait_ge(xw_ready, nth(s, 6, 2 * c + 2))
                    for n in range(NP):
                        ins = mm(MAIN[1][:, n * 64:(n + 1) * 64], btok[:, at(n)], xw[:, n, :, :].rearrange("p t d -> p (t d)"),
                                 start=True, stop=True)
                    ins.then_inc(s_psum, 1)
                pe.wait_ge(mg_ready, nth(s, 8, 2 * c + 2))
                for hf in range(2):
                    for n in range(NP):
                        h = 2 * n + hf
                        ins = mm(MAIN[0][:, h * HD:(h + 1) * HD], mg[:, hf, n, :], xs[:, c, h * HD:(h + 1) * HD],
                                 start=True, stop=True)
                ins.then_inc(y_psum, 1)

            def y_transposes(s, c):
                if c < NCH - 1:
                    pe.wait_ge(btok_ready, nth(s, 3, c + 1))
                else:
                    pe.wait_ge(yT_ready, nth(s, 4, c))
                pe.wait_ge(yz_ready, nth(s, 4, c + 1))
                for b in range(NB):
                    ins = nc.tensor.transpose(TR[:, at(b)], yz[:, at(b)], ident[:])
                ins.then_inc(yT_psum, 1)

            def out_projection(s):
                pe.wait_ge(mg_ready, nth(s, 8, 8))
                pe.wait_ge(yT_ready, nth(s, 4, 4))
                for c in range(NCH):
                    for b in range(NB):
                        ins = mm(MAIN[2][:, at(c)], yT[:, b, at(c)], w_out[:, b, :], start=(b == 0), stop=(b == NB - 1))
                ins.then_inc(o_psum, 1)

            def f_transposes(s, prev):
                if s is not None:
                    pe.wait_ge(hTl_ready, nth(s, 1, 1))
                else:
                    pe.wait_ge(yT_ready, nth(prev, 4, 4))
                for c in range(NCH):
                    pe.wait_ge(fn_ready, nth(prev, 4, c + 1))
                    ins = nc.tensor.transpose(TR[:, at(c)], fn[:, c, :], ident[:])
                ins.then_inc(fT_psum, 1)

            def gate(prev):
                pe.wait_ge(fTl_ready, nth(prev, 1, 1))
                for c in range(NCH):
                    ins = split(TR[:, c * NE:(c + 1) * NE], fTh[:, at(c)], fTl[:, at(c)], gwh[:], gwl[:])
                ins.then_inc(gate_psum, 1)

            def g_transposes(prev, older):
                if older is not None:
                    pe.wait_ge(out_ready, nth(older, 1, 1))
                pe.wait_ge(gate_steps, nth(prev, 13, 13))
                for c in range(NCH):
                    ins = nc.tensor.transpose(TR_BF[0:3 * NE, at(c)], gparts[:, c, :, :].rearrange("p a h -> p (a h)"), ident_bf[:])
                ins.then_inc(gT_psum, 1)

            def weight_rows(s, prev, e):
                if e == 0:
                    pe.wait_ge(gT_ready, nth(prev, 1, 1))
                if e < 2 and s is not None:
                    pe.wait_ge(c_ready, nth(s, 4, e + 3))
                if e >= 2:
                    pe.wait_ge(wbc_ready, nth(prev, 4, e - 1))
                mm(MAIN[2 + e % 2][:], pick_expert[:, e, :], gT[:], start=True, stop=True).then_inc(wbc_psum, 1)

            def first(prev, b):
                if is_seq(prev, 0) and b == 0:
                    pe.wait_ge(fh_set, 4)
                g, k = divmod(b, NF)
                if (v := nth(prev, NBLK, b - 1)) is not None:
                    pe.wait_ge(act_ready, v)
                if b == 0:
                    pe.wait_ge(fTl_ready, nth(prev, 1, 1))
                split(HID[b % 2][:], w1h[:, g, at(k)], w1l[:, g, at(k)], fTh[:], fTl[:]).then_inc(hid_psum, 1)

            def second(prev, b):
                g, k = divmod(b, NF)
                begins = b in (0, 8, 12, 16, 20)
                ends = b in (7, 11, 15, 19, 23)
                if b == 0:
                    if (v := nth(prev, 4, 0)) is not None:
                        pe.wait_ge(term_ready, v)
                if b == 8:
                    pe.wait_ge(shared_ready, nth(prev, 1, 1))
                if b in (12, 16, 20):
                    pe.wait_ge(term_ready, nth(prev, 4, b // 4 - 2))
                r = b % RING
                pe.wait_ge(act_l_ready, nth(prev, NBLK, b + 1))
                mm(FOUT[:], w2h[:, g, k, :], act_l[:, r, :], start=begins, stop=False)
                mm(FOUT[:], w2l[:, g, k, :], act_h[:, r, :], start=False, stop=False)
                mm(FOUT[:], w2h[:, g, k, :], act_h[:, r, :], start=False, stop=ends).then_inc(second_done, 1)

            def out_transposes(prev, older):
                if prev is not None:
                    pe.wait_ge(gate_logits, nth(prev, 3, 1))
                else:
                    pe.wait_ge(gT_ready, nth(older, 1, 1))
                pe.wait_ge(acc_ready, nth(older, 4, 4))
                for c in range(NCH):
                    ins = nc.tensor.transpose(TR[:, at(c)], acc[:, at(c)], ident[:])
                ins.then_inc(outT_psum, 1)

            def scan_part(s, prev, older, i):
                if i == 0:
                    hn_transposes(s)
                if i == 1:
                    proj(s, 0)
                    proj(s, 1)
                if i == 2:
                    proj(s, 2)
                    proj(s, 3)
                if i == 3:
                    proj(s, 4)
                if i == 4:
                    proj(s, 5)
                if i in (4, 5):
                    proj(s, 2 * i - 2)
                    proj(s, 2 * i - 1)
                if i in (6, 7):
                    x_tokens(s, i - 6)
                if i in (6, 7, 8, 9):
                    proj_c(s, i - 6)
                if i == 10:
                    lcs(s, prev, older)
                if i == 11:
                    l_transposes(s)
                if i >= CHUNKS_FROM:
                    c, step = divmod(i - CHUNKS_FROM, 3)
                    if step == 0:
                        if c > 0:
                            y_transposes(s, c - 1)
                        segments(s, c)
                        if c < NCH - 1:
                            b_tokens(s, c)
                    if step == 1:
                        gram(s, c, prev)
                    if step == 2:
                        y_product(s, c)

            def body(s, prev, older):
                for i in range(NBLK):
                    if prev is not None and i == 5:
                        gate(prev)
                    if s is not None:
                        scan_part(s, prev, older, i)
                    if prev is not None:
                        if i == 4:
                            f_transposes(s, prev)
                        if i == 9:
                            g_transposes(prev, older)
                        if i in (10, 11):
                            weight_rows(s, prev, 2 * i - 20)
                            weight_rows(s, prev, 2 * i - 19)
                    if older is not None and i == 7:
                        out_transposes(prev, older)
                    if new := block_at(i, prev, older):
                        first(*new)
                    if old := block_at(i - LAG, prev, older):
                        second(*old)
                if prev is not None:
                    second(prev, NBLK - LATE - 2)
                if s is not None:
                    y_transposes(s, NCH - 1)
                    out_projection(s)
                if prev is not None:
                    second(prev, NBLK - LATE - 1)

            bodies(pe, body)

        @block.scalar
        def _(act):
            nc.scalar.preload_act_table_set("natural_log_exp_and_others")
            act.wait_ge(small_in, 7 * 16)
            nc.scalar.activation(a_exp[:], a_log[:], ACT.Exp).then_inc(a_set, 1)
            act.wait_ge(cols_psum, 1)
            nc.scalar.copy(cols[:], MAIN[0][:, 0:35]).then_inc(cols_set, 1)
            act.wait_ge(wdtT_psum, 1)
            nc.scalar.copy(wdtT[:], MAIN[1][0:NH, 0:P]).then_inc(wdtT_set, 1)
            act.wait_ge(cols_set, 1)
            nc.scalar.activation(b2sh[:], b2s[:, 0:1], ACT.Identity, bias=b2s[:, 1:2]).then_inc(b2_set, 1)
            act.wait_ge(b2_set, 1)
            nc.scalar.mul(b2sum[:], b2sh[:], 0.5).then_inc(b2_set, 1)
            act.wait_ge(b2_set, 2)

            def hT(s):
                act.wait_ge(hnT_psum, nth(s, 1, 1))
                nc.scalar.copy(hTh[:], TR[:]).then_inc(hTh_ready, 1)

            def x_copy(s, b):
                act.wait_ge(proj_psum, nth(s, 14, b + 1))
                nc.scalar.copy(xpad[:, b, TAPS - 1:], MAIN[b][:]).then_inc(xpad_ready, 1)

            def fT(prev):
                act.wait_ge(fT_psum, nth(prev, 1, 1))
                nc.scalar.copy(fTh[:], TR[:]).then_inc(fTh_ready, 1)

            def silu_z(s, c):
                act.wait_ge(proj_psum, nth(s, 14, c + 3))
                nc.scalar.activation(sz[:, c, :], MAIN[(c + 2) % 4][:, 0:DI], ACT.Silu).then_inc(sz_ready, 1)

            def b_copy(s, b):
                act.wait_ge(proj_psum, nth(s, 14, b + 7))
                nc.scalar.copy(BT[:, b, :], MAIN[(b + 2) % 4][:]).then_inc(b_ready, 1)

            def silu_x(s, i):
                act.wait_ge(xtok_psum, nth(s, 2, i + 1))
                nc.scalar.activation(xs[:, 2 * i:2 * i + 2, :].rearrange("p c d -> p (c d)"), MAIN[2 * (1 - i)][:], ACT.Silu)\
                    .then_inc(xs_ready, 1)

            def softplus(s):
                act.wait_ge(dt_clamped, nth(s, 1, 1))
                nc.scalar.activation(sp[:], sp[:], ACT.Exp).then_inc(dt_exp, 1)
                act.wait_ge(dt_exp, nth(s, 1, 1))
                nc.scalar.activation(sp[:], sp[:], ACT.Ln, bias=1.0).then_inc(dt_log, 1)

            def gate_exps(prev):
                act.wait_ge(gate_logits, nth(prev, 3, 3))
                nc.scalar.activation(gexp[:], lg[:], ACT.Exp).then_inc(gate_exp, 1)

            def chunk_decays(s):
                act.wait_ge(lcs_psum, nth(s, 1, 1))
                nc.scalar.activation(ecs[:].rearrange("p c h -> p (c h)"), TR[:, 0:32], ACT.Exp).then_inc(ecs_ready, 1)
                tot = TR[:, 32:64].rearrange("p (c n t) -> p c n t", n=NP, t=2)
                for t in range(2):
                    q = slice(64 * t, 64 * t + 64)
                    nc.scalar.activation(tdx[q, :, :], tot[q, :, :, t], ACT.Exp).then_inc(ecs_ready, 1)

            def weight_copy(prev, e):
                act.wait_ge(wbc_psum, nth(prev, 4, e + 1))
                nc.scalar.copy(wbc[:, e, :], MAIN[2 + e % 2][:]).then_inc(wbc_ready, 1)

            def relu(prev, b):
                act.wait_ge(hid_psum, nth(prev, NBLK, b + 1))
                if (v := nth(prev, NBLK, b + 1 - RING)) is not None:
                    act.wait_ge(second_done, v)
                nc.scalar.activation(act_h[:, b % RING, :], HID[b % 2][:], ACT.Relu, bias=b1[:, b:b + 1])\
                    .then_inc(act_h_ready, 1)
                nc.scalar.activation(act_f[:, b % RING, :], HID[b % 2][:], ACT.Relu, bias=b1[:, b:b + 1])\
                    .then_inc(act_ready, 1)

            def keep_x1(prev, older):
                if older is not None:
                    act.wait_ge(out_ready, nth(older, 1, 1))
                act.wait_ge(x1_ready, nth(prev, 4, 4))
                nc.scalar.copy(x1_kept[:], x1).then_inc(x1_kept_ready, 1)

            def shared_out(prev):
                act.wait_ge(second_done, nth(prev, NBLK, 8))
                if (v := nth(prev, 1, 0)) is not None:
                    act.wait_ge(outT_psum, v)
                nc.scalar.activation(acc, FOUT[:], ACT.Identity, bias=b2sum[:], scale=0.5).then_inc(shared_ready, 1)

            def decays(s, c):
                for hf in range(2):
                    act.wait_ge(seg_psum, nth(s, 8, 2 * c + hf + 1))
                    if hf == 0 and (v := nth(s, 8, 2 * c)) is not None:
                        act.wait_ge(mg_ready, v)
                    if c > 0 and hf == 0:
                        act.wait_ge(xw_ready, nth(s, 6, 2 * c))
                    nc.scalar.activation(decay[:, hf, :, :].rearrange("p n l -> p (n l)"), MAIN[hf][:], ACT.Exp)\
                        .then_inc(decay_ready, 1)
                if c < NCH - 1:
                    act.wait_ge(btok_psum, nth(s, 3, c + 1))
                    nc.scalar.copy(btok[:], TR[:]).then_inc(btok_ready, 1)

            def y_out(s, c):
                act.wait_ge(yz_ready, nth(s, 4, c + 1))
                nc.scalar.activation(junk[:], yz[:], ACT.Square, accum_out=ssq[:, c:c + 1]).then_inc(ssq_ready, 1)
                act.wait_ge(yT_psum, nth(s, 4, c + 1))
                nc.scalar.copy(yT[:, :, at(c)], TR[:, 0:DI].rearrange("p (b t) -> p b t", t=P)).then_inc(yT_ready, 1)

            def scan_part(s, i):
                if i == 0:
                    hT(s)
                if i == 1:
                    x_copy(s, 0)
                    x_copy(s, 1)
                if i == 2:
                    nc.scalar.preload_act_table_set("silu_and_others")
                    silu_z(s, 0)
                    silu_z(s, 1)
                if i in (3, 4):
                    silu_z(s, i - 1)
                if i in (4, 5):
                    b_copy(s, 2 * i - 8)
                    b_copy(s, 2 * i - 7)
                if i in (6, 7):
                    silu_x(s, i - 6)
                if i == 7:
                    nc.scalar.preload_act_table_set("natural_log_exp_and_others")
                    softplus(s)
                if i == 10:
                    chunk_decays(s)
                if i >= CHUNKS_FROM:
                    c, step = divmod(i - CHUNKS_FROM, 3)
                    if step == 0:
                        if c > 0:
                            y_out(s, c - 1)
                        decays(s, c)

            def body(s, prev, older):
                for i in range(NBLK):
                    if s is not None:
                        scan_part(s, i)
                    if prev is not None:
                        if i == 4:
                            fT(prev)
                        if i == 7:
                            gate_exps(prev)
                        if i == 9:
                            keep_x1(prev, older)
                        if i in (10, 11):
                            weight_copy(prev, 2 * i - 20)
                            weight_copy(prev, 2 * i - 19)
                    if new := block_at(i, prev, older):
                        relu(*new)
                    if prev is not None and i == 7 + LATE + LAG:
                        shared_out(prev)
                if s is not None:
                    y_out(s, NCH - 1)

            bodies(act, body)

        @block.vector
        def _(dve):
            v_ = nc.vector

            dve.wait_ge(cols_set, 1)
            dve.wait_ge(win_in, 16)
            v_.tensor_scalar(w_raw, w_raw, wn_in, None, ALU.mult).then_inc(w_scaled, 1)
            dve.wait_ge(w_scaled, 1)
            v_.tensor_copy(w_all[:, 0:256], w_raw[:, 0:256]).then_inc(wdt_set, 1)
            v_.tensor_copy(w_all[:, X0:], w_raw[:, 256:1536]).then_inc(wdt_set, 1)
            dve.wait_ge(wdt_psum, 1)
            v_.tensor_copy(w_all[:, DT0:DT0 + DI], MAIN[2][:, 0:DI]).then_inc(wdt_set, 1)
            dve.wait_ge(wdt_set, 3)
            v_.tensor_copy(wh[:], w_all).then_inc(wh_set, 1)
            dve.wait_ge(wh_set, 1)
            v_.tensor_tensor(wl[:], w_all, f(wh[:]), ALU.subtract).then_inc(weights_set, 1)
            dve.wait_ge(a_set, 1)
            v_.tensor_scalar(a_neg[:], a_exp[:], -1.0 / HD, None, ALU.mult).then_inc(a_set, 1)
            v_.tensor_copy(gwh[:], gw[:]).then_inc(a_set, 1)
            dve.wait_ge(a_set, 3)
            v_.tensor_tensor(gwl[:], gw[:], f(gwh[:]), ALU.subtract).then_inc(a_set, 1)
            for b in range(NB):
                v_.tensor_scalar(w_out[:, b, :], w_out_raw[:, b, :], wn_out[:, b:b + 1], None, ALU.mult).then_inc(a_set, 1)
            dve.wait_ge(a_set, 6)

            def split_ffn():
                dve.wait_ge(wf_in, 4 * 16)
                v_.tensor_copy(w1h[:], wf_raw[:, 0]).then_inc(fh_set, 1)
                v_.tensor_copy(w2h[:].rearrange("p n b o -> p (n b o)"), wf_raw[:, 1].rearrange("p n f -> p (n f)")).then_inc(fh_set, 1)
                dve.wait_ge(fh_set, 2)
                v_.tensor_tensor(w1l[:], wf_raw[:, 0], f(w1h[:]), ALU.subtract).then_inc(fh_set, 1)
                v_.tensor_tensor(w2l[:].rearrange("p n b o -> p (n b o)"), wf_raw[:, 1].rearrange("p n f -> p (n f)"),
                                 f(w2h[:].rearrange("p n b o -> p (n b o)")), ALU.subtract).then_inc(fh_set, 1)

            def norm1(s):
                dve.wait_ge(x_loaded, nth(s, 16, 16))
                for c in range(NCH):
                    v_.bn_stats(st1[:, c, :], x_in[:, c, :]).then_inc(ln1_stats, 1)
                dve.wait_ge(ln1_stats, nth(s, 4, 4))
                v_.memset(carrier[:, RING:RING + 1], 0.0)
                for c in range(NCH):
                    v_.bn_aggr(mv1[:, c, :], st1[:, c, :]).then_inc(ln1_mv, 1)
                dve.wait_ge(ln1_mv, nth(s, 4, 4))
                v_.tensor_scalar(v1[:, 0, :], mv1[:, :, 1], LN_EPS, None, ALU.add).then_inc(ln1_v, 1)
                v_.tensor_scalar(v1[:, 1, :], mv1[:, :, 1], 1.0 + RMS_EPS, LN_EPS * RMS_EPS, ALU.mult, ALU.add).then_inc(ln1_v, 1)

            def norm1_apply(s):
                dve.wait_ge(ln1_rs, nth(s, 1, 1))
                if (v := nth(s, 1, 0)) is not None:
                    dve.wait_ge(hnT_psum, v)
                for c in range(NCH):
                    v_.tensor_scalar(hn[:, c, :], x_in[:, c, :], mv1[:, c, 0:1], rs1[:, 1, c:c + 1], ALU.subtract, ALU.mult)\
                        .then_inc(hn_ready, 1)

            def residual(s):
                v_.tensor_scalar(one_rs[:], rs1[:, 0, :], 1.0, None, ALU.add).then_inc(xr_scales, 1)
                v_.tensor_tensor(mean_rs[:], mv1[:, :, 0], rs1[:, 0, :], ALU.mult).then_inc(xr_scales, 1)
                dve.wait_ge(xr_scales, nth(s, 2, 2))
                for c in range(NCH):
                    v_.tensor_scalar(xr[:, c, :], x_in[:, c, :], one_rs[:, c:c + 1], mean_rs[:, c:c + 1], ALU.mult, ALU.subtract)\
                        .then_inc(xr_ready, 1)

            def hT_low(s):
                dve.wait_ge(hTh_ready, nth(s, 1, 1))
                v_.tensor_tensor(hTl[:], TR[:], f(hTh[:]), ALU.subtract).then_inc(hTl_ready, 1)

            def conv(s, b):
                dve.wait_ge(xpad_ready, nth(s, 2, b + 1))
                v_.tensor_scalar(cv[:, b, :], xpad[:, b, 0:SEQ], conv_w[:, b, 0:1], conv_b[:, b:b + 1], ALU.mult, ALU.add)\
                    .then_inc(conv_step, 1)
                for k in range(1, TAPS):
                    dve.wait_ge(conv_step, nth(s, 8, 4 * b + k))
                    v_.scalar_tensor_tensor(cv[:, b, :], xpad[:, b, k:k + SEQ], conv_w[:, b, k:k + 1], cv[:, b, :],
                                            ALU.mult, ALU.add).then_inc(conv_step, 1)

            def dt_add(s, c):
                dve.wait_ge(sz_ready, nth(s, 4, c + 1))
                v_.tensor_tensor(dtv[:, c, :], MAIN[(c + 2) % 4][:, DI:2 * DI], b_dt[:], ALU.add).then_inc(dtv_ready, 1)

            def dt_clamp(s):
                dve.wait_ge(dtv_ready, nth(s, 4, 4))
                v_.tensor_scalar(sp[:], dtv[:], CLAMP, None, ALU.min).then_inc(dt_clamped, 1)

            def dt_decay(s):
                dve.wait_ge(dt_log, nth(s, 1, 1))
                v_.tensor_tensor(dtv[:], dtv[:], sp[:], ALU.max).then_inc(dt_steps, 1)
                dve.wait_ge(dt_steps, nth(s, 3, 1))
                v_.tensor_reduce(dsum[:], dtv[:].rearrange("p c (h d) -> p (c h) d", d=HD), AX_X, ALU.add).then_inc(dt_steps, 1)
                dve.wait_ge(dt_steps, nth(s, 3, 2))
                v_.tensor_tensor(dta[:].rearrange("p (c h) -> p c h", h=NH), dsum[:].rearrange("p (c h) -> p c h", h=NH),
                                 a_neg[:].unsqueeze(1).to_broadcast([P, NCH, NH]), ALU.mult).then_inc(dt_steps, 1)

            def three_parts(src, parts, r1, r2, steps, s, per, first):
                v_.tensor_copy(parts[:, :, 0, :], src).then_inc(steps, 1)
                dve.wait_ge(steps, nth(s, per, first + 1))
                v_.tensor_tensor(r1[:], src, parts[:, :, 0, :], ALU.subtract).then_inc(steps, 1)
                dve.wait_ge(steps, nth(s, per, first + 2))
                v_.tensor_copy(parts[:, :, 1, :], r1[:]).then_inc(steps, 1)
                dve.wait_ge(steps, nth(s, per, first + 3))
                v_.tensor_tensor(r2[:], r1[:], parts[:, :, 1, :], ALU.subtract).then_inc(steps, 1)
                dve.wait_ge(steps, nth(s, per, first + 4))
                v_.tensor_copy(parts[:, :, 2, :], r2[:]).then_inc(steps, 1)

            def l_parts(s):
                dve.wait_ge(ecs_ready, nth(s, 3, 3))
                three_parts(TR[:, 0:32].rearrange("p (c h) -> p c h", h=NH), lparts, rem1, rem2, lpart_steps, s, 5, 0)

            def lT_copy(s):
                dve.wait_ge(lT_psum, nth(s, 1, 1))
                v_.tensor_copy(lT[:], TR_BF[0:3 * NH, :]).then_inc(lT_ready, 1)

            def c_copy(s, b):
                dve.wait_ge(proj_psum, nth(s, 14, b + 11))
                v_.tensor_copy(CT[:, b, :], MAIN[(3, 1, 2, 3)[b]][:]).then_inc(c_ready, 1)

            def attend(s, c, step):
                if step == 1:
                    for hf in range(2):
                        dve.wait_ge(g_psum, nth(s, 8, 2 * c + hf + 1))
                        dve.wait_ge(decay_ready, nth(s, 8, 2 * c + hf + 1))
                        if hf == 0 and (v := nth(s, 4, c)) is not None:
                            dve.wait_ge(y_psum, v)
                        v_.tensor_tensor(mg[:, hf, :, :].rearrange("p n l -> p (n l)"), MAIN[2 + hf][:],
                                         decay[:, hf, :, :].rearrange("p n l -> p (n l)"), ALU.mult).then_inc(mg_ready, 1)
                if step == 2:
                    if c < NCH - 1:
                        first = (0, 2, 5)[c]
                        if c > 0:
                            v_.tensor_tensor(state_m[:], state[:], tdx[:, c, :].unsqueeze(2).to_broadcast([P, NP, 2 * HD]),
                                             ALU.mult).then_inc(state_step, 1)
                            dve.wait_ge(state_step, nth(s, 8, first + 1))
                            first += 1
                        dve.wait_ge(s_psum, nth(s, 3, c + 1))
                        if (v := nth(s, 4, c + 1 if c > 0 else 0)) is not None:
                            dve.wait_ge(y_psum, v)
                        own = MAIN[1][:, 0:256].rearrange("p (n d) -> p n d", n=NP)
                        for t in range(2):
                            q, d = slice(64 * t, 64 * t + 64), slice(HD * t, HD * t + HD)
                            if c == 0:
                                v_.tensor_copy(state[q, :, d], own[q, :, d]).then_inc(state_step, 1)
                            else:
                                v_.tensor_tensor(state[q, :, d], own[q, :, d], state_m[q, :, d], ALU.add).then_inc(state_step, 1)
                        dve.wait_ge(state_step, nth(s, 8, first + 2))
                    dve.wait_ge(y_psum, nth(s, 4, c + 1))
                    dve.wait_ge(xd_ready, nth(s, 4, c + 1))
                    if c == 0:
                        v_.tensor_tensor(yt[:], MAIN[0][:, 0:DI], xd[:], ALU.add).then_inc(y_steps, 1)
                        dve.wait_ge(y_steps, nth(s, 10, 1))
                    else:
                        first = 3 * c - 2
                        v_.tensor_tensor(yt[:].rearrange("p (h d) -> p h d", h=NH),
                                         MAIN[0][:, DI:2 * DI].rearrange("p (h d) -> p h d", h=NH),
                                         ecs[:, c, :].unsqueeze(2).to_broadcast([P, NH, HD]), ALU.mult).then_inc(y_steps, 1)
                        dve.wait_ge(y_steps, nth(s, 10, first + 1))
                        v_.tensor_tensor(yt[:], MAIN[0][:, 0:DI], yt[:], ALU.add).then_inc(y_steps, 1)
                        dve.wait_ge(y_steps, nth(s, 10, first + 2))
                        v_.tensor_tensor(yt[:], yt[:], xd[:], ALU.add).then_inc(y_steps, 1)
                        dve.wait_ge(y_steps, nth(s, 10, first + 3))
                    if (v := nth(s, 4, c)) is not None:
                        dve.wait_ge(ssq_ready, v)
                        dve.wait_ge(yT_psum, v)
                    v_.tensor_tensor(yz[:], yt[:], sz[:, c, :], ALU.mult).then_inc(yz_ready, 1)

            def mean_square(s):
                dve.wait_ge(ssq_ready, nth(s, 4, 4))
                v_.tensor_scalar(msq[:], ssq[:], 1.0 / DI, RMS_EPS, ALU.mult, ALU.add).then_inc(msq_ready, 1)

            def add_residual(prev):
                dve.wait_ge(o_psum, nth(prev, 1, 1))
                dve.wait_ge(rstd_ready, nth(prev, 1, 1))
                if (v := nth(prev, 1, 0)) is not None:
                    dve.wait_ge(x1_kept_ready, v)
                for c in range(NCH):
                    v_.scalar_tensor_tensor(x1[:, c, :], MAIN[2][:, at(c)], rstd[:, c:c + 1], xr[:, c, :], ALU.mult, ALU.add)\
                        .then_inc(x1_ready, 1)

            def norm2(prev):
                dve.wait_ge(x1_ready, nth(prev, 4, 4))
                for c in range(NCH):
                    v_.bn_stats(st2[:, c, :], x1[:, c, :]).then_inc(ln2_stats, 1)
                dve.wait_ge(ln2_stats, nth(prev, 4, 4))
                v_.memset(carrier[:, RING:RING + 1], 0.0)
                for c in range(NCH):
                    v_.bn_aggr(mv2[:, c, :], st2[:, c, :]).then_inc(ln2_mv, 1)
                dve.wait_ge(ln2_mv, nth(prev, 4, 4))
                v_.tensor_scalar(v2[:], mv2[:, :, 1], LN_EPS, None, ALU.add).then_inc(ln2_v, 1)

            def norm2_apply(prev):
                dve.wait_ge(ln2_rs, nth(prev, 1, 1))
                for c in range(NCH):
                    v_.tensor_scalar(fn[:, c, :], x1[:, c, :], mv2[:, c, 0:1], rs2[:, c:c + 1], ALU.subtract, ALU.mult)\
                        .then_inc(fn_ready, 1)

            def fT_low(prev):
                dve.wait_ge(fTh_ready, nth(prev, 1, 1))
                v_.tensor_tensor(fTl[:], TR[:], f(fTh[:]), ALU.subtract).then_inc(fTl_ready, 1)

            def logits(prev):
                dve.wait_ge(gate_psum, nth(prev, 1, 1))
                v_.tensor_tensor(lg[:], TR[:, 0:NCH * NE].rearrange("p (c e) -> p c e", e=NE),
                                 gb[:].unsqueeze(1).to_broadcast([P, NCH, NE]), ALU.add).then_inc(gate_logits, 1)
                dve.wait_ge(gate_logits, nth(prev, 3, 1))
                v_.tensor_reduce(gmax[:], lg[:], AX_X, ALU.max).then_inc(gate_logits, 1)
                dve.wait_ge(gate_logits, nth(prev, 3, 2))
                v_.tensor_tensor(lg[:], lg[:], gmax[:].unsqueeze(2).to_broadcast([P, NCH, NE]), ALU.subtract).then_inc(gate_logits, 1)

            def top_two(prev):
                def step(k):
                    dve.wait_ge(gate_steps, nth(prev, 13, k))
                dve.wait_ge(gate_exp, nth(prev, 1, 1))
                v_.tensor_reduce(gsum[:], gexp[:], AX_X, ALU.add).then_inc(gate_steps, 1)
                step(1)
                v_.reciprocal(gsum[:], gsum[:]).then_inc(gate_steps, 1)
                step(2)
                v_.tensor_tensor(gw_n[:], gexp[:], gsum[:].unsqueeze(2).to_broadcast([P, NCH, NE]), ALU.mult).then_inc(gate_steps, 1)
                step(3)
                mine = gw_n[:].unsqueeze(3).to_broadcast([P, NCH, NE, NE])
                other = gw_n[:].unsqueeze(2).to_broadcast([P, NCH, NE, NE])
                v_.tensor_tensor(above[:], mine, other, ALU.is_lt).then_inc(gate_steps, 1)
                v_.tensor_tensor(level[:], mine, other, ALU.is_le).then_inc(gate_steps, 1)
                step(5)
                v_.tensor_tensor(level[:].rearrange("p c e j -> p c (e j)"), level[:].rearrange("p c e j -> p c (e j)"),
                                 lower[:].rearrange("p e j -> p (e j)").unsqueeze(1).to_broadcast([P, NCH, NE * NE]),
                                 ALU.mult).then_inc(gate_steps, 1)
                step(6)
                v_.tensor_tensor(above[:], above[:], level[:], ALU.max).then_inc(gate_steps, 1)
                step(7)
                v_.tensor_reduce(rank[:], above[:].rearrange("p c e j -> p (c e) j"), AX_X, ALU.add).then_inc(gate_steps, 1)
                step(8)
                v_.scalar_tensor_tensor(kept[:].rearrange("p c e -> p (c e)"), rank[:], 1.5, gw_n[:].rearrange("p c e -> p (c e)"),
                                        ALU.is_lt, ALU.mult).then_inc(gate_kept, 1)
                dve.wait_ge(gate_kept, nth(prev, 1, 1))
                three_parts(kept[:], gparts, grem1, grem2, gate_steps, prev, 13, 8)

            def gT_copy(prev):
                dve.wait_ge(gT_psum, nth(prev, 1, 1))
                v_.tensor_copy(gT[:], TR_BF[0:3 * NE, :]).then_inc(gT_ready, 1)

            def act_low(prev, b):
                r = b % RING
                dve.wait_ge(act_ready, nth(prev, NBLK, b + 1))
                v_.tensor_tensor(act_l[:, r, :], act_f[:, r, :], f(act_h[:, r, :]), ALU.subtract).then_inc(act_l_ready, 1)

            def routed_out(prev, e):
                dve.wait_ge(second_done, nth(prev, NBLK, 12 + 4 * e))
                dve.wait_ge(wbc_ready, nth(prev, 4, 4))
                if (v := nth(prev, 4, e)) is not None:
                    dve.wait_ge(acc_ready, v)
                v_.scalar_tensor_tensor(term, FOUT[:], b2r[:, e:e + 1], wbc[:, e, :], ALU.add, ALU.mult).then_inc(term_ready, 1)

            def store(prev):
                dve.wait_ge(x1_kept_ready, nth(prev, 1, 1))
                dve.wait_ge(outT_psum, nth(prev, 1, 1))
                if (v := nth(prev, 16, 0)) is not None:
                    dve.wait_ge(out_stored, v)
                v_.tensor_tensor(out_t.rearrange("p c d -> p (c d)"), TR[:], x1_kept[:].rearrange("p c d -> p (c d)"), ALU.add)\
                    .then_inc(out_ready, 1)



            def scan_part(s, i):
                last = is_seq(s, n_seq - 1)
                if i == 0:
                    hT_low(s)
                if i == 1:
                    residual(s)
                if i == 2:
                    dt_add(s, 0)
                    dt_add(s, 1)
                if i == 3:
                    conv(s, 0)
                    dt_add(s, 2)
                if i == 4:
                    dt_add(s, 3)
                    dt_clamp(s)
                if i == 5:
                    conv(s, 1)
                if i in (6, 7, 8, 9):
                    c_copy(s, i - 6)
                if i == 9:
                    dt_decay(s)
                if i == 10:
                    l_parts(s)
                if i == 11:
                    lT_copy(s)
                if i >= CHUNKS_FROM:
                    attend(s, *divmod(i - CHUNKS_FROM, 3))
                if i == 15 and not last:
                    norm1(s + 1)
                if i == 18 and not last:
                    norm1_apply(s + 1)

            def body(s, prev, older):
                if is_seq(s, 0):
                    norm1(s)
                    norm1_apply(s)
                for i in range(NBLK):
                    if prev is not None:
                        if i == 1:
                            norm2_apply(prev)
                        if i == 4:
                            fT_low(prev)
                        if i == 8:
                            top_two(prev)
                        if i == 9:
                            gT_copy(prev)
                    if s is not None:
                        scan_part(s, i)
                    if prev is not None:
                        if i == 0:
                            add_residual(prev)
                            norm2(prev)
                        if i == 5:
                            logits(prev)
                    if is_seq(s, 0) and i == 5:
                        split_ffn()
                    if older is not None and i == 7:
                        store(older)
                    if new := block_at(i, prev, older):
                        act_low(*new)
                    if older is not None and i == 3 + LAG:
                        routed_out(older, 3)
                    if prev is not None and i in (15 + LAG, 19 + LAG):
                        routed_out(prev, (i - 15 - LAG) // 4)
                if s is not None:
                    mean_square(s)
                if prev is not None:
                    routed_out(prev, 2)

            bodies(dve, body)

        @block.gpsimd
        def _(pool):
            g = nc.gpsimd
            for t, v in ((ident, 0.0), (ident_bf, 0.0), (ones, 1.0), (upto, 1.0), (mask, 0.0), (pick_head, 0.0),
                         (minus_head, 0.0), (pick_expert, 0.0), (lower, 1.0), (half, -0.5), (state, 0.0)):
                g.memset(t[:], v).then_inc(zeros_set, 1)
            g.memset(xpad[:, :, 0:TAPS - 1], 0.0).then_inc(zeros_set, 1)
            pool.wait_ge(zeros_set, 12)
            g.affine_select(out=ident[:], in_=ident[:], pattern=[[-1, P]], compare_op=ALU.not_equal, fill=1.0, base=0,
                            channel_multiplier=1).then_inc(tables_set, 1)
            g.affine_select(out=ident_bf[:], in_=ident_bf[:], pattern=[[-1, P]], compare_op=ALU.not_equal, fill=1.0, base=0,
                            channel_multiplier=1).then_inc(tables_set, 1)
            g.affine_select(out=upto[:], in_=upto[:], pattern=[[1, P]], compare_op=ALU.is_ge, fill=0.0, base=0,
                            channel_multiplier=-1).then_inc(tables_set, 1)
            g.affine_select(out=mask[:], in_=mask[:], pattern=[[0, NP], [1, P]], compare_op=ALU.is_ge, fill=MASKED, base=0,
                            channel_multiplier=-1).then_inc(tables_set, 1)
            g.affine_select(out=lower[:], in_=lower[:], pattern=[[1, NE], [-1, NE]], compare_op=ALU.is_gt, fill=0.0, base=0,
                            channel_multiplier=0).then_inc(tables_set, 1)
            k = 5
            for t, n, v in ((pick_head, NH, 1.0), (minus_head, NH, -1.0), (pick_expert, NE, 1.0)):
                for part in range(3):
                    g.affine_select(out=t[:], in_=t[:], pattern=[[-1, n], [0, P]], compare_op=ALU.not_equal, fill=v,
                                    base=-part * n, channel_multiplier=1).then_inc(tables_set, 1)
                    k += 1
                    pool.wait_ge(tables_set, k)

            def rsqrt1(s):
                pool.wait_ge(ln1_v, nth(s, 2, 2))
                g.tensor_tensor(rs1[:].rearrange("p a c -> p (a c)"), v1[:].rearrange("p a c -> p (a c)"), half[:], ALU.pow)\
                    .then_inc(ln1_rs, 1)

            def rsqrt2(prev):
                pool.wait_ge(ln2_v, nth(prev, 1, 1))
                g.tensor_tensor(rs2[:], v2[:], half[:, 0:NCH], ALU.pow).then_inc(ln2_rs, 1)

            def rsqrt_y(s):
                pool.wait_ge(msq_ready, nth(s, 1, 1))
                g.tensor_tensor(rstd[:], msq[:], half[:, 0:NCH], ALU.pow).then_inc(rstd_ready, 1)

            def skip(s, c):
                if c == 0:
                    pool.wait_ge(xs_ready, nth(s, 2, 2))
                if (v := nth(s, 4, c)) is not None:
                    pool.wait_ge(yz_ready, v)
                g.tensor_tensor(xd[:].rearrange("p (h d) -> p h d", h=NH), xs[:, c, :].rearrange("p (h d) -> p h d", h=NH),
                                d_bc[:].unsqueeze(2).to_broadcast([P, NH, HD]), ALU.mult).then_inc(xd_ready, 1)

            def weigh(s, c):
                for hf in range(2):
                    pool.wait_ge(decay_ready, nth(s, 8, 2 * c + hf + 1))
                    if hf == 0 and (v := nth(s, 3, c)) is not None:
                        pool.wait_ge(s_psum, v)
                    g.tensor_tensor(xw[:, :, hf, :], xs[:, c, :].rearrange("p (n t d) -> p n t d", n=NP, t=2)[:, :, hf, :],
                                    decay[:, hf, :, P - 1:P].to_broadcast([P, NP, HD]), ALU.mult).then_inc(xw_ready, 1)

            def add_term(prev, e):
                pool.wait_ge(term_ready, nth(prev, 4, e + 1))
                if e == 0:
                    pool.wait_ge(shared_ready, nth(prev, 1, 1))
                else:
                    pool.wait_ge(acc_ready, nth(prev, 4, e))
                g.tensor_tensor(acc, acc, term, ALU.add).then_inc(acc_ready, 1)

            def body(s, prev, older):
                last = is_seq(s, n_seq - 1)
                if is_seq(s, 0):
                    rsqrt1(0)
                if prev is not None:
                    rsqrt2(prev)
                if older is not None:
                    add_term(older, 3)
                for i in range(CHUNKS_FROM, NBLK):
                    c, step = divmod(i - CHUNKS_FROM, 3)
                    if s is not None and step == 0:
                        skip(s, c)
                        if c < NCH - 1:
                            weigh(s, c)
                    if s is not None and i == 16 and not last:
                        rsqrt1(s + 1)
                    if prev is not None and i in (15 + LAG, 19 + LAG):
                        add_term(prev, (i - 15 - LAG) // 4)
                if prev is not None:
                    add_term(prev, 2)
                if s is not None:
                    rsqrt_y(s)

            bodies(pool, body)


_INS = ["hidden", "w_norm_in", "w_in_proj", "conv_w", "conv_b", "w_dt", "b_dt", "A_log", "D", "w_norm_out", "w_out_proj"]
_FFN = ["gate_w", "gate_b", "sw1", "sb1", "sw2", "sb2", "rw1", "rb1", "rw2", "rb2"]


def kernel(**inputs):
    import concourse.bacc as _bacc
    from concourse import mybir as _mybir
    from concourse.bass_utils import run_bass_kernel_spmd as _run

    nc = _bacc.Bacc("TRN2", target_bir_lowering=False, num_devices=1)
    arrays, args = {}, {}
    for name in ["L0_attn_" + n for n in _INS] + ["L0_ffn_" + n for n in _FFN]:
        v = np.ascontiguousarray(inputs[name])
        arrays[name + "_dram"] = v
        args[name.split("_", 2)[2]] = nc.dram_tensor(name + "_dram", v.shape, _mybir.dt.from_np(v.dtype), kind="ExternalInput").ap()
    out = nc.dram_tensor("out_dram", inputs["L0_attn_hidden"].shape, _mybir.dt.float32, kind="ExternalOutput").ap()
    build(nc, args, out)
    r = _run(nc, [arrays], core_ids=[0])
    return r.results[0]["out_dram"]
```

```python
from contextlib import ExitStack

import numpy as np

import concourse.bass as bass
from concourse import mybir

ALU = mybir.AluOpType
ACT = mybir.ActivationFunctionType
AX_X = mybir.AxisListType.X
F32 = mybir.dt.float32
F32R = mybir.dt.float32r
BF16 = mybir.dt.bfloat16

P = 128
NCH = 4
SEQ = NCH * P
DI = 256
NB = DI // P
NH = 8
NP = NH // 2
HD = DI // NH
NS = 64
NG = 6
NE = 4
NF = 4
NBLK = NG * NF
TAPS = 4
RING = 3
LAG = 2
CHUNKS_FROM = 12
LATE = 4
LN_EPS = 1e-5
RMS_EPS = float(np.finfo(np.float32).eps)
CLAMP = 30.0
MASKED = -1e30

Z0, DT0, X0, B0, C0, WCOLS = 0, 256, 512, 768, 1280, 1792


def nth(s, per, k):
    if isinstance(s, int) and s * per + k <= 0:
        return None
    return s * per + k


def is_seq(s, n):
    return isinstance(s, int) and s == n


def build(nc, a, out):
    n_seq = a["hidden"].shape[0]
    x_dram = a["hidden"].rearrange("s (c p) d -> s p c d", p=P)
    out_dram = out.rearrange("s (c p) d -> s p c d", p=P)

    with ExitStack() as ctx:
        def sb(name, shape, dt=F32):
            return ctx.enter_context(nc.sbuf_tensor(name, shape, dt))

        def sem(name):
            return ctx.enter_context(nc.semaphore(name))

        bank = [ctx.enter_context(nc.psum_tensor(f"bank{i}", [P, 512], F32)) for i in range(8)]
        HID = bank[0:2]
        FOUT = bank[2]
        TR = bank[3]
        MAIN = bank[4:8]
        TR_BF = TR[:, 0:256].bitcast(BF16)
        B2_BF = MAIN[2][:, 0:256].bitcast(BF16)

        ident = sb("ident", [P, P])
        ident_bf = sb("ident_bf", [P, P], BF16)
        ones = sb("ones", [P, P])
        upto = sb("upto", [P, P])
        mask = sb("mask", [P, NP, P], BF16)
        pick_head = sb("pick_head", [3 * NH, NH, P], BF16)
        minus_head = sb("minus_head", [3 * NH, NH, P], BF16)
        pick_expert = sb("pick_expert", [3 * NE, NE, P], BF16)
        lower = sb("lower", [P, NE, NE])
        carrier = sb("carrier", [P, RING + 1])
        half = sb("half", [P, 8])

        BT = sb("BT", [P, NP, SEQ])
        CT = sb("CT", [P, NP, SEQ])
        w_raw = CT[:].rearrange("p n t -> p (n t)")[:, 0:1544]
        wh = sb("wh", [P, WCOLS], F32R)
        wl = sb("wl", [P, WCOLS], F32R)
        rows = sb("rows", [35, P])
        cols = sb("cols", [P, 35])
        b1 = cols[:, 0:24]
        b2s = cols[:, 24:26]
        b2r = cols[:, 26:30]
        conv_b = cols[:, 30:32]
        wn_in = cols[:, 32:33]
        wn_out = cols[:, 33:35]
        b2sh = sb("b2sh", [P, 1])
        b2sum = sb("b2sum", [P, 1])
        conv_w = sb("conv_w", [P, NB, TAPS])
        w_dt = sb("w_dt", [NH, DI])
        wdtT = sb("wdtT", [NH, P])
        b_dt = sb("b_dt", [P, DI])
        a_log = sb("a_log", [P, NH])
        a_exp = sb("a_exp", [P, NH])
        a_neg = sb("a_neg", [P, NH])
        d_bc = sb("d_bc", [P, NH])
        w_out_raw = sb("w_out_raw", [P, NB, P])
        w_out = sb("w_out", [P, NB, P])
        gw = sb("gw", [P, NE])
        gwh = sb("gwh", [P, NE], F32R)
        gwl = sb("gwl", [P, NE], F32R)
        gb = sb("gb", [P, NE])
        late = sb("late", [P, 2 * NG * 512])
        wf_raw = late[:].rearrange("p (a n f) -> p a n f", a=2, n=NG)
        used = [0]

        def late_part(n):
            used[0] += n
            return late[:, used[0] - n:used[0]]

        w1h = sb("w1h", [P, NG, 512], F32R)
        w1l = sb("w1l", [P, NG, 512], F32R)
        w2h = sb("w2h", [P, NG, NF, P], F32R)
        w2l = sb("w2l", [P, NG, NF, P], F32R)

        x_in = sb("x_in", [P, NCH, P])
        st1 = sb("st1", [P, NCH, 6])
        mv1 = sb("mv1", [P, NCH, 2])
        v1 = sb("v1", [P, 2, NCH])
        rs1 = sb("rs1", [P, 2, NCH])
        one_rs = sb("one_rs", [P, NCH])
        mean_rs = sb("mean_rs", [P, NCH])
        hn = sb("hn", [P, NCH, P])
        xr = sb("xr", [P, NCH, P])
        hTh = sb("hTh", [P, SEQ], F32R)
        hTl = sb("hTl", [P, SEQ], F32R)
        xpad = sb("xpad", [P, NB, TAPS - 1 + SEQ])
        cv = sb("cv", [P, NB, SEQ])
        tap = sb("tap", [P, SEQ])
        xs = sb("xs", [P, NCH, DI])
        sz = sb("sz", [P, NCH, DI])
        dtv = sb("dtv", [P, NCH, DI])
        sp = sb("sp", [P, NCH, DI])
        dsum = sb("dsum", [P, NCH * NH])
        dta = sb("dta", [P, NCH * NH])
        ecs = sb("ecs", [P, NCH, NH])
        tdx = sb("tdx", [P, NCH, NP])
        rem1 = sb("rem1", [P, NCH, NH])
        rem2 = sb("rem2", [P, NCH, NH])
        lparts = sb("lparts", [P, NCH, 3, NH], BF16)
        lT = sb("lT", [3 * NH, SEQ], BF16)
        btok = sb("btok", [P, NP * P])
        decay = sb("decay", [P, 2, NP, P])
        mg = sb("mg", [P, 2, NP, P])
        xw = sb("xw", [P, NP, 2, HD])
        xd = sb("xd", [P, DI])
        state = sb("state", [P, NP, 2 * HD])
        state_m = sb("state_m", [P, NP, 2 * HD])
        yt = sb("yt", [P, DI])
        yz = sb("yz", [P, DI])
        junk = sb("junk", [P, DI])
        ssq = sb("ssq", [P, NCH])
        msq = sb("msq", [P, NCH])
        rstd = sb("rstd", [P, NCH])
        yT = sb("yT", [P, NB, SEQ])
        x1 = late_part(NCH * P).rearrange("p (c d) -> p c d", c=NCH)
        st2 = sb("st2", [P, NCH, 6])
        mv2 = sb("mv2", [P, NCH, 2])
        v2 = sb("v2", [P, NCH])
        rs2 = sb("rs2", [P, NCH])
        x1_kept = sb("x1_kept", [P, NCH, P])
        fn = late_part(NCH * P).rearrange("p (c d) -> p c d", c=NCH)
        fTh = sb("fTh", [P, SEQ], F32R)
        fTl = sb("fTl", [P, SEQ], F32R)
        lg = sb("lg", [P, NCH, NE])
        gmax = sb("gmax", [P, NCH])
        gexp = sb("gexp", [P, NCH, NE])
        gsum = sb("gsum", [P, NCH])
        gw_n = sb("gw_n", [P, NCH, NE])
        above = sb("above", [P, NCH, NE, NE])
        level = sb("level", [P, NCH, NE, NE])
        rank = sb("rank", [P, NCH * NE])
        kept = sb("kept", [P, NCH, NE])
        grem1 = sb("grem1", [P, NCH, NE])
        grem2 = sb("grem2", [P, NCH, NE])
        gparts = sb("gparts", [P, NCH, 3, NE], BF16)
        gT = sb("gT", [3 * NE, SEQ], BF16)
        wbc = late_part(NE * SEQ).rearrange("p (e t) -> p e t", e=NE)
        act_f = late_part(RING * SEQ).rearrange("p (r t) -> p r t", r=RING)
        act_h = sb("act_h", [P, RING, SEQ], F32R)
        act_l = sb("act_l", [P, RING, SEQ], F32R)
        acc = late_part(SEQ)
        term = late_part(SEQ)
        out_t = late_part(NCH * P).rearrange("p (c d) -> p c d", c=NCH)

        def f(ap):
            return ap.bitcast(F32)

        rows_in, win_in, wdt_in, wf_in, small_in = (sem(n) for n in ("rows_in", "win_in", "wdt_in", "wf_in", "small_in"))
        zeros_set, consts_set, tables_set = sem("zeros_set"), sem("consts_set"), sem("tables_set")
        cols_psum, cols_set, w_scaled, wdtT_psum, wdtT_set = (sem(n) for n in ("cols_psum", "cols_set", "w_scaled", "wdtT_psum", "wdtT_set"))
        wdt_psum, wh_set, wl_set, weights_set, a_set, b2_set = (sem(n) for n in ("wdt_psum", "wh_set", "wl_set", "weights_set", "a_set", "b2_set"))
        fh_set, fl_set = sem("fh_set"), sem("fl_set")
        x_loaded = sem("x_loaded")
        ln1_stats = sem("ln1_stats")
        ln1_mv = sem("ln1_mv")
        ln1_v = sem("ln1_v")
        ln1_rs = sem("ln1_rs")
        hn_ready = sem("hn_ready")
        hnT_psum = sem("hnT_psum")
        hTh_ready = sem("hTh_ready")
        hTl_ready = sem("hTl_ready")
        xr_scales = sem("xr_scales")
        xr_ready = sem("xr_ready")
        proj_psum = sem("proj_psum")
        xpad_ready = sem("xpad_ready")
        sz_ready = sem("sz_ready")
        dtv_ready = sem("dtv_ready")
        b_ready = sem("b_ready")
        c_ready = sem("c_ready")
        c2_ready = sem("c2_ready")
        conv_step = sem("conv_step")
        conv1_step = sem("conv1_step")
        xtok_psum = sem("xtok_psum")
        xs_ready = sem("xs_ready")
        dt_clamped = sem("dt_clamped")
        dt_exp = sem("dt_exp")
        dt_log = sem("dt_log")
        dt_steps = sem("dt_steps")
        lcs_psum = sem("lcs_psum")
        ecs_ready = sem("ecs_ready")
        lpart_steps = sem("lpart_steps")
        lT_psum = sem("lT_psum")
        lT_ready = sem("lT_ready")
        seg_psum = sem("seg_psum")
        decay_ready = sem("decay_ready")
        btok_psum = sem("btok_psum")
        btok_ready = sem("btok_ready")
        g_psum = sem("g_psum")
        mg_ready = sem("mg_ready")
        xw_ready = sem("xw_ready")
        xd_ready = sem("xd_ready")
        y_psum = sem("y_psum")
        s_psum = sem("s_psum")
        state_step = sem("state_step")
        y_steps = sem("y_steps")
        yz_ready = sem("yz_ready")
        ssq_ready = sem("ssq_ready")
        yT_psum = sem("yT_psum")
        yT_ready = sem("yT_ready")
        o_psum = sem("o_psum")
        msq_ready = sem("msq_ready")
        rstd_ready = sem("rstd_ready")
        x1_ready = sem("x1_ready")
        x1_kept_ready = sem("x1_kept_ready")
        ln2_stats = sem("ln2_stats")
        ln2_mv = sem("ln2_mv")
        ln2_v = sem("ln2_v")
        ln2_rs = sem("ln2_rs")
        fn_ready = sem("fn_ready")
        fT_psum = sem("fT_psum")
        fTh_ready = sem("fTh_ready")
        fTl_ready = sem("fTl_ready")
        gate_psum = sem("gate_psum")
        gate_logits = sem("gate_logits")
        gate_exp = sem("gate_exp")
        gate_steps = sem("gate_steps")
        gate_kept = sem("gate_kept")
        gT_psum = sem("gT_psum")
        gT_ready = sem("gT_ready")
        wbc_psum = sem("wbc_psum")
        wbc_ready = sem("wbc_ready")
        hid_psum = sem("hid_psum")
        act_ready = sem("act_ready")
        act_h_ready = sem("act_h_ready")
        act_l_ready = sem("act_l_ready")
        second_done = sem("second_done")
        shared_ready = sem("shared_ready")
        term_ready = sem("term_ready")
        acc_ready = sem("acc_ready")
        outT_psum = sem("outT_psum")
        out_ready = sem("out_ready")
        out_stored = sem("out_stored")

        block = ctx.enter_context(nc.Block())

        def bodies(eng, body):
            body(0, None, None)
            body(1, 0, None)
            body(2, 1, 0)
            with eng.Fori(3, n_seq - 1) as s:
                body(s, s - 1, s - 2)
            body(n_seq - 1, n_seq - 2, n_seq - 3)
            body(None, n_seq - 1, n_seq - 2)
            body(None, None, n_seq - 1)

        def block_at(i, prev, older):
            q, b = (older, NBLK - LATE + i) if i < LATE else (prev, i - LATE)
            return None if q is None or i < 0 else (q, b)

        def at(k):
            return slice(k * P, (k + 1) * P)

        @block.sync
        def _(sp_eng):
            src = [a["sb1"].rearrange("n (b p) -> (n b) p", p=P), a["rb1"].rearrange("n (b p) -> (n b) p", p=P),
                   a["sb2"], a["rb2"], a["conv_b"].rearrange("(b p) -> b p", p=P),
                   a["w_norm_in"].rearrange("(b p) -> b p", p=P), a["w_norm_out"].rearrange("(b p) -> b p", p=P)]
            sp_eng.dma_start(x_in[:], x_dram[0]).then_inc(x_loaded, 16)
            sp_eng.dma_start(w_raw, a["w_in_proj"]).then_inc(win_in, 16)
            r = 0
            for v in src:
                sp_eng.dma_start(rows[r:r + v.shape[0], :], v).then_inc(rows_in, 16)
                r += v.shape[0]
            sp_eng.dma_start(w_dt[:], a["w_dt"]).then_inc(wdt_in, 16)
            sp_eng.dma_start(b_dt[:], a["b_dt"].partition_broadcast(P)).then_inc(small_in, 16)
            sp_eng.dma_start(a_log[:], a["A_log"].partition_broadcast(P)).then_inc(small_in, 16)
            sp_eng.dma_start(d_bc[:], a["D"].partition_broadcast(P)).then_inc(small_in, 16)
            sp_eng.dma_start(gb[:], a["gate_b"].partition_broadcast(P)).then_inc(small_in, 16)
            sp_eng.dma_start(gw[:], a["gate_w"]).then_inc(small_in, 16)
            sp_eng.dma_start(conv_w[:], a["conv_w"].rearrange("(b p) one k -> p b (one k)", p=P)).then_inc(small_in, 16)
            sp_eng.dma_start(w_out_raw[:], a["w_out_proj"].rearrange("(b p) o -> p b o", p=P)).then_inc(small_in, 16)
            sp_eng.dma_start(wf_raw[:, 0, 0:2, :], a["sw1"].rearrange("n d f -> d n f")).then_inc(wf_in, 16)
            sp_eng.dma_start(wf_raw[:, 0, 2:6, :], a["rw1"].rearrange("n d f -> d n f")).then_inc(wf_in, 16)
            sp_eng.dma_start(wf_raw[:, 1, 0:2, :].rearrange("p n (b o) -> p n b o", o=P),
                             a["sw2"].rearrange("n (b p) o -> p n b o", p=P)).then_inc(wf_in, 16)
            sp_eng.dma_start(wf_raw[:, 1, 2:6, :].rearrange("p n (b o) -> p n b o", o=P),
                             a["rw2"].rearrange("n (b p) o -> p n b o", p=P)).then_inc(wf_in, 16)

            def body(s, prev, older):
                if s is not None and not is_seq(s, n_seq - 1):
                    sp_eng.wait_ge(xr_ready, nth(s, 4, 4))
                    sp_eng.dma_start(x_in[:], x_dram[s + 1]).then_inc(x_loaded, 16)
                if older is not None:
                    sp_eng.wait_ge(out_ready, nth(older, 1, 1))
                    sp_eng.dma_start(out_dram[older], out_t).then_inc(out_stored, 16)

            bodies(sp_eng, body)
            sp_eng.wait_ge(out_stored, 16 * n_seq)

        @block.tensor
        def _(pe):
            mm = nc.tensor.matmul

            def split(dst, stat_h, stat_l, mov_h, mov_l):
                mm(dst, stat_h, mov_l, start=True, stop=False)
                mm(dst, stat_l, mov_h, start=False, stop=False)
                return mm(dst, stat_h, mov_h, start=False, stop=True)

            def hn_transposes(s):
                if (v := nth(s, 4, -1)) is not None:
                    pe.wait_ge(yT_ready, v)
                for c in range(NCH):
                    pe.wait_ge(hn_ready, nth(s, 4, c + 1))
                    ins = nc.tensor.transpose(TR[:, at(c)], hn[:, c, :], ident[:])
                ins.then_inc(hnT_psum, 1)

            def proj(s, j):
                dst = MAIN[j % 4 if j > 1 else 1 - j]
                pe.wait_ge(hTl_ready, nth(s, 1, 1))
                if is_seq(s, 0) and j in (0, 2):
                    pe.wait_ge(weights_set, 1 + j // 2)
                if j == 1 and (v := nth(s, 4, 0)) is not None:
                    pe.wait_ge(yz_ready, v)
                if j == 0 and (v := nth(s, 8, 0)) is not None:
                    pe.wait_ge(decay_ready, v)
                if j == 2 and (v := nth(s, 4, 0)) is not None:
                    pe.wait_ge(x1_ready, v)
                if j in (4, 5):
                    pe.wait_ge(xpad_ready, nth(s, 2, 2))
                if j in (6, 7, 8, 9):
                    pe.wait_ge(dtv_ready, nth(s, 4, j - 5))
                if j >= 10:
                    dst = MAIN[j - 10]
                    last, k = ((b_ready, 3), (b_ready, 4), (xs_ready, 1), (xs_ready, 2))[j - 10]
                    pe.wait_ge(last, nth(s, 2 if last is xs_ready else 4, k))
                if j < 2:
                    ins = split(dst[:], wh[:, X0 + j * P:X0 + (j + 1) * P], wl[:, X0 + j * P:X0 + (j + 1) * P], hTh[:], hTl[:])
                elif j < 6:
                    c = j - 2
                    ins = split(dst[:], hTh[:, at(c)], hTl[:, at(c)], wh[:, 0:512], wl[:, 0:512])
                else:
                    k = B0 + (j - 6) * P
                    ins = split(dst[:], wh[:, k:k + P], wl[:, k:k + P], hTh[:], hTl[:])
                ins.then_inc(proj_psum, 1)

            def x_tokens(s, i):
                pe.wait_ge(b_ready, nth(s, 4, i + 1))
                if i == 0:
                    pe.wait_ge(conv_step, nth(s, 4, 4))
                    pe.wait_ge(conv1_step, nth(s, 8, 8))
                for j in range(2):
                    for b in range(NB):
                        ins = nc.tensor.transpose(MAIN[2 + i][:, at(2 * j + b)], cv[:, b, at(2 * i + j)], ident[:])
                ins.then_inc(xtok_psum, 1)

            def lcs(s, prev, older):
                if older is not None:
                    pe.wait_ge(out_ready, nth(older, 1, 1))
                elif prev is not None:
                    pe.wait_ge(gate_logits, nth(prev, 3, 1))
                if is_seq(s, 0):
                    pe.wait_ge(tables_set, 14)
                pe.wait_ge(dt_steps, nth(s, 3, 3))
                mm(TR[:, 0:32], upto[:], dta[:], start=True, stop=True)
                mm(TR[:, 32:64], ones[:], dta[:], start=True, stop=True).then_inc(lcs_psum, 1)

            def l_transposes(s):
                pe.wait_ge(ecs_ready, nth(s, 3, 3))
                pe.wait_ge(lpart_steps, nth(s, 5, 5))
                for c in range(NCH):
                    ins = nc.tensor.transpose(TR_BF[0:3 * NH, at(c)], lparts[:, c, :, :].rearrange("p a h -> p (a h)"), ident_bf[:])
                ins.then_inc(lT_psum, 1)

            def segments(s, c):
                for hf in range(2):
                    dst = MAIN[hf]
                    if c == 0 and hf == 0:
                        pe.wait_ge(lT_ready, nth(s, 1, 1))
                        pe.wait_ge(c_ready, nth(s, 1, 1))
                        pe.wait_ge(c2_ready, nth(s, 3, 1))
                    if c > 0 and hf == 0:
                        pe.wait_ge(y_steps, nth(s, 10, 1 if c == 1 else 3 * c - 3))
                    if c > 0 and hf == 1:
                        pe.wait_ge(state_step, nth(s, 8, (2, 5, 8)[c - 1]))
                    mm(dst[:], ident_bf[:], mask[:].rearrange("p n l -> p (n l)"), start=True, stop=False)
                    for n in range(NP):
                        mm(dst[:, at(n)], pick_head[:, 2 * n + hf, :], lT[:, at(c)], start=False, stop=False)
                    mm(dst[:], lT[:, at(c)], minus_head[:].rearrange("r (n t) l -> r t n l", t=2)[:, hf, :, :],
                       start=False, stop=True).then_inc(seg_psum, 1)

            def b_tokens(s, c):
                if c == 0:
                    pe.wait_ge(lT_ready, nth(s, 1, 1))
                    pe.wait_ge(b_ready, nth(s, 4, 4))
                if c > 1:
                    pe.wait_ge(yT_ready, nth(s, 4, c - 1))
                for n in range(NP):
                    ins = nc.tensor.transpose(TR[:, at(n)], BT[:, n, at(c)], ident[:])
                ins.then_inc(btok_psum, 1)

            def gram(s, c, prev):
                if c == 0:
                    pe.wait_ge(c2_ready, nth(s, 3, 3))
                    if prev is not None:
                        pe.wait_ge(wbc_ready, nth(prev, 4, 4))
                else:
                    pe.wait_ge(mg_ready, nth(s, 8, 2 * c))
                for n in range(NP):
                    for hf in range(2):
                        q = slice(NS * hf, NS * hf + NS)
                        ins = mm(MAIN[2 + hf][:, at(n)], BT[q, n, at(c)], CT[q, n, at(c)], start=True, stop=True)
                        if n == NP - 1:
                            ins.then_inc(g_psum, 1)

            def y_product(s, c):
                pe.wait_ge(decay_ready, nth(s, 8, 2 * c + 2))
                if c > 0:
                    pe.wait_ge(state_step, nth(s, 8, (2, 5, 8)[c - 1]))
                    for n in range(NP):
                        mm(MAIN[0][:, 256 + n * 64:320 + n * 64], CT[:, n, at(c)], state[:, n, :], start=True, stop=True)
                if c < NCH - 1:
                    pe.wait_ge(btok_ready, nth(s, 3, c + 1))
                    pe.wait_ge(xw_ready, nth(s, 6, 2 * c + 2))
                    for n in range(NP):
                        ins = mm(MAIN[1][:, n * 64:(n + 1) * 64], btok[:, at(n)], xw[:, n, :, :].rearrange("p t d -> p (t d)"),
                                 start=True, stop=True)
                    ins.then_inc(s_psum, 1)
                pe.wait_ge(mg_ready, nth(s, 8, 2 * c + 2))
                for hf in range(2):
                    for n in range(NP):
                        h = 2 * n + hf
                        ins = mm(MAIN[0][:, h * HD:(h + 1) * HD], mg[:, hf, n, :], xs[:, c, h * HD:(h + 1) * HD],
                                 start=True, stop=True)
                ins.then_inc(y_psum, 1)

            def y_transposes(s, c):
                if c < NCH - 2:
                    pe.wait_ge(btok_ready, nth(s, 3, c + 2))
                elif c < NCH - 1 or is_seq(s, n_seq - 1):
                    pe.wait_ge(yT_ready, nth(s, 4, c))
                else:
                    pe.wait_ge(hTl_ready, nth(s + 1, 1, 1))
                pe.wait_ge(yz_ready, nth(s, 4, c + 1))
                for b in range(NB):
                    ins = nc.tensor.transpose(TR[:, at(b)], yz[:, at(b)], ident[:])
                ins.then_inc(yT_psum, 1)

            def out_projection(s):
                pe.wait_ge(mg_ready, nth(s, 8, 8))
                pe.wait_ge(yT_ready, nth(s, 4, 4))
                for c in range(NCH):
                    for b in range(NB):
                        ins = mm(MAIN[2][:, at(c)], yT[:, b, at(c)], w_out[:, b, :], start=(b == 0), stop=(b == NB - 1))
                ins.then_inc(o_psum, 1)

            def f_transposes(s, prev):
                pe.wait_ge(yT_ready, nth(prev, 4, 4))
                for c in range(NCH):
                    pe.wait_ge(fn_ready, nth(prev, 4, c + 1))
                    ins = nc.tensor.transpose(TR[:, at(c)], fn[:, c, :], ident[:])
                ins.then_inc(fT_psum, 1)

            def gate(prev):
                pe.wait_ge(fTl_ready, nth(prev, 1, 1))
                for c in range(NCH):
                    ins = split(TR[:, c * NE:(c + 1) * NE], fTh[:, at(c)], fTl[:, at(c)], gwh[:], gwl[:])
                ins.then_inc(gate_psum, 1)

            def g_transposes(s, prev):
                if s is not None:
                    pe.wait_ge(c2_ready, nth(s, 3, 2))
                pe.wait_ge(gate_steps, nth(prev, 13, 13))
                for c in range(NCH):
                    ins = nc.tensor.transpose(B2_BF[0:3 * NE, at(c)], gparts[:, c, :, :].rearrange("p a h -> p (a h)"), ident_bf[:])
                ins.then_inc(gT_psum, 1)

            def weight_rows(s, prev, e):
                if e == 0:
                    pe.wait_ge(gT_ready, nth(prev, 1, 1))
                if e == 0 and s is not None:
                    pe.wait_ge(c2_ready, nth(s, 3, 3))
                if e >= 2:
                    pe.wait_ge(wbc_ready, nth(prev, 4, e - 1))
                mm(MAIN[3 - e % 2][:], pick_expert[:, e, :], gT[:], start=True, stop=True).then_inc(wbc_psum, 1)

            def first(prev, b):
                if is_seq(prev, 0) and b == 0:
                    pe.wait_ge(fl_set, 2)
                g, k = divmod(b, NF)
                if (v := nth(prev, NBLK, b - 1)) is not None:
                    pe.wait_ge(act_ready, v)
                if b == 0:
                    pe.wait_ge(fTl_ready, nth(prev, 1, 1))
                split(HID[b % 2][:], w1h[:, g, at(k)], w1l[:, g, at(k)], fTh[:], fTl[:]).then_inc(hid_psum, 1)

            def second(prev, b):
                g, k = divmod(b, NF)
                begins = b in (0, 8, 12, 16, 20)
                ends = b in (7, 11, 15, 19, 23)
                if b == 0:
                    if (v := nth(prev, 4, 0)) is not None:
                        pe.wait_ge(term_ready, v)
                if b == 8:
                    pe.wait_ge(shared_ready, nth(prev, 1, 1))
                if b in (12, 16, 20):
                    pe.wait_ge(term_ready, nth(prev, 4, b // 4 - 2))
                r = b % RING
                pe.wait_ge(act_l_ready, nth(prev, NBLK, b + 1))
                mm(FOUT[:], w2h[:, g, k, :], act_l[:, r, :], start=begins, stop=False)
                mm(FOUT[:], w2l[:, g, k, :], act_h[:, r, :], start=False, stop=False)
                mm(FOUT[:], w2h[:, g, k, :], act_h[:, r, :], start=False, stop=ends).then_inc(second_done, 1)

            def out_transposes(prev, older):
                if prev is not None:
                    pe.wait_ge(gate_logits, nth(prev, 3, 1))
                else:
                    pe.wait_ge(fTl_ready, nth(older, 1, 1))
                pe.wait_ge(acc_ready, nth(older, 4, 4))
                for c in range(NCH):
                    ins = nc.tensor.transpose(TR[:, at(c)], acc[:, at(c)], ident[:])
                ins.then_inc(outT_psum, 1)

            def scan_part(s, prev, older, i):
                if i == 0 and is_seq(s, 0):
                    proj(s, 0)
                    proj(s, 1)
                if i == 2:
                    proj(s, 2)
                    proj(s, 3)
                if i == 3:
                    proj(s, 4)
                if i == 4:
                    proj(s, 5)
                    proj(s, 6)
                    proj(s, 7)
                if i in (5, 6):
                    proj(s, i + 3)
                    x_tokens(s, i - 5)
                if i == 7:
                    proj(s, 10)
                    proj(s, 11)
                if i in (8, 9):
                    proj(s, i + 4)
                if i == 10:
                    lcs(s, prev, older)
                if i == 11:
                    l_transposes(s)
                if i >= CHUNKS_FROM:
                    c, step = divmod(i - CHUNKS_FROM, 3)
                    if step == 0:
                        segments(s, c)
                        if c < NCH - 1:
                            b_tokens(s, c)
                    if step == 1:
                        if c > 0:
                            y_transposes(s, c - 1)
                        gram(s, c, prev)
                    if step == 2:
                        if c == NCH - 1 and not is_seq(s, n_seq - 1):
                            hn_transposes(s + 1)
                        y_product(s, c)

            def body(s, prev, older):
                for i in range(NBLK):
                    if prev is not None:
                        if i == 5:
                            gate(prev)
                    if s is not None and i != CHUNKS_FROM:
                        scan_part(s, prev, older, i)
                    if prev is not None:
                        if i == 10:
                            g_transposes(s, prev)
                        if i in (11, 12):
                            weight_rows(s, prev, 2 * i - 22)
                            weight_rows(s, prev, 2 * i - 21)
                    if s is not None and i == CHUNKS_FROM:
                        scan_part(s, prev, older, i)
                    if older is not None and i == 7:
                        out_transposes(prev, older)
                    if new := block_at(i, prev, older):
                        first(*new)
                    if prev is not None and i == LATE - 1:
                        f_transposes(s, prev)
                    if old := block_at(i - LAG, prev, older):
                        second(*old)
                if prev is not None:
                    second(prev, NBLK - LATE - 2)
                    second(prev, NBLK - LATE - 1)
                if s is not None:
                    ahead = not is_seq(s, n_seq - 1)
                    if ahead:
                        proj(s + 1, 0)
                    y_transposes(s, NCH - 1)
                    if ahead:
                        proj(s + 1, 1)
                    out_projection(s)

            pe.wait_ge(tables_set, 1)
            pe.wait_ge(rows_in, 7 * 16)
            nc.tensor.transpose(MAIN[0][:, 0:35], rows[:], ident[0:35, 0:35]).then_inc(cols_psum, 1)
            hn_transposes(0)
            pe.wait_ge(w_scaled, 1)
            nc.tensor.transpose(MAIN[1][0:NH, 0:P], w_raw[:, 1536:1544], ident[:]).then_inc(wdtT_psum, 1)
            pe.wait_ge(wdtT_set, 1)
            pe.wait_ge(wdt_in, 16)
            mm(MAIN[2][:, 0:DI], wdtT[:], w_dt[:], start=True, stop=True).then_inc(wdt_psum, 1)

            bodies(pe, body)

        @block.scalar
        def _(act):
            nc.scalar.preload_act_table_set("natural_log_exp_and_others")
            def ffn_high(k):
                if k == 0:
                    act.wait_ge(wf_in, 4 * 16)
                    nc.scalar.copy(w1h[:], wf_raw[:, 0]).then_inc(fh_set, 1)
                else:
                    nc.scalar.copy(w2h[:].rearrange("p n b o -> p (n b o)"), wf_raw[:, 1].rearrange("p n f -> p (n f)"))\
                        .then_inc(fh_set, 1)

            def hT(s):
                act.wait_ge(hnT_psum, nth(s, 1, 1))
                nc.scalar.copy(hTh[:], TR[:]).then_inc(hTh_ready, 1)

            def x_copy(s, b):
                act.wait_ge(proj_psum, nth(s, 14, b + 1))
                nc.scalar.copy(xpad[:, b, TAPS - 1:], MAIN[1 - b][:]).then_inc(xpad_ready, 1)

            def fT(prev):
                act.wait_ge(fT_psum, nth(prev, 1, 1))
                nc.scalar.copy(fTh[:], TR[:]).then_inc(fTh_ready, 1)

            def silu_z(s, c):
                act.wait_ge(proj_psum, nth(s, 14, c + 3))
                nc.scalar.activation(sz[:, c, :], MAIN[(c + 2) % 4][:, 0:DI], ACT.Silu).then_inc(sz_ready, 1)

            def b_copy(s, b):
                act.wait_ge(proj_psum, nth(s, 14, b + 7))
                nc.scalar.copy(BT[:, b, :], MAIN[(b + 2) % 4][:]).then_inc(b_ready, 1)

            def c_copy(s, b):
                act.wait_ge(proj_psum, nth(s, 14, b + 11))
                nc.scalar.copy(CT[:, b, :], MAIN[b][:]).then_inc(c2_ready, 1)

            def silu_x(s, i):
                act.wait_ge(xtok_psum, nth(s, 2, i + 1))
                nc.scalar.activation(xs[:, 2 * i:2 * i + 2, :].rearrange("p c d -> p (c d)"), MAIN[2 + i][:], ACT.Silu)\
                    .then_inc(xs_ready, 1)

            def softplus(s):
                act.wait_ge(dt_clamped, nth(s, 1, 1))
                nc.scalar.activation(sp[:], sp[:], ACT.Exp).then_inc(dt_exp, 1)
                act.wait_ge(dt_exp, nth(s, 1, 1))
                nc.scalar.activation(sp[:], sp[:], ACT.Ln, bias=1.0).then_inc(dt_log, 1)

            def gate_exps(prev):
                act.wait_ge(gate_logits, nth(prev, 3, 3))
                nc.scalar.activation(gexp[:], lg[:], ACT.Exp).then_inc(gate_exp, 1)

            def chunk_decays(s):
                act.wait_ge(lcs_psum, nth(s, 1, 1))
                nc.scalar.activation(ecs[:].rearrange("p c h -> p (c h)"), TR[:, 0:32], ACT.Exp).then_inc(ecs_ready, 1)
                tot = TR[:, 32:64].rearrange("p (c n t) -> p c n t", n=NP, t=2)
                for t in range(2):
                    q = slice(64 * t, 64 * t + 64)
                    nc.scalar.activation(tdx[q, :, :], tot[q, :, :, t], ACT.Exp).then_inc(ecs_ready, 1)

            def weight_copy(prev, e):
                act.wait_ge(wbc_psum, nth(prev, 4, e + 1))
                nc.scalar.copy(wbc[:, e, :], MAIN[3 - e % 2][:]).then_inc(wbc_ready, 1)

            def relu(prev, b):
                act.wait_ge(hid_psum, nth(prev, NBLK, b + 1))
                if (v := nth(prev, NBLK, b + 1 - RING)) is not None:
                    act.wait_ge(second_done, v)
                nc.scalar.activation(act_h[:, b % RING, :], HID[b % 2][:], ACT.Relu, bias=b1[:, b:b + 1])\
                    .then_inc(act_h_ready, 1)
                nc.scalar.activation(act_f[:, b % RING, :], HID[b % 2][:], ACT.Relu, bias=b1[:, b:b + 1])\
                    .then_inc(act_ready, 1)

            def keep_x1(prev, older):
                if older is not None:
                    act.wait_ge(out_ready, nth(older, 1, 1))
                act.wait_ge(x1_ready, nth(prev, 4, 4))
                nc.scalar.copy(x1_kept[:], x1).then_inc(x1_kept_ready, 1)

            def shared_out(prev):
                act.wait_ge(second_done, nth(prev, NBLK, 8))
                if (v := nth(prev, 1, 0)) is not None:
                    act.wait_ge(outT_psum, v)
                nc.scalar.activation(acc, FOUT[:], ACT.Identity, bias=b2sum[:], scale=0.5).then_inc(shared_ready, 1)

            def decays(s, c):
                for hf in range(2):
                    act.wait_ge(seg_psum, nth(s, 8, 2 * c + hf + 1))
                    if hf == 0 and (v := nth(s, 8, 2 * c)) is not None:
                        act.wait_ge(mg_ready, v)
                    if c > 0 and hf == 0:
                        act.wait_ge(xw_ready, nth(s, 6, 2 * c))
                    nc.scalar.activation(decay[:, hf, :, :].rearrange("p n l -> p (n l)"), MAIN[hf][:], ACT.Exp)\
                        .then_inc(decay_ready, 1)
                if c < NCH - 1:
                    act.wait_ge(btok_psum, nth(s, 3, c + 1))
                    nc.scalar.copy(btok[:], TR[:]).then_inc(btok_ready, 1)

            def y_out(s, c):
                act.wait_ge(yz_ready, nth(s, 4, c + 1))
                nc.scalar.activation(junk[:], yz[:], ACT.Square, accum_out=ssq[:, c:c + 1]).then_inc(ssq_ready, 1)
                act.wait_ge(yT_psum, nth(s, 4, c + 1))
                nc.scalar.copy(yT[:, :, at(c)], TR[:, 0:DI].rearrange("p (b t) -> p b t", t=P)).then_inc(yT_ready, 1)

            def scan_part(s, i):
                if i == 0:
                    x_copy(s, 0)
                    x_copy(s, 1)
                if i == 2:
                    nc.scalar.preload_act_table_set("silu_and_others")
                    silu_z(s, 0)
                    silu_z(s, 1)
                if i in (3, 4):
                    silu_z(s, i - 1)
                if i == 4:
                    b_copy(s, 0)
                    b_copy(s, 1)
                if i in (5, 6):
                    b_copy(s, i - 3)
                    silu_x(s, i - 5)
                if i in (7, 8, 9):
                    c_copy(s, i - 6)
                if i == 10:
                    if is_seq(s, 0):
                        ffn_high(0)
                    chunk_decays(s)
                if i >= CHUNKS_FROM:
                    c, step = divmod(i - CHUNKS_FROM, 3)
                    if step == 0:
                        decays(s, c)
                    if step == 1 and c > 0:
                        y_out(s, c - 1)
                    if step == 2 and c == NCH - 1 and not is_seq(s, n_seq - 1):
                        hT(s + 1)

            def body(s, prev, older):
                for i in range(NBLK):
                    if prev is not None and i == LATE - 1:
                        fT(prev)
                    if prev is not None and i in (11, 12):
                        weight_copy(prev, 2 * i - 22)
                        weight_copy(prev, 2 * i - 21)
                    if s is not None:
                        scan_part(s, i)
                    if is_seq(s, 0) and i == 14:
                        ffn_high(1)
                    if prev is not None and i == 9:
                        keep_x1(prev, older)
                    if new := block_at(i, prev, older):
                        relu(*new)
                    if s is not None and i == 6:
                        nc.scalar.preload_act_table_set("natural_log_exp_and_others")
                    if prev is not None and i == 6:
                        gate_exps(prev)
                    if s is not None and i == 6:
                        softplus(s)
                    if prev is not None and i == 7 + LATE + LAG:
                        shared_out(prev)
                if s is not None:
                    y_out(s, NCH - 1)

            act.wait_ge(cols_psum, 1)
            nc.scalar.copy(cols[:], MAIN[0][:, 0:35]).then_inc(cols_set, 1)
            hT(0)
            act.wait_ge(wdtT_psum, 1)
            nc.scalar.copy(wdtT[:], MAIN[1][0:NH, 0:P]).then_inc(wdtT_set, 1)
            act.wait_ge(cols_set, 1)
            nc.scalar.activation(b2sh[:], b2s[:, 0:1], ACT.Identity, bias=b2s[:, 1:2]).then_inc(b2_set, 1)
            act.wait_ge(b2_set, 1)
            nc.scalar.mul(b2sum[:], b2sh[:], 0.5).then_inc(b2_set, 1)
            act.wait_ge(b2_set, 2)
            act.wait_ge(small_in, 7 * 16)
            nc.scalar.activation(a_exp[:], a_log[:], ACT.Exp).then_inc(a_set, 1)

            bodies(act, body)

        @block.vector
        def _(dve):
            v_ = nc.vector

            def split_small():
                dve.wait_ge(a_set, 1)
                v_.tensor_scalar(a_neg[:], a_exp[:], -1.0 / HD, None, ALU.mult).then_inc(a_set, 1)
                v_.tensor_copy(gwh[:], gw[:]).then_inc(a_set, 1)
                dve.wait_ge(a_set, 3)
                v_.tensor_tensor(gwl[:], gw[:], f(gwh[:]), ALU.subtract).then_inc(a_set, 1)
                for b in range(NB):
                    v_.tensor_scalar(w_out[:, b, :], w_out_raw[:, b, :], wn_out[:, b:b + 1], None, ALU.mult).then_inc(a_set, 1)
                dve.wait_ge(a_set, 6)

            def norm1(s):
                dve.wait_ge(x_loaded, nth(s, 16, 16))
                for c in range(NCH):
                    v_.bn_stats(st1[:, c, :], x_in[:, c, :]).then_inc(ln1_stats, 1)
                dve.wait_ge(ln1_stats, nth(s, 4, 4))
                v_.memset(carrier[:, RING:RING + 1], 0.0)
                for c in range(NCH):
                    v_.bn_aggr(mv1[:, c, :], st1[:, c, :]).then_inc(ln1_mv, 1)
                dve.wait_ge(ln1_mv, nth(s, 4, 4))
                v_.tensor_scalar(v1[:, 0, :], mv1[:, :, 1], LN_EPS, None, ALU.add).then_inc(ln1_v, 1)
                v_.tensor_scalar(v1[:, 1, :], mv1[:, :, 1], 1.0 + RMS_EPS, LN_EPS * RMS_EPS, ALU.mult, ALU.add).then_inc(ln1_v, 1)

            def norm1_apply(s):
                dve.wait_ge(ln1_rs, nth(s, 1, 1))
                if (v := nth(s, 1, 0)) is not None:
                    dve.wait_ge(hnT_psum, v)
                for c in range(NCH):
                    v_.tensor_scalar(hn[:, c, :], x_in[:, c, :], mv1[:, c, 0:1], rs1[:, 1, c:c + 1], ALU.subtract, ALU.mult)\
                        .then_inc(hn_ready, 1)

            def residual(s):
                v_.tensor_scalar(one_rs[:], rs1[:, 0, :], 1.0, None, ALU.add).then_inc(xr_scales, 1)
                v_.tensor_tensor(mean_rs[:], mv1[:, :, 0], rs1[:, 0, :], ALU.mult).then_inc(xr_scales, 1)
                dve.wait_ge(xr_scales, nth(s, 2, 2))
                for c in range(NCH):
                    v_.tensor_scalar(xr[:, c, :], x_in[:, c, :], one_rs[:, c:c + 1], mean_rs[:, c:c + 1], ALU.mult, ALU.subtract)\
                        .then_inc(xr_ready, 1)

            def hT_low(s):
                dve.wait_ge(hTh_ready, nth(s, 1, 1))
                v_.tensor_tensor(hTl[:], TR[:], f(hTh[:]), ALU.subtract).then_inc(hTl_ready, 1)

            def conv(s, taps):
                for k in taps:
                    if k == 0:
                        dve.wait_ge(xpad_ready, nth(s, 2, 1))
                        v_.tensor_scalar(cv[:, 0, :], xpad[:, 0, 0:SEQ], conv_w[:, 0, 0:1], conv_b[:, 0:1], ALU.mult, ALU.add)\
                            .then_inc(conv_step, 1)
                    else:
                        dve.wait_ge(conv_step, nth(s, 4, k))
                        v_.scalar_tensor_tensor(cv[:, 0, :], xpad[:, 0, k:k + SEQ], conv_w[:, 0, k:k + 1], cv[:, 0, :],
                                                ALU.mult, ALU.add).then_inc(conv_step, 1)

            def dt_add(s, c):
                dve.wait_ge(sz_ready, nth(s, 4, c + 1))
                v_.tensor_tensor(dtv[:, c, :], MAIN[(c + 2) % 4][:, DI:2 * DI], b_dt[:], ALU.add).then_inc(dtv_ready, 1)

            def dt_clamp(s):
                dve.wait_ge(dtv_ready, nth(s, 4, 4))
                v_.tensor_scalar(sp[:], dtv[:], CLAMP, None, ALU.min).then_inc(dt_clamped, 1)

            def dt_decay(s):
                dve.wait_ge(dt_log, nth(s, 1, 1))
                v_.tensor_tensor(dtv[:], dtv[:], sp[:], ALU.max).then_inc(dt_steps, 1)
                dve.wait_ge(dt_steps, nth(s, 3, 1))
                v_.tensor_reduce(dsum[:], dtv[:].rearrange("p c (h d) -> p (c h) d", d=HD), AX_X, ALU.add).then_inc(dt_steps, 1)
                dve.wait_ge(dt_steps, nth(s, 3, 2))
                v_.tensor_tensor(dta[:].rearrange("p (c h) -> p c h", h=NH), dsum[:].rearrange("p (c h) -> p c h", h=NH),
                                 a_neg[:].unsqueeze(1).to_broadcast([P, NCH, NH]), ALU.mult).then_inc(dt_steps, 1)

            def three_parts(src, parts, r1, r2, steps, s, per, first):
                v_.tensor_copy(parts[:, :, 0, :], src).then_inc(steps, 1)
                dve.wait_ge(steps, nth(s, per, first + 1))
                v_.tensor_tensor(r1[:], src, parts[:, :, 0, :], ALU.subtract).then_inc(steps, 1)
                dve.wait_ge(steps, nth(s, per, first + 2))
                v_.tensor_copy(parts[:, :, 1, :], r1[:]).then_inc(steps, 1)
                dve.wait_ge(steps, nth(s, per, first + 3))
                v_.tensor_tensor(r2[:], r1[:], parts[:, :, 1, :], ALU.subtract).then_inc(steps, 1)
                dve.wait_ge(steps, nth(s, per, first + 4))
                v_.tensor_copy(parts[:, :, 2, :], r2[:]).then_inc(steps, 1)

            def l_parts(s):
                dve.wait_ge(ecs_ready, nth(s, 3, 3))
                three_parts(TR[:, 0:32].rearrange("p (c h) -> p c h", h=NH), lparts, rem1, rem2, lpart_steps, s, 5, 0)

            def lT_copy(s):
                dve.wait_ge(lT_psum, nth(s, 1, 1))
                v_.tensor_copy(lT[:], TR_BF[0:3 * NH, :]).then_inc(lT_ready, 1)

            def c_copy(s, b):
                dve.wait_ge(proj_psum, nth(s, 14, b + 11))
                v_.tensor_copy(CT[:, b, :], MAIN[b][:]).then_inc(c_ready, 1)

            def attend(s, c, step):
                if step == 1:
                    for hf in range(2):
                        dve.wait_ge(g_psum, nth(s, 8, 2 * c + hf + 1))
                        dve.wait_ge(decay_ready, nth(s, 8, 2 * c + hf + 1))
                        if hf == 0 and (v := nth(s, 4, c)) is not None:
                            dve.wait_ge(y_psum, v)
                        v_.tensor_tensor(mg[:, hf, :, :].rearrange("p n l -> p (n l)"), MAIN[2 + hf][:],
                                         decay[:, hf, :, :].rearrange("p n l -> p (n l)"), ALU.mult).then_inc(mg_ready, 1)
                if step == 2:
                    dve.wait_ge(y_psum, nth(s, 4, c + 1))
                    dve.wait_ge(xd_ready, nth(s, 4, c + 1))
                    if c == 0:
                        v_.tensor_tensor(yt[:], MAIN[0][:, 0:DI], xd[:], ALU.add).then_inc(y_steps, 1)
                        dve.wait_ge(y_steps, nth(s, 10, 1))
                    else:
                        first = 3 * c - 2
                        v_.tensor_tensor(yt[:].rearrange("p (h d) -> p h d", h=NH),
                                         MAIN[0][:, DI:2 * DI].rearrange("p (h d) -> p h d", h=NH),
                                         ecs[:, c, :].unsqueeze(2).to_broadcast([P, NH, HD]), ALU.mult).then_inc(y_steps, 1)
                        dve.wait_ge(y_steps, nth(s, 10, first + 1))
                        v_.tensor_tensor(yt[:], MAIN[0][:, 0:DI], yt[:], ALU.add).then_inc(y_steps, 1)
                        dve.wait_ge(y_steps, nth(s, 10, first + 2))
                        v_.tensor_tensor(yt[:], yt[:], xd[:], ALU.add).then_inc(y_steps, 1)
                        dve.wait_ge(y_steps, nth(s, 10, first + 3))
                    if (v := nth(s, 4, c)) is not None:
                        dve.wait_ge(ssq_ready, v)
                        dve.wait_ge(yT_psum, v)
                    v_.tensor_tensor(yz[:], yt[:], sz[:, c, :], ALU.mult).then_inc(yz_ready, 1)
                    if c < NCH - 1:
                        first = (0, 2, 5)[c]
                        if c > 0:
                            v_.tensor_tensor(state_m[:], state[:], tdx[:, c, :].unsqueeze(2).to_broadcast([P, NP, 2 * HD]),
                                             ALU.mult).then_inc(state_step, 1)
                            dve.wait_ge(state_step, nth(s, 8, first + 1))
                            first += 1
                        dve.wait_ge(s_psum, nth(s, 3, c + 1))
                        if (v := nth(s, 4, c + 1 if c > 0 else 0)) is not None:
                            dve.wait_ge(y_psum, v)
                        own = MAIN[1][:, 0:256].rearrange("p (n d) -> p n d", n=NP)
                        for t in range(2):
                            q, d = slice(64 * t, 64 * t + 64), slice(HD * t, HD * t + HD)
                            if c == 0:
                                v_.tensor_copy(state[q, :, d], own[q, :, d]).then_inc(state_step, 1)
                            else:
                                v_.tensor_tensor(state[q, :, d], own[q, :, d], state_m[q, :, d], ALU.add).then_inc(state_step, 1)
                        dve.wait_ge(state_step, nth(s, 8, first + 2))

            def mean_square(s):
                dve.wait_ge(ssq_ready, nth(s, 4, 4))
                v_.tensor_scalar(msq[:], ssq[:], 1.0 / DI, RMS_EPS, ALU.mult, ALU.add).then_inc(msq_ready, 1)

            def add_residual(prev):
                if is_seq(prev, 0):
                    dve.wait_ge(fl_set, 2)
                dve.wait_ge(o_psum, nth(prev, 1, 1))
                dve.wait_ge(rstd_ready, nth(prev, 1, 1))
                if (v := nth(prev, 1, 0)) is not None:
                    dve.wait_ge(x1_kept_ready, v)
                for c in range(NCH):
                    v_.scalar_tensor_tensor(x1[:, c, :], MAIN[2][:, at(c)], rstd[:, c:c + 1], xr[:, c, :], ALU.mult, ALU.add)\
                        .then_inc(x1_ready, 1)

            def norm2(prev):
                dve.wait_ge(x1_ready, nth(prev, 4, 4))
                for c in range(NCH):
                    v_.bn_stats(st2[:, c, :], x1[:, c, :]).then_inc(ln2_stats, 1)
                dve.wait_ge(ln2_stats, nth(prev, 4, 4))
                v_.memset(carrier[:, RING:RING + 1], 0.0)
                for c in range(NCH):
                    v_.bn_aggr(mv2[:, c, :], st2[:, c, :]).then_inc(ln2_mv, 1)
                dve.wait_ge(ln2_mv, nth(prev, 4, 4))
                v_.tensor_scalar(v2[:], mv2[:, :, 1], LN_EPS, None, ALU.add).then_inc(ln2_v, 1)

            def norm2_apply(prev):
                dve.wait_ge(ln2_rs, nth(prev, 1, 1))
                for c in range(NCH):
                    v_.tensor_scalar(fn[:, c, :], x1[:, c, :], mv2[:, c, 0:1], rs2[:, c:c + 1], ALU.subtract, ALU.mult)\
                        .then_inc(fn_ready, 1)

            def fT_low(prev):
                dve.wait_ge(fTh_ready, nth(prev, 1, 1))
                v_.tensor_tensor(fTl[:], TR[:], f(fTh[:]), ALU.subtract).then_inc(fTl_ready, 1)

            def logits(prev):
                dve.wait_ge(gate_psum, nth(prev, 1, 1))
                v_.tensor_tensor(lg[:], TR[:, 0:NCH * NE].rearrange("p (c e) -> p c e", e=NE),
                                 gb[:].unsqueeze(1).to_broadcast([P, NCH, NE]), ALU.add).then_inc(gate_logits, 1)
                dve.wait_ge(gate_logits, nth(prev, 3, 1))
                v_.tensor_reduce(gmax[:], lg[:], AX_X, ALU.max).then_inc(gate_logits, 1)
                dve.wait_ge(gate_logits, nth(prev, 3, 2))
                v_.tensor_tensor(lg[:], lg[:], gmax[:].unsqueeze(2).to_broadcast([P, NCH, NE]), ALU.subtract).then_inc(gate_logits, 1)

            def top_two(prev):
                def step(k):
                    dve.wait_ge(gate_steps, nth(prev, 13, k))
                dve.wait_ge(gate_exp, nth(prev, 1, 1))
                v_.tensor_reduce(gsum[:], gexp[:], AX_X, ALU.add).then_inc(gate_steps, 1)
                step(1)
                v_.reciprocal(gsum[:], gsum[:]).then_inc(gate_steps, 1)
                step(2)
                v_.tensor_tensor(gw_n[:], gexp[:], gsum[:].unsqueeze(2).to_broadcast([P, NCH, NE]), ALU.mult).then_inc(gate_steps, 1)
                step(3)
                mine = gw_n[:].unsqueeze(3).to_broadcast([P, NCH, NE, NE])
                other = gw_n[:].unsqueeze(2).to_broadcast([P, NCH, NE, NE])
                v_.tensor_tensor(above[:], mine, other, ALU.is_lt).then_inc(gate_steps, 1)
                v_.tensor_tensor(level[:], mine, other, ALU.is_le).then_inc(gate_steps, 1)
                step(5)
                v_.tensor_tensor(level[:].rearrange("p c e j -> p c (e j)"), level[:].rearrange("p c e j -> p c (e j)"),
                                 lower[:].rearrange("p e j -> p (e j)").unsqueeze(1).to_broadcast([P, NCH, NE * NE]),
                                 ALU.mult).then_inc(gate_steps, 1)
                step(6)
                v_.tensor_tensor(above[:], above[:], level[:], ALU.max).then_inc(gate_steps, 1)
                step(7)
                v_.tensor_reduce(rank[:], above[:].rearrange("p c e j -> p (c e) j"), AX_X, ALU.add).then_inc(gate_steps, 1)
                step(8)
                v_.scalar_tensor_tensor(kept[:].rearrange("p c e -> p (c e)"), rank[:], 1.5, gw_n[:].rearrange("p c e -> p (c e)"),
                                        ALU.is_lt, ALU.mult).then_inc(gate_kept, 1)
                dve.wait_ge(gate_kept, nth(prev, 1, 1))
                three_parts(kept[:], gparts, grem1, grem2, gate_steps, prev, 13, 8)

            def gT_copy(prev):
                dve.wait_ge(gT_psum, nth(prev, 1, 1))
                v_.tensor_copy(gT[:], B2_BF[0:3 * NE, :]).then_inc(gT_ready, 1)

            def act_low(prev, b):
                r = b % RING
                dve.wait_ge(act_ready, nth(prev, NBLK, b + 1))
                v_.tensor_tensor(act_l[:, r, :], act_f[:, r, :], f(act_h[:, r, :]), ALU.subtract).then_inc(act_l_ready, 1)

            def routed_out(prev, e):
                dve.wait_ge(second_done, nth(prev, NBLK, 12 + 4 * e))
                dve.wait_ge(wbc_ready, nth(prev, 4, 4))
                if (v := nth(prev, 4, e)) is not None:
                    dve.wait_ge(acc_ready, v)
                v_.scalar_tensor_tensor(term, FOUT[:], b2r[:, e:e + 1], wbc[:, e, :], ALU.add, ALU.mult).then_inc(term_ready, 1)

            def store(prev):
                dve.wait_ge(x1_kept_ready, nth(prev, 1, 1))
                dve.wait_ge(outT_psum, nth(prev, 1, 1))
                if (v := nth(prev, 16, 0)) is not None:
                    dve.wait_ge(out_stored, v)
                v_.tensor_tensor(out_t.rearrange("p c d -> p (c d)"), TR[:], x1_kept[:].rearrange("p c d -> p (c d)"), ALU.add)\
                    .then_inc(out_ready, 1)



            def scan_part(s, i):
                last = is_seq(s, n_seq - 1)
                if i == 2:
                    dt_add(s, 0)
                    dt_add(s, 1)
                if i == 3:
                    dt_add(s, 2)
                if i == 4:
                    dt_add(s, 3)
                    dt_clamp(s)
                if i == 7:
                    c_copy(s, 0)
                if i == 8:
                    dt_decay(s)
                if i == 10:
                    l_parts(s)
                    residual(s)
                if i == 11:
                    lT_copy(s)
                if i >= CHUNKS_FROM:
                    attend(s, *divmod(i - CHUNKS_FROM, 3))
                if i == 15 and not last:
                    norm1(s + 1)
                if i == 18 and not last:
                    norm1_apply(s + 1)

            def body(s, prev, older):
                for i in range(NBLK):
                    if prev is not None:
                        if i == 1:
                            norm2_apply(prev)
                        if i == 4:
                            fT_low(prev)
                    if s is not None:
                        if i == 0:
                            conv(s, (0, 1))
                        scan_part(s, i)
                    if prev is not None:
                        if i == 0:
                            add_residual(prev)
                            norm2(prev)
                        if i == 5:
                            logits(prev)
                        if i == 7:
                            top_two(prev)
                        if i == 10:
                            gT_copy(prev)
                    if is_seq(s, 0) and i == 3:
                        split_small()
                    if older is not None and i == 7:
                        store(older)
                    if new := block_at(i, prev, older):
                        act_low(*new)
                    if s is not None:
                        if i == 1:
                            conv(s, (2, 3))
                        if i == NBLK - 1 and not is_seq(s, n_seq - 1):
                            hT_low(s + 1)
                    if older is not None and i == 3 + LAG:
                        routed_out(older, 3)
                    if prev is not None and i in (15 + LAG, 19 + LAG):
                        routed_out(prev, (i - 15 - LAG) // 4)
                if s is not None:
                    mean_square(s)
                if prev is not None:
                    routed_out(prev, 2)

            norm1(0)
            dve.wait_ge(cols_set, 1)
            dve.wait_ge(win_in, 16)
            v_.tensor_scalar(w_raw, w_raw, wn_in, None, ALU.mult).then_inc(w_scaled, 1)
            norm1_apply(0)
            dve.wait_ge(w_scaled, 1)
            v_.tensor_copy(wh[:, X0:], w_raw[:, 256:1536]).then_inc(wh_set, 1)
            dve.wait_ge(wh_set, 1)
            v_.tensor_tensor(wl[:, X0:], w_raw[:, 256:1536], f(wh[:, X0:]), ALU.subtract).then_inc(weights_set, 1)
            hT_low(0)
            v_.tensor_copy(wh[:, 0:256], w_raw[:, 0:256]).then_inc(wh_set, 1)
            dve.wait_ge(wdt_psum, 1)
            v_.tensor_copy(wh[:, DT0:DT0 + DI], MAIN[2][:, 0:DI]).then_inc(wh_set, 1)
            dve.wait_ge(wh_set, 3)
            v_.tensor_tensor(wl[:, 0:256], w_raw[:, 0:256], f(wh[:, 0:256]), ALU.subtract).then_inc(wl_set, 1)
            dve.wait_ge(wl_set, 1)
            v_.tensor_tensor(wl[:, DT0:DT0 + DI], MAIN[2][:, 0:DI], f(wh[:, DT0:DT0 + DI]), ALU.subtract).then_inc(weights_set, 1)

            bodies(dve, body)

        @block.gpsimd
        def _(pool):
            g = nc.gpsimd

            def ffn_low(k):
                pool.wait_ge(fh_set, k + 1)
                if k == 0:
                    g.tensor_tensor(w1l[:], wf_raw[:, 0], f(w1h[:]), ALU.subtract).then_inc(fl_set, 1)
                else:
                    g.tensor_tensor(w2l[:].rearrange("p n b o -> p (n b o)"), wf_raw[:, 1].rearrange("p n f -> p (n f)"),
                                    f(w2h[:].rearrange("p n b o -> p (n b o)")), ALU.subtract).then_inc(fl_set, 1)

            def rsqrt1(s):
                pool.wait_ge(ln1_v, nth(s, 2, 2))
                g.tensor_tensor(rs1[:].rearrange("p a c -> p (a c)"), v1[:].rearrange("p a c -> p (a c)"), half[:], ALU.pow)\
                    .then_inc(ln1_rs, 1)

            for t, v in ((ident, 0.0), (half, -0.5), (state, 0.0)):
                g.memset(t[:], v).then_inc(zeros_set, 1)
            g.memset(xpad[:, :, 0:TAPS - 1], 0.0).then_inc(zeros_set, 1)
            pool.wait_ge(zeros_set, 4)
            g.affine_select(out=ident[:], in_=ident[:], pattern=[[-1, P]], compare_op=ALU.not_equal, fill=1.0, base=0,
                            channel_multiplier=1).then_inc(tables_set, 1)
            rsqrt1(0)
            for t, v in ((ident_bf, 0.0), (ones, 1.0), (upto, 1.0), (mask, 0.0), (pick_head, 0.0),
                         (minus_head, 0.0), (pick_expert, 0.0), (lower, 1.0)):
                g.memset(t[:], v).then_inc(zeros_set, 1)
            pool.wait_ge(zeros_set, 12)
            g.affine_select(out=ident_bf[:], in_=ident_bf[:], pattern=[[-1, P]], compare_op=ALU.not_equal, fill=1.0, base=0,
                            channel_multiplier=1).then_inc(tables_set, 1)
            g.affine_select(out=upto[:], in_=upto[:], pattern=[[1, P]], compare_op=ALU.is_ge, fill=0.0, base=0,
                            channel_multiplier=-1).then_inc(tables_set, 1)
            g.affine_select(out=mask[:], in_=mask[:], pattern=[[0, NP], [1, P]], compare_op=ALU.is_ge, fill=MASKED, base=0,
                            channel_multiplier=-1).then_inc(tables_set, 1)
            g.affine_select(out=lower[:], in_=lower[:], pattern=[[1, NE], [-1, NE]], compare_op=ALU.is_gt, fill=0.0, base=0,
                            channel_multiplier=0).then_inc(tables_set, 1)
            k = 5
            for t, n, v in ((pick_head, NH, 1.0), (minus_head, NH, -1.0), (pick_expert, NE, 1.0)):
                for part in range(3):
                    g.affine_select(out=t[:], in_=t[:], pattern=[[-1, n], [0, P]], compare_op=ALU.not_equal, fill=v,
                                    base=-part * n, channel_multiplier=1).then_inc(tables_set, 1)
                    k += 1
                    pool.wait_ge(tables_set, k)

            def conv(s):
                pool.wait_ge(xpad_ready, nth(s, 2, 2))
                g.tensor_tensor(cv[:, 1, :], xpad[:, 1, 0:SEQ], conv_w[:, 1, 0:1].to_broadcast([P, SEQ]), ALU.mult)\
                    .then_inc(conv1_step, 1)
                pool.wait_ge(conv1_step, nth(s, 8, 1))
                g.tensor_tensor(cv[:, 1, :], cv[:, 1, :], conv_b[:, 1:2].to_broadcast([P, SEQ]), ALU.add).then_inc(conv1_step, 1)
                for k in range(1, TAPS):
                    pool.wait_ge(conv1_step, nth(s, 8, 2 * k))
                    g.tensor_tensor(tap[:], xpad[:, 1, k:k + SEQ], conv_w[:, 1, k:k + 1].to_broadcast([P, SEQ]), ALU.mult)\
                        .then_inc(conv1_step, 1)
                    pool.wait_ge(conv1_step, nth(s, 8, 2 * k + 1))
                    g.tensor_tensor(cv[:, 1, :], cv[:, 1, :], tap[:], ALU.add).then_inc(conv1_step, 1)

            def rsqrt2(prev):
                pool.wait_ge(ln2_v, nth(prev, 1, 1))
                g.tensor_tensor(rs2[:], v2[:], half[:, 0:NCH], ALU.pow).then_inc(ln2_rs, 1)

            def rsqrt_y(s):
                pool.wait_ge(msq_ready, nth(s, 1, 1))
                g.tensor_tensor(rstd[:], msq[:], half[:, 0:NCH], ALU.pow).then_inc(rstd_ready, 1)

            def skip(s, c):
                if c == 0:
                    pool.wait_ge(xs_ready, nth(s, 2, 2))
                if (v := nth(s, 4, c)) is not None:
                    pool.wait_ge(yz_ready, v)
                g.tensor_tensor(xd[:].rearrange("p (h d) -> p h d", h=NH), xs[:, c, :].rearrange("p (h d) -> p h d", h=NH),
                                d_bc[:].unsqueeze(2).to_broadcast([P, NH, HD]), ALU.mult).then_inc(xd_ready, 1)

            def weigh(s, c):
                for hf in range(2):
                    pool.wait_ge(decay_ready, nth(s, 8, 2 * c + hf + 1))
                    if hf == 0 and (v := nth(s, 3, c)) is not None:
                        pool.wait_ge(s_psum, v)
                    g.tensor_tensor(xw[:, :, hf, :], xs[:, c, :].rearrange("p (n t d) -> p n t d", n=NP, t=2)[:, :, hf, :],
                                    decay[:, hf, :, P - 1:P].to_broadcast([P, NP, HD]), ALU.mult).then_inc(xw_ready, 1)

            def add_term(prev, e):
                pool.wait_ge(term_ready, nth(prev, 4, e + 1))
                if e == 0:
                    pool.wait_ge(shared_ready, nth(prev, 1, 1))
                else:
                    pool.wait_ge(acc_ready, nth(prev, 4, e))
                g.tensor_tensor(acc, acc, term, ALU.add).then_inc(acc_ready, 1)

            def body(s, prev, older):
                last = is_seq(s, n_seq - 1)
                if prev is not None:
                    rsqrt2(prev)
                if s is not None:
                    conv(s)
                if older is not None:
                    add_term(older, 3)
                if is_seq(s, 0):
                    ffn_low(0)
                for i in range(CHUNKS_FROM, NBLK):
                    c, step = divmod(i - CHUNKS_FROM, 3)
                    if is_seq(s, 0) and i == CHUNKS_FROM + 4:
                        ffn_low(1)
                    if s is not None and step == 0:
                        skip(s, c)
                        if c < NCH - 1:
                            weigh(s, c)
                    if s is not None and i == 16 and not last:
                        rsqrt1(s + 1)
                    if prev is not None and i in (15 + LAG, 19 + LAG):
                        add_term(prev, (i - 15 - LAG) // 4)
                if prev is not None:
                    add_term(prev, 2)
                if s is not None:
                    rsqrt_y(s)

            bodies(pool, body)


_INS = ["hidden", "w_norm_in", "w_in_proj", "conv_w", "conv_b", "w_dt", "b_dt", "A_log", "D", "w_norm_out", "w_out_proj"]
_FFN = ["gate_w", "gate_b", "sw1", "sb1", "sw2", "sb2", "rw1", "rb1", "rw2", "rb2"]


def kernel(**inputs):
    import concourse.bacc as _bacc
    from concourse import mybir as _mybir
    from concourse.bass_utils import run_bass_kernel_spmd as _run

    nc = _bacc.Bacc("TRN2", target_bir_lowering=False, num_devices=1)
    arrays, args = {}, {}
    for name in ["L0_attn_" + n for n in _INS] + ["L0_ffn_" + n for n in _FFN]:
        v = np.ascontiguousarray(inputs[name])
        arrays[name + "_dram"] = v
        args[name.split("_", 2)[2]] = nc.dram_tensor(name + "_dram", v.shape, _mybir.dt.from_np(v.dtype), kind="ExternalInput").ap()
    out = nc.dram_tensor("out_dram", inputs["L0_attn_hidden"].shape, _mybir.dt.float32, kind="ExternalOutput").ap()
    build(nc, args, out)
    r = _run(nc, [arrays], core_ids=[0])
    return r.results[0]["out_dram"]
```
